# Optimizing a Trainium2 kernel written in Bass

```python
import numpy as np
import jax
import jax.numpy as jnp

def _softmax(x, axis=-1):
    return jax.nn.softmax(x, axis=axis)

def _gelu(x):
    return jax.nn.gelu(x, approximate=True)

def _silu(x):
    return jax.nn.silu(x)

def _sigmoid(x):
    return jax.nn.sigmoid(x)

def _layernorm(x, axis=-1, eps=1e-05):
    m = jnp.mean(x, axis=axis, keepdims=True)
    v = jnp.var(x, axis=axis, keepdims=True)
    return (x - m) / jnp.sqrt(v + eps)

def _scatter_add(tgt, idx, src, axis=0):
    return tgt.at[idx].add(src)

def _segment_sum(src, seg, n):
    return jax.ops.segment_sum(src, seg, n)
kernel_name = 'mk_perceiver_d2_seqx_r4_4dc64f'

def setup_inputs(seed: int=0):
    np.random.seed(seed)
    _w = jnp.asarray

    def _rec_inputs():
        import jax
        import jax.numpy as jnp
        _rk = jax.random.key(seed)
        x = 7.22e-05 + 1 * jax.random.normal(jax.random.fold_in(_rk, 1), (16, 64, 256), jnp.float32)
        _lenS = 64 - jax.random.randint(jax.random.fold_in(_rk, 7), (16,), 0, max(1, 64 // 4) + 1, jnp.int32)
        _lenS2 = 1601 - jax.random.randint(jax.random.fold_in(_rk, 8), (16,), 0, max(1, 1601 // 4) + 1, jnp.int32)
        _ctx_1024P = jax.random.normal(jax.random.fold_in(_rk, 11), (16, 16, 256), jnp.float32)
        _ctx_1024c = jax.random.dirichlet(jax.random.fold_in(_rk, 511), 0.3 * jnp.ones((16,), jnp.float32), (16, 1601))
        _ctx_1024t = jnp.einsum('bsk,bkd->bsd', _ctx_1024c, _ctx_1024P)
        _ctx_1024t = _ctx_1024t * jax.lax.rsqrt(jnp.mean(jnp.square(_ctx_1024t)) + 1e-12) * 0.953939
        ctx_1024 = 4.13588e-05 + 0.999923 * (_ctx_1024t + 0.3 * jax.random.normal(jax.random.fold_in(_rk, 611), (16, 1601, 256), jnp.float32))
        return (x, ctx_1024)
    x, ctx_1024 = _rec_inputs()

    def _L0_xattn_setup():
        import jax, jax.numpy as jnp
        import numpy as np
        B, LQ, LK = (4, 512, 512)
        DQ, DK, DO = (256, 256, 256)
        key = jax.random.key(seed)
        ks = jax.random.split(key, 9)
        s = 0.02
        return {'query_input': jax.random.normal(ks[0], (B, LQ, DQ), jnp.float32), 'key_input': jax.random.normal(ks[1], (B, LK, DK), jnp.float32), 'value_input': jax.random.normal(ks[2], (B, LK, DK), jnp.float32), 'Wq': jax.random.normal(ks[3], (DQ, DO), jnp.float32) * s, 'bq': jax.random.normal(ks[4], (DO,), jnp.float32) * s, 'Wk': jax.random.normal(ks[5], (DK, DO), jnp.float32) * s, 'bk': jax.random.normal(ks[6], (DO,), jnp.float32) * s, 'Wv': jax.random.normal(ks[7], (DK, DO), jnp.float32) * s, 'bv': jax.random.normal(ks[8], (DO,), jnp.float32) * s}
    _L0_xattn_all = _L0_xattn_setup()
    _L0_xattn_in = {k: v for k, v in _L0_xattn_all.items() if k in ('Wq', 'bq', 'Wk', 'bk', 'Wv', 'bv')}
    del _L0_xattn_all

    def _L0_attn_setup():
        import jax, jax.numpy as jnp
        import numpy as np
        from jax import lax
        D_MODEL = 256
        D_STATE = 16
        D_CONV = 4
        EXPAND = 2
        D_INNER = EXPAND * D_MODEL
        DT_RANK = -(-D_MODEL // 16)
        B, L = (2, 256)

        def _selective_scan(u, delta, a, b, c):
            deltaA = jnp.exp(jnp.einsum('bld,dn->bldn', delta, a))
            deltaBu = jnp.einsum('bld,bln,bld->bldn', delta, b, u)

            def step(h, inp):
                dA_t, dBu_t, c_t = inp
                h = dA_t * h + dBu_t
                y = jnp.einsum('bdn,bn->bd', h, c_t)
                return (h, y)
            h0 = jnp.zeros((u.shape[0], u.shape[2], a.shape[1]), dtype=u.dtype)
            xs = (jnp.moveaxis(deltaA, 1, 0), jnp.moveaxis(deltaBu, 1, 0), jnp.moveaxis(c, 1, 0))
            _, ys = lax.scan(step, h0, xs)
            return jnp.moveaxis(ys, 0, 1)
        key = jax.random.key(seed)
        ks = jax.random.split(key, 10)
        s = 0.02
        x = jax.random.normal(ks[0], (B, L, D_MODEL), dtype=jnp.float32)
        in_proj_w = jax.random.normal(ks[1], (2 * D_INNER, D_MODEL), dtype=jnp.float32) * s
        in_proj_b = jnp.zeros((2 * D_INNER,), dtype=jnp.float32)
        conv_w = jax.random.normal(ks[2], (D_INNER, 1, D_CONV), dtype=jnp.float32) * 0.1
        conv_b = jnp.zeros((D_INNER,), dtype=jnp.float32)
        x_proj_w = jax.random.normal(ks[3], (DT_RANK + 2 * D_STATE, D_INNER), dtype=jnp.float32) * s
        dt_proj_w = jax.random.normal(ks[4], (D_INNER, DT_RANK), dtype=jnp.float32) * s
        dt_proj_b = jnp.zeros((D_INNER,), dtype=jnp.float32)
        A_log = jnp.log(jnp.broadcast_to(jnp.arange(1, D_STATE + 1, dtype=jnp.float32), (D_INNER, D_STATE)))
        D_param = jnp.ones((D_INNER,), dtype=jnp.float32)
        out_proj_w = jax.random.normal(ks[5], (D_MODEL, D_INNER), dtype=jnp.float32) * s
        out_proj_b = jnp.zeros((D_MODEL,), dtype=jnp.float32)
        return dict(x=x, in_proj_w=in_proj_w, in_proj_b=in_proj_b, conv_w=conv_w, conv_b=conv_b, x_proj_w=x_proj_w, dt_proj_w=dt_proj_w, dt_proj_b=dt_proj_b, A_log=A_log, D_param=D_param, out_proj_w=out_proj_w, out_proj_b=out_proj_b)
    _L0_attn_all = _L0_attn_setup()
    _L0_attn_in = {k: v for k, v in _L0_attn_all.items() if k in ('in_proj_w', 'in_proj_b', 'conv_w', 'conv_b', 'x_proj_w', 'dt_proj_w', 'dt_proj_b', 'A_log', 'D_param', 'out_proj_w', 'out_proj_b')}
    del _L0_attn_all

    def _L0_ffn_setup():
        import jax, jax.numpy as jnp
        import numpy as np
        import math
        BETA = 0.9
        THRESHOLD = 1.0
        NUM_STEPS = 5
        ALPHA = 2.0

        @jax.custom_vjp
        def spike_fn(u):
            return (u > 0).astype(u.dtype)

        def _spike_fwd(u):
            return (spike_fn(u), u)

        def _spike_bwd(u, g):
            s = jnp.pi / 2.0 * ALPHA * u
            return (g * (ALPHA / 2.0) / (1.0 + s * s),)
        spike_fn.defvjp(_spike_fwd, _spike_bwd)
        key = jax.random.key(seed)
        k1, k2, k3 = jax.random.split(key, 3)
        n_embd = 256
        x = jax.random.normal(k1, (4, 512, n_embd), dtype=jnp.float32)
        W_fc = jax.random.normal(k2, (4 * n_embd, n_embd), dtype=jnp.float32) / math.sqrt(n_embd)
        W_proj = jax.random.normal(k3, (n_embd, 4 * n_embd), dtype=jnp.float32) / math.sqrt(4 * n_embd)
        return {'x': x, 'W_fc': W_fc, 'W_proj': W_proj}
    _L0_ffn_all = _L0_ffn_setup()
    _L0_ffn_in = {k: v for k, v in _L0_ffn_all.items() if k in ('W_fc', 'W_proj')}
    del _L0_ffn_all

    def _L1_xattn_setup():
        import jax, jax.numpy as jnp
        import numpy as np
        EMBED_DIM = 256
        NUM_HEADS = 16
        HEAD_DIM = EMBED_DIM // NUM_HEADS
        WINDOW = 128
        B, S_Q, S_K = (2, 512, 512)

        def apply_rope(x):
            Dh = x.shape[-1]
            half = Dh // 2
            pos = jnp.arange(x.shape[2], dtype=jnp.float32)
            inv_freq = 1.0 / 10000.0 ** (jnp.arange(0, half, dtype=jnp.float32) / half)
            ang = pos[:, None] * inv_freq[None, :]
            cos = jnp.cos(ang)[None, None, :, :].astype(x.dtype)
            sin = jnp.sin(ang)[None, None, :, :].astype(x.dtype)
            x1, x2 = (x[..., :half], x[..., half:])
            return jnp.concatenate([x1 * cos - x2 * sin, x1 * sin + x2 * cos], axis=-1)
        key = jax.random.key(seed)
        ks = jax.random.split(key, 11)
        scale = 1.0 / np.sqrt(EMBED_DIM)
        inp = {'query': jax.random.normal(ks[0], (B, S_Q, EMBED_DIM), jnp.float32), 'key': jax.random.normal(ks[1], (B, S_K, EMBED_DIM), jnp.float32), 'value': jax.random.normal(ks[2], (B, S_K, EMBED_DIM), jnp.float32), 'Wq': jax.random.normal(ks[3], (EMBED_DIM, EMBED_DIM), jnp.float32) * scale, 'bq': jnp.zeros((EMBED_DIM,), jnp.float32), 'Wk': jax.random.normal(ks[4], (EMBED_DIM, EMBED_DIM), jnp.float32) * scale, 'bk': jnp.zeros((EMBED_DIM,), jnp.float32), 'Wv': jax.random.normal(ks[5], (EMBED_DIM, EMBED_DIM), jnp.float32) * scale, 'bv': jnp.zeros((EMBED_DIM,), jnp.float32), 'Wo': jax.random.normal(ks[6], (EMBED_DIM, EMBED_DIM), jnp.float32) * scale, 'bo': jnp.zeros((EMBED_DIM,), jnp.float32)}
        return inp
    _L1_xattn_all = _L1_xattn_setup()
    _L1_xattn_in = {k: v for k, v in _L1_xattn_all.items() if k in ('Wq', 'bq', 'Wk', 'bk', 'Wv', 'bv', 'Wo', 'bo')}
    del _L1_xattn_all

    def _L1_attn_setup():
        import jax, jax.numpy as jnp
        import numpy as np
        B, N, D = (4, 512, 256)
        THRESHOLD_FACTOR = 1.25

        def _linear(x, W, b):
            return x @ W.T + b
        key = jax.random.key(seed)
        ks = jax.random.split(key, 8)
        s = 0.02
        return {'hidden_states': jax.random.normal(ks[0], (B, N, D), jnp.float32), 'Wq': jax.random.normal(ks[1], (D, D), jnp.float32) * s, 'bq': jnp.zeros((D,), jnp.float32), 'Wk': jax.random.normal(ks[2], (D, D), jnp.float32) * s, 'bk': jnp.zeros((D,), jnp.float32), 'Wv': jax.random.normal(ks[3], (D, D), jnp.float32) * s, 'bv': jnp.zeros((D,), jnp.float32), 'Wo': jax.random.normal(ks[4], (D, D), jnp.float32) * s, 'bo': jnp.zeros((D,), jnp.float32), 'Wtq': jax.random.normal(ks[5], (2, D), jnp.float32) * s, 'btq': jnp.zeros((2,), jnp.float32), 'Wfq': jax.random.normal(ks[6], (D, 2), jnp.float32) * s, 'bfq': jnp.zeros((D,), jnp.float32)}
    _L1_attn_all = _L1_attn_setup()
    _L1_attn_in = {k: v for k, v in _L1_attn_all.items() if k in ('Wq', 'bq', 'Wk', 'bk', 'Wv', 'bv', 'Wo', 'bo', 'Wtq', 'btq', 'Wfq', 'bfq')}
    del _L1_attn_all

    def _L1_ffn_setup():
        import jax, jax.numpy as jnp
        import numpy as np
        D_MODEL = 256
        EXPERT_DIM = 256
        NUM_EXPERTS = 8
        TOP_K = 2
        B, T = (8, 1024)
        key = jax.random.key(seed)
        ks = jax.random.split(key, 5)
        scale_in = 1.0 / np.sqrt(D_MODEL)
        scale_h = 1.0 / np.sqrt(EXPERT_DIM)
        return {'x': jax.random.normal(ks[0], (B, T, D_MODEL), dtype=jnp.float32), 'gate_w': jax.random.normal(ks[1], (D_MODEL, NUM_EXPERTS), dtype=jnp.float32) * scale_in, 'gate_b': jnp.zeros((NUM_EXPERTS,), dtype=jnp.float32), 'w1': jax.random.normal(ks[2], (NUM_EXPERTS, D_MODEL, EXPERT_DIM), dtype=jnp.float32) * scale_in, 'b1': jnp.zeros((NUM_EXPERTS, EXPERT_DIM), dtype=jnp.float32), 'w2': jax.random.normal(ks[3], (NUM_EXPERTS, EXPERT_DIM, D_MODEL), dtype=jnp.float32) * scale_h, 'b2': jnp.zeros((NUM_EXPERTS, D_MODEL), dtype=jnp.float32)}
    _L1_ffn_all = _L1_ffn_setup()
    _L1_ffn_in = {k: v for k, v in _L1_ffn_all.items() if k in ('gate_w', 'gate_b', 'w1', 'b1', 'w2', 'b2')}
    del _L1_ffn_all
    return {'x': x, 'ctx_1024': ctx_1024, 'L0_xattn_Wq': _L0_xattn_in['Wq'], 'L0_xattn_bq': _L0_xattn_in['bq'], 'L0_xattn_Wk': _L0_xattn_in['Wk'], 'L0_xattn_bk': _L0_xattn_in['bk'], 'L0_xattn_Wv': _L0_xattn_in['Wv'], 'L0_xattn_bv': _L0_xattn_in['bv'], 'L0_attn_in_proj_w': _L0_attn_in['in_proj_w'], 'L0_attn_in_proj_b': _L0_attn_in['in_proj_b'], 'L0_attn_conv_w': _L0_attn_in['conv_w'], 'L0_attn_conv_b': _L0_attn_in['conv_b'], 'L0_attn_x_proj_w': _L0_attn_in['x_proj_w'], 'L0_attn_dt_proj_w': _L0_attn_in['dt_proj_w'], 'L0_attn_dt_proj_b': _L0_attn_in['dt_proj_b'], 'L0_attn_A_log': _L0_attn_in['A_log'], 'L0_attn_D_param': _L0_attn_in['D_param'], 'L0_attn_out_proj_w': _L0_attn_in['out_proj_w'], 'L0_attn_out_proj_b': _L0_attn_in['out_proj_b'], 'L0_ffn_W_fc': _L0_ffn_in['W_fc'], 'L0_ffn_W_proj': _L0_ffn_in['W_proj'], 'L1_xattn_Wq': _L1_xattn_in['Wq'], 'L1_xattn_bq': _L1_xattn_in['bq'], 'L1_xattn_Wk': _L1_xattn_in['Wk'], 'L1_xattn_bk': _L1_xattn_in['bk'], 'L1_xattn_Wv': _L1_xattn_in['Wv'], 'L1_xattn_bv': _L1_xattn_in['bv'], 'L1_xattn_Wo': _L1_xattn_in['Wo'], 'L1_xattn_bo': _L1_xattn_in['bo'], 'L1_attn_Wq': _L1_attn_in['Wq'], 'L1_attn_bq': _L1_attn_in['bq'], 'L1_attn_Wk': _L1_attn_in['Wk'], 'L1_attn_bk': _L1_attn_in['bk'], 'L1_attn_Wv': _L1_attn_in['Wv'], 'L1_attn_bv': _L1_attn_in['bv'], 'L1_attn_Wo': _L1_attn_in['Wo'], 'L1_attn_bo': _L1_attn_in['bo'], 'L1_attn_Wtq': _L1_attn_in['Wtq'], 'L1_attn_btq': _L1_attn_in['btq'], 'L1_attn_Wfq': _L1_attn_in['Wfq'], 'L1_attn_bfq': _L1_attn_in['bfq'], 'L1_ffn_gate_w': _L1_ffn_in['gate_w'], 'L1_ffn_gate_b': _L1_ffn_in['gate_b'], 'L1_ffn_w1': _L1_ffn_in['w1'], 'L1_ffn_b1': _L1_ffn_in['b1'], 'L1_ffn_w2': _L1_ffn_in['w2'], 'L1_ffn_b2': _L1_ffn_in['b2']}

def reference(x, ctx_1024, L0_xattn_Wq, L0_xattn_bq, L0_xattn_Wk, L0_xattn_bk, L0_xattn_Wv, L0_xattn_bv, L0_attn_in_proj_w, L0_attn_in_proj_b, L0_attn_conv_w, L0_attn_conv_b, L0_attn_x_proj_w, L0_attn_dt_proj_w, L0_attn_dt_proj_b, L0_attn_A_log, L0_attn_D_param, L0_attn_out_proj_w, L0_attn_out_proj_b, L0_ffn_W_fc, L0_ffn_W_proj, L1_xattn_Wq, L1_xattn_bq, L1_xattn_Wk, L1_xattn_bk, L1_xattn_Wv, L1_xattn_bv, L1_xattn_Wo, L1_xattn_bo, L1_attn_Wq, L1_attn_bq, L1_attn_Wk, L1_attn_bk, L1_attn_Wv, L1_attn_bv, L1_attn_Wo, L1_attn_bo, L1_attn_Wtq, L1_attn_btq, L1_attn_Wfq, L1_attn_bfq, L1_ffn_gate_w, L1_ffn_gate_b, L1_ffn_w1, L1_ffn_b1, L1_ffn_w2, L1_ffn_b2):
    import jax
    import jax.numpy as jnp

    def _L0_xattn_ref(query_input, key_input, value_input, Wq, bq, Wk, bk, Wv, bv):
        import jax, jax.numpy as jnp
        import numpy as np
        B, LQ, LK = (4, 512, 512)
        DQ, DK, DO = (256, 256, 256)
        scale = jnp.asarray(DO, query_input.dtype) ** 0.5
        q = query_input @ Wq + bq
        k = key_input @ Wk + bk
        v = value_input @ Wv + bv
        attn = jnp.einsum('bqd,bkd->bqk', q, k) / scale
        attn = jax.nn.softmax(attn, axis=-1)
        return jnp.einsum('bqk,bkd->bqd', attn, v)

    def _L0_attn_ref(x, in_proj_w, in_proj_b, conv_w, conv_b, x_proj_w, dt_proj_w, dt_proj_b, A_log, D_param, out_proj_w, out_proj_b):
        import jax, jax.numpy as jnp
        import numpy as np
        from jax import lax
        D_MODEL = 256
        D_STATE = 16
        D_CONV = 4
        EXPAND = 2
        D_INNER = EXPAND * D_MODEL
        DT_RANK = -(-D_MODEL // 16)
        B, L = (2, 256)

        def _selective_scan(u, delta, a, b, c):
            deltaA = jnp.exp(jnp.einsum('bld,dn->bldn', delta, a))
            deltaBu = jnp.einsum('bld,bln,bld->bldn', delta, b, u)

            def step(h, inp):
                dA_t, dBu_t, c_t = inp
                h = dA_t * h + dBu_t
                y = jnp.einsum('bdn,bn->bd', h, c_t)
                return (h, y)
            h0 = jnp.zeros((u.shape[0], u.shape[2], a.shape[1]), dtype=u.dtype)
            xs = (jnp.moveaxis(deltaA, 1, 0), jnp.moveaxis(deltaBu, 1, 0), jnp.moveaxis(c, 1, 0))
            _, ys = lax.scan(step, h0, xs)
            return jnp.moveaxis(ys, 0, 1)
        x_and_res = x @ in_proj_w.T + in_proj_b
        x_b, res = jnp.split(x_and_res, [D_INNER], axis=-1)
        xc = jnp.transpose(x_b, (0, 2, 1))
        xc = lax.conv_general_dilated(xc, conv_w, window_strides=(1,), padding=[(D_CONV - 1, 0)], dimension_numbers=('NCH', 'OIH', 'NCH'), feature_group_count=D_INNER)
        xc = xc + conv_b[None, :, None]
        x_b = jax.nn.silu(jnp.transpose(xc, (0, 2, 1)))
        x_dbl = x_b @ x_proj_w.T
        delta, b, c = jnp.split(x_dbl, [DT_RANK, DT_RANK + D_STATE], axis=-1)
        delta = jax.nn.softplus(delta @ dt_proj_w.T + dt_proj_b)
        a = -jnp.exp(A_log)
        y = _selective_scan(x_b, delta, a, b, c)
        y = y + x_b * D_param
        y = y * jax.nn.silu(res)
        return y @ out_proj_w.T + out_proj_b

    def _L0_ffn_ref(x, W_fc, W_proj):
        import jax, jax.numpy as jnp
        import numpy as np
        import math
        BETA = 0.9
        THRESHOLD = 1.0
        NUM_STEPS = 5
        ALPHA = 2.0

        @jax.custom_vjp
        def spike_fn(u):
            return (u > 0).astype(u.dtype)

        def _spike_fwd(u):
            return (spike_fn(u), u)

        def _spike_bwd(u, g):
            s = jnp.pi / 2.0 * ALPHA * u
            return (g * (ALPHA / 2.0) / (1.0 + s * s),)
        spike_fn.defvjp(_spike_fwd, _spike_bwd)
        h = jnp.square(jax.nn.relu(jnp.einsum('bsd,fd->bsf', x, W_fc)))
        y = jnp.einsum('bsf,df->bsd', h, W_proj)

        def step(mem, _):
            reset = jax.lax.stop_gradient(spike_fn(mem - THRESHOLD))
            mem_new = BETA * mem + y - reset * THRESHOLD
            spk = spike_fn(mem_new - THRESHOLD)
            return (mem_new, spk)
        mem0 = jnp.zeros_like(y)
        _, spks = jax.lax.scan(step, mem0, None, length=NUM_STEPS)
        return jnp.sum(spks, axis=0) / NUM_STEPS

    def _L1_xattn_ref(query, key, value, Wq, bq, Wk, bk, Wv, bv, Wo, bo):
        import jax, jax.numpy as jnp
        import numpy as np
        EMBED_DIM = 256
        NUM_HEADS = 16
        HEAD_DIM = EMBED_DIM // NUM_HEADS
        WINDOW = 128
        B, S_Q, S_K = (2, 512, 512)

        def apply_rope(x):
            Dh = x.shape[-1]
            half = Dh // 2
            pos = jnp.arange(x.shape[2], dtype=jnp.float32)
            inv_freq = 1.0 / 10000.0 ** (jnp.arange(0, half, dtype=jnp.float32) / half)
            ang = pos[:, None] * inv_freq[None, :]
            cos = jnp.cos(ang)[None, None, :, :].astype(x.dtype)
            sin = jnp.sin(ang)[None, None, :, :].astype(x.dtype)
            x1, x2 = (x[..., :half], x[..., half:])
            return jnp.concatenate([x1 * cos - x2 * sin, x1 * sin + x2 * cos], axis=-1)
        Bq, Sq, D = query.shape
        Sk = key.shape[1]
        H, Dh = (NUM_HEADS, HEAD_DIM)

        def proj(x, W, b):
            return (x @ W.T + b).reshape(x.shape[0], x.shape[1], H, Dh).transpose(0, 2, 1, 3)
        q = apply_rope(proj(query, Wq, bq))
        k = apply_rope(proj(key, Wk, bk))
        v = proj(value, Wv, bv)
        q = q * Dh ** (-0.5)
        scores = jnp.einsum('bhqd,bhkd->bhqk', q, k)
        q_idx = jnp.arange(Sq)[:, None]
        kv_idx = jnp.arange(Sk)[None, :]
        rel = kv_idx - q_idx
        mask = (rel > 0) | (rel < -WINDOW)
        mask4 = mask[None, None, :, :]
        neg = jnp.finfo(scores.dtype).min
        scores = jnp.where(mask4, neg, scores)
        probs = jax.nn.softmax(scores, axis=-1)
        all_masked = jnp.all(mask4, axis=-1, keepdims=True)
        probs = jnp.where(all_masked, jnp.zeros((), probs.dtype), probs)
        out = jnp.einsum('bhqk,bhkd->bhqd', probs, v)
        out = out.transpose(0, 2, 1, 3).reshape(Bq, Sq, D)
        return out @ Wo.T + bo

    def _L1_attn_ref(hidden_states, Wq, bq, Wk, bk, Wv, bv, Wo, bo, Wtq, btq, Wfq, bfq):
        import jax, jax.numpy as jnp
        import numpy as np
        B, N, D = (4, 512, 256)
        THRESHOLD_FACTOR = 1.25

        def _linear(x, W, b):
            return x @ W.T + b
        d = hidden_states.shape[-1]
        q = _linear(hidden_states, Wq, bq)
        k = _linear(hidden_states, Wk, bk)
        v = _linear(hidden_states, Wv, bv)
        scores = jnp.einsum('bid,bjd->bij', q, k) / jnp.sqrt(jnp.asarray(d, (scores_dtype := q.dtype)))
        qp = _linear(hidden_states, Wtq, btq)
        diff = qp[:, :, None, :] - qp[:, None, :, :]
        dist_sq = jnp.sum(diff * diff, axis=-1)
        phase_diff = jnp.arctan2(diff[..., 1], diff[..., 0])
        forward_bias = 0.5 * (1.0 + jnp.cos(phase_diff))
        mean_dist = jnp.mean(dist_sq, axis=(-1, -2), keepdims=True)
        std_dist = jnp.std(dist_sq, axis=(-1, -2), keepdims=True, ddof=1)
        threshold = mean_dist + THRESHOLD_FACTOR * std_dist
        n = dist_sq.shape[-1]
        causal = jnp.tril(jnp.ones((n, n), bool))
        valid = (dist_sq <= threshold) & causal[None]
        binary_attn = valid.astype(scores.dtype) * forward_bias
        masked = jnp.where(binary_attn == 0, -jnp.inf, scores)
        weights = jax.nn.softmax(masked, axis=-1)
        context = jnp.einsum('bij,bjd->bid', weights, v)
        output = _linear(context, Wo, bo)
        r_embed = qp / jnp.maximum(jnp.linalg.norm(qp, axis=-1, keepdims=True), 1e-12)
        quantum_output = _linear(r_embed, Wfq, bfq)
        return hidden_states + output + 0.1 * quantum_output

    def _L1_ffn_ref(x, gate_w, gate_b, w1, b1, w2, b2):
        import jax, jax.numpy as jnp
        import numpy as np
        D_MODEL = 256
        EXPERT_DIM = 256
        NUM_EXPERTS = 8
        TOP_K = 2
        B, T = (8, 1024)
        b, t, d = x.shape
        xf = x.reshape(b * t, d)
        scores = xf @ gate_w + gate_b
        topk_s, topk_i = jax.lax.top_k(scores, TOP_K)
        n = xf.shape[0]
        comb = jnp.zeros_like(scores).at[jnp.arange(n)[:, None], topk_i].add(topk_s)
        h = jnp.maximum(jnp.einsum('nd,edh->neh', xf, w1) + b1, 0.0)
        eo = jnp.einsum('neh,ehd->ned', h, w2) + b2
        out = jnp.einsum('ne,ned->nd', comb, eo)
        return out.reshape(b, t, d)
    x = x + _L0_xattn_ref(_layernorm(x, axis=-1), ctx_1024, ctx_1024, L0_xattn_Wq, L0_xattn_bq, L0_xattn_Wk, L0_xattn_bk, L0_xattn_Wv, L0_xattn_bv)
    x = x + _L0_attn_ref(_layernorm(x, axis=-1), L0_attn_in_proj_w, L0_attn_in_proj_b, L0_attn_conv_w, L0_attn_conv_b, L0_attn_x_proj_w, L0_attn_dt_proj_w, L0_attn_dt_proj_b, L0_attn_A_log, L0_attn_D_param, L0_attn_out_proj_w, L0_attn_out_proj_b)
    x = x + _L0_ffn_ref(_layernorm(x, axis=-1), L0_ffn_W_fc, L0_ffn_W_proj)
    x = x + _L1_xattn_ref(_layernorm(x, axis=-1), ctx_1024, ctx_1024, L1_xattn_Wq, L1_xattn_bq, L1_xattn_Wk, L1_xattn_bk, L1_xattn_Wv, L1_xattn_bv, L1_xattn_Wo, L1_xattn_bo)
    x = x + _L1_attn_ref(_layernorm(x, axis=-1), L1_attn_Wq, L1_attn_bq, L1_attn_Wk, L1_attn_bk, L1_attn_Wv, L1_attn_bv, L1_attn_Wo, L1_attn_bo, L1_attn_Wtq, L1_attn_btq, L1_attn_Wfq, L1_attn_bfq)
    x = x + _L1_ffn_ref(_layernorm(x, axis=-1), L1_ffn_gate_w, L1_ffn_gate_b, L1_ffn_w1, L1_ffn_b1, L1_ffn_w2, L1_ffn_b2)
    return x

_drawn_inputs = setup_inputs


def setup_inputs(seed=0):
    import zlib

    import numpy as np

    out = dict(_drawn_inputs(seed))
    spreads = {'L0_attn_in_proj_b': (0.0, 0.8),
     'L0_attn_conv_b': (0.0, 0.1),
     'L0_attn_dt_proj_b': (0.0, 0.8),
     'L0_attn_D_param': (1.0, 0.6),
     'L0_attn_out_proj_b': (0.0, 0.1),
     'L1_xattn_bq': (0.0, 0.1),
     'L1_xattn_bk': (0.0, 0.275),
     'L1_xattn_bv': (0.0, 0.1),
     'L1_xattn_bo': (0.0, 0.1),
     'L1_attn_bq': (0.0, 0.8),
     'L1_attn_bk': (0.0, 2.0),
     'L1_attn_bv': (0.0, 0.329),
     'L1_attn_bo': (0.0, 0.1),
     'L1_attn_btq': (0.0, 2.0),
     'L1_attn_bfq': (0.0, 0.611),
     'L1_ffn_gate_b': (0.0, 0.1),
     'L1_ffn_b1': (0.0, 0.1),
     'L1_ffn_b2': (0.0, 0.1)}
    factors = {'L0_xattn_bq': 29.055,
     'L0_xattn_bk': 200.0,
     'L0_attn_conv_w': 2.902,
     'L0_attn_x_proj_w': 8.0,
     'L0_attn_dt_proj_w': 8.0,
     'L0_attn_A_log': 8.0,
     'L1_attn_Wq': 8.0,
     'L1_attn_Wk': 8.0,
     'L1_attn_Wtq': 3.789,
     'L1_attn_Wfq': 13.211,
     'L0_xattn_Wq': 3.486}
    for name, (base, spread) in spreads.items():
        noise = np.random.default_rng([zlib.crc32(name.encode()), seed]).standard_normal(out[name].shape)
        drawn = base * np.exp(spread * noise) if base else spread * noise
        out[name] = jnp.asarray(drawn.astype(out[name].dtype))
    for name, factor in factors.items():
        out[name] = (out[name] * factor).astype(out[name].dtype)
    return out
```

```python
from contextlib import ExitStack

import numpy as np
import concourse.bass as bass
from concourse import mybir

F32 = mybir.dt.float32
BF16 = mybir.dt.bfloat16
U32 = mybir.dt.uint32
ALU = mybir.AluOpType
ACT = mybir.ActivationFunctionType
AX = mybir.AxisListType

P = 128
B, L, D = 16, 64, 256
LK = 1601
TOK = B * L
TILES = TOK // P
KD = D // P
HALF = 512
EPS = 1e-5
NEG = -3.0e38

ROWS = 13
FULL = LK // ROWS
LAST = LK - FULL * ROWS
SC_W = [min(HALF, LK - c * HALF) for c in range(4)]

DI, DS, DTR, KC = 512, 16, 16, 4
CH = DI // P
FF = 1024
FM = FF // P
H, DH = 16, 16
HG = P // DH
DV = DH + 1
E, TOPK = 8, 2

COLS = {}
_n = 0
for _name, _w in (("bq0", 2), ("bk0", 2), ("inb", 8), ("convw", 16), ("convb", 4), ("dtb", 4),
                  ("dpar", 4), ("alog", 64), ("bq5", 2), ("bk5", 2), ("b1", 16)):
    COLS[_name] = (_n, _w)
    _n += _w
NCOLS = _n
ROWV = {n: i for i, n in enumerate(("bv0", "outb", "bq4", "bk4", "bv4", "bo4", "bv5", "bo5", "bfq"))}
NROWS = len(ROWV)


class Names:
    pass


def tools(nc, ctx):
    def sb(name, shape, dt=F32):
        return ctx.enter_context(nc.sbuf_tensor(name, shape, dt))

    def ps(name, shape=(P, HALF), dt=F32):
        return ctx.enter_context(nc.psum_tensor(name, list(shape), dt))

    def sem(name):
        return ctx.enter_context(nc.semaphore(name))

    return sb, ps, sem


def col(k, name, i=0):
    a, _ = COLS[name]
    return k.cols[:, a + i:a + i + 1]


def rowvec(k, name):
    return k.rows[:, ROWV[name], :]


def layer_norm(nc, k, tag, loads=None):
    with ExitStack() as ctx:
        sb, ps, sem = tools(nc, ctx)
        stats = sb(f"{tag}_stats", [P, TILES, 6])
        mv = sb(f"{tag}_mv", [P, TILES, 2])
        veps = sb(f"{tag}_veps", [P, TILES])
        sd = sb(f"{tag}_sd", [P, TILES])
        rstd = sb(f"{tag}_rstd", [P, TILES])
        tp = [ps(f"{tag}_tp{i}") for i in range(4)]
        s_dve = sem(f"{tag}_dve")
        s_sd = sem(f"{tag}_sd_ready")
        s_xn = sem(f"{tag}_xn")
        s_tp = sem(f"{tag}_tp_done")
        s_ev = sem(f"{tag}_ev")
        block = ctx.enter_context(nc.Block())
        if loads:
            loads(block)

        @block.vector
        def _(e):
            if tag == "ln0":
                e.wait_ge(k.s_x, 16)
            for t in range(TILES):
                i = e.bn_stats(stats[:, t, :], k.x[:, t, :])
            i.then_inc(s_dve, 1)
            e.wait_ge(s_dve, 1)
            for t in range(TILES):
                i = e.bn_aggr(mv[:, t, :], stats[:, t, :])
            i.then_inc(s_dve, 1)
            e.wait_ge(s_dve, 2)
            e.tensor_scalar(veps[:, :], mv[:, :, 1], EPS, None, ALU.add).then_inc(s_dve, 1)
            e.wait_ge(s_sd, 1)
            e.reciprocal(rstd[:, :], sd[:, :]).then_inc(s_dve, 1)
            e.wait_ge(s_dve, 4)
            for t in range(TILES):
                e.tensor_scalar(k.xn[:, t, :], k.x[:, t, :], mv[:, t, 0:1], rstd[:, t:t + 1],
                                ALU.subtract, ALU.mult).then_inc(s_xn, 1)

        @block.scalar
        def _(e):
            e.wait_ge(s_dve, 3)
            e.activation(sd[:, :], veps[:, :], ACT.Sqrt).then_inc(s_sd, 1)
            for t in range(TILES):
                e.wait_ge(s_tp, t + 1)
                e.activation(k.xT[:, :, t * P:(t + 1) * P],
                             tp[t % 4][:, 0:D].rearrange("p (c n) -> p c n", c=KD), ACT.Copy
                             ).then_inc(s_ev, 1)

        @block.tensor
        def _(e):
            if tag == "ln0":
                e.wait_ge(k.s_const, k.n_ident)
            for t in range(TILES):
                e.wait_ge(s_xn, t + 1)
                if t >= 4:
                    e.wait_ge(s_ev, t - 3)
                for c in range(KD):
                    i = e.transpose(tp[t % 4][:, c * P:(c + 1) * P], k.xn[:, t, c * P:(c + 1) * P],
                                    k.ident[:, :])
                i.then_inc(s_tp, 1)


def load_columns(e, k, i, r):
    src = k.ctxT[2 * i:2 * i + 2] if isinstance(i, int) else k.ctxT[bass.ds(i * 2, 2), :, :]
    e.dma_start(k.cT[r][:, :, :, :], src.rearrange("b (c p) n -> p b c n", p=P)).then_inc(k.s_dT[r], 16)


def load_rows(e, k, i, r):
    src = k.ctx[2 * i:2 * i + 2] if isinstance(i, int) else k.ctx[bass.ds(i * 2, 2), :, :]
    e.dma_start(k.cN[r][0:FULL, :, :, :],
                src[:, 0:FULL * ROWS, :].rearrange("b (p c) d -> p b c d", c=ROWS)).then_inc(k.s_dN[r], 16)
    e.dma_start(k.cN[r][FULL:FULL + 1, :, 0:LAST, :],
                src[:, FULL * ROWS:LK, :].rearrange("b (p c) d -> p b c d", p=1)).then_inc(k.s_dN[r], 16)


def cross_attention(nc, k):
    scale = 1.0 / float(D) ** 0.5
    with ExitStack() as ctx:
        sb, ps, sem = tools(nc, ctx)
        qT = sb("qT", [P, KD, TOK])
        qkT = sb("qkT", [P, KD, TOK + P])
        qbk = sb("qbk", [P, TILES])
        qs = [sb(f"qs{r}", [P, KD, P]) for r in range(2)]
        cT, cN, s_dT, s_dN = k.cT, k.cN, k.s_dT, k.s_dN
        prob = [sb(f"prob{r}", [P, LK]) for r in range(2)]
        pT = sb("pT", [P, ROWS, P])
        mx = sb("mx", [P, 1])
        full_max = sb("full_max", [P, 1])
        nbias = sb("nbias", [P, 1])
        total = [sb(f"total{r}", [P, 1]) for r in range(2)]
        rinv = sb("rinv", [P, 1])
        on = [sb(f"on{r}", [P, D]) for r in range(2)]
        onT = sb("onT", [P, KD, P])
        S = ps("S", [P, 4 * HALF])
        tps = [ps(f"ptp{i}") for i in range(2)]
        O = ps("O")
        X = ps("X")
        s_pp = sem("a_pp")
        s_pe = sem("a_pe")
        s_qb = sem("a_qb")
        s_q0 = sem("a_q0")
        s_qs = sem("a_qs")
        s_sc = sem("a_sc")
        s_m1 = sem("a_m1")
        s_mx = sem("a_mx")
        s_ex = sem("a_ex")
        s_tp = sem("a_tp")
        s_te = sem("a_te")
        s_pv = sem("a_pv")
        s_ri = sem("a_ri")
        s_on = sem("a_on")
        s_ot = sem("a_ot")
        s_oe = sem("a_oe")
        s_wv = sem("a_wv")
        s_xa = sem("a_xa")
        block = ctx.enter_context(nc.Block())
        groups = [range(0, 4), range(4, 8), range(8, 12), range(12, 13)]

        def pipeline(e, sub):
            for i in range(2):
                sub(i, i % 2, lambda d, i=i: i - d >= 0)
            with e.Fori(1, TILES // 2) as j:
                sub(j * 2, 0, lambda d: True)
                sub(j * 2 + 1, 1, lambda d: True)
            for i in range(TILES, TILES + 2):
                sub(i, i % 2, lambda d, i=i: i - d < TILES)

        @block.sync
        def _(e):
            e.wait_ge(s_sc, 1)
            load_columns(e, k, 2, 0)
            e.wait_ge(s_sc, 2)
            load_columns(e, k, 3, 1)
            e.wait_ge(s_pv, 1)
            load_rows(e, k, 2, 0)
            with e.Fori(2, TILES // 2) as j:
                for r in range(2):
                    e.wait_ge(s_sc, j * 2 + (r - 1))
                    load_columns(e, k, j * 2 + r, r)
                    e.wait_ge(s_pv, j * 2 + (r - 2))
                    load_rows(e, k, j * 2 + (r - 1), 1 - r)
            e.wait_ge(s_pv, TILES - 2)
            load_rows(e, k, TILES - 1, 1)

        @block.tensor
        def _(e):
            e.wait_ge(k.s_w0, k.n_w0)
            n = 0
            for w, src in ((k.wq0, k.xT), (k.wk0T, qT)):
                for m in range(KD):
                    for h in range(2):
                        if n >= 2:
                            e.wait_ge(s_pe, n - 1 if n != 4 else 4)
                        for c in range(KD):
                            i = e.matmul(tps[n % 2][:, :], w[:, c, m * P:(m + 1) * P],
                                         src[:, c, h * HALF:(h + 1) * HALF], start=c == 0, stop=c == 1)
                        i.then_inc(s_pp, 1)
                        n += 1
            for t in range(TILES):
                for c in range(KD):
                    i = e.matmul(X[:, t:t + 1], qT[:, c, t * P:(t + 1) * P], col(k, "bk0", c),
                                 start=c == 0, stop=c == 1)
            i.then_inc(s_qb, 1)
            e.wait_ge(s_q0, 1)
            e.wait_ge(s_pe, 8)

            def turn(i, q, g):
                if g >= 2:
                    e.wait_ge(s_te, (i - 1) * 4 + g - 1)
                for c in groups[g]:
                    kc = FULL + (c < LAST)
                    j = e.transpose(tps[g % 2][0:kc, (c % 4) * P:(c % 4 + 1) * P],
                                    prob[q][:, c:c + (kc - 1) * ROWS + 1:ROWS], k.ident[:, :])
                j.then_inc(s_tp, 1)

            def sub(i, r, live):
                if live(1):
                    e.wait_ge(s_ex, i)
                    for g in range(2):
                        turn(i, 1 - r, g)
                if live(2):
                    e.wait_ge(s_on, i - 1)
                    for c in range(KD):
                        j = e.transpose(X[:, c * P:(c + 1) * P], on[r][:, c * P:(c + 1) * P], k.ident[:, :])
                    j.then_inc(s_ot, 1)
                if live(0):
                    e.wait_ge(s_qs, i + 1)
                    e.wait_ge(s_dT[r], 16 * (i // 2 + 1) if isinstance(i, int) else (i - r) * 8 + 16)
                    e.wait_ge(s_ex, i)
                    for c, w in enumerate(SC_W):
                        for kt in range(KD):
                            for b in range(2):
                                j = e.matmul(S[64 * b:64 * b + 64, c * HALF:c * HALF + w],
                                             qs[r][:, kt, 64 * b:64 * b + 64],
                                             cT[r][:, b, kt, c * HALF:c * HALF + w],
                                             start=kt == 0, stop=kt == 1)
                    j.then_inc(s_sc, 1)
                if live(2):
                    e.wait_ge(s_oe, i - 1)
                    for c in range(KD):
                        j = e.matmul(X[:, D:2 * D], onT[:, c, :], k.wv0[:, c, :], start=c == 0, stop=c == 1)
                    j.then_inc(s_wv, 1)
                if live(1):
                    q = 1 - r
                    e.wait_ge(s_dN[q], 32 * ((i - 1) // 2 + 1) if isinstance(i, int) else (i - 1 - q) * 16 + 32)

                    def pv(g):
                        e.wait_ge(s_te, (i - 1) * 4 + g + 1)
                        if g == 0:
                            e.wait_ge(s_on, i - 1)
                        for c in groups[g]:
                            kc = FULL + (c < LAST)
                            for b in range(2):
                                j = e.matmul(O[64 * b:64 * b + 64, 0:D], pT[0:kc, c, 64 * b:64 * b + 64],
                                             cN[q][0:kc, b, c, :], start=c == 0, stop=c == ROWS - 1)
                        return j

                    for g in range(2):
                        pv(g)
                        turn(i, q, g + 2)
                    pv(2)
                    pv(3).then_inc(s_pv, 1)

            pipeline(e, sub)

        @block.scalar
        def _(e):
            n = 0
            for b in ("bq0", None):
                for m in range(KD):
                    for h in range(2):
                        e.wait_ge(s_pp, n + 1)
                        dst = (qT if b else qkT)[:, m, h * HALF:(h + 1) * HALF]
                        if b:
                            e.activation(dst, tps[n % 2][:, :], ACT.Identity, bias=col(k, b, m)).then_inc(s_pe, 1)
                        else:
                            e.activation(dst, tps[n % 2][:, :], ACT.Copy).then_inc(s_pe, 1)
                        n += 1

            def sub(i, r, live):
                if live(2):
                    e.wait_ge(s_ot, i - 1)
                    if not isinstance(i, int) or i > 2:
                        e.wait_ge(s_wv, i - 2)
                    e.activation(onT[:, :, :], X[:, 0:D].rearrange("p (c n) -> p c n", c=KD), ACT.Copy
                                 ).then_inc(s_oe, 1)
                if live(0):
                    if not isinstance(i, int) or i >= 2:
                        e.wait_ge(s_tp, (i - 1) * 4)
                    e.wait_ge(s_mx, i + 1)
                    e.activation(prob[r][:, :], S[:, 0:LK], ACT.Exp, bias=nbias[:, :], scale=scale,
                                 accum_out=total[r][:, :]).then_inc(s_ex, 1)

            pipeline(e, sub)

        @block.vector
        def _(e):
            e.wait_ge(k.s_rows, 16)
            e.tensor_tensor(k.x[:, :, :], k.x[:, :, :],
                            rowvec(k, "bv0").unsqueeze(1).to_broadcast([P, TILES, D]), ALU.add)
            e.memset(qkT[:, :, TOK:TOK + P], 0.0)
            e.wait_ge(s_qb, 1)
            e.tensor_scalar(qbk[:, :], X[:, 0:TILES], scale, None, ALU.mult).then_inc(s_q0, 1)
            e.wait_ge(s_pe, 8)

            def queries(i, r):
                src = qkT[:, :, i * P:(i + 1) * P] if isinstance(i, int) else qkT[:, :, bass.ds(i * P, P)]
                e.tensor_copy(qs[r][:, :, :], src).then_inc(s_qs, 1)

            queries(0, 0)
            e.wait_ge(s_q0, 1)

            def evacuate(i, g):
                e.wait_ge(s_tp, (i - 1) * 4 + g + 1)
                if g == 0:
                    e.wait_ge(s_pv, i - 1)
                n, c0 = len(groups[g]), groups[g][0]
                if c0 < LAST:
                    e.tensor_copy(pT[0:FULL + 1, 0:LAST, :],
                                  tps[0][0:FULL + 1, 0:LAST * P].rearrange("p (c n) -> p c n", n=P))
                    e.tensor_copy(pT[0:FULL, LAST:4, :],
                                  tps[0][0:FULL, LAST * P:4 * P].rearrange("p (c n) -> p c n", n=P)
                                  ).then_inc(s_te, 1)
                else:
                    e.tensor_copy(pT[0:FULL, c0:c0 + n, :],
                                  tps[g % 2][0:FULL, 0:n * P].rearrange("p (c n) -> p c n", n=P)
                                  ).then_inc(s_te, 1)

            def sub(i, r, live):
                if live(1):
                    for g in range(2):
                        evacuate(i, g)
                one = (lambda a, n: a[:, n:n + 1] if isinstance(n, int) else a[:, bass.ds(n, 1)])
                if live(0):
                    e.wait_ge(s_sc, i + 1)
                    e.reduce_max(mx[:, :], S[:, 0:LK], AX.X).then_inc(s_m1, 1)
                    e.wait_ge(s_m1, i * 2 + 1)
                    e.tensor_scalar(full_max[:, :], mx[:, :], scale, one(qbk, i), ALU.mult, ALU.add
                                    ).then_inc(s_m1, 1)
                    e.wait_ge(s_m1, i * 2 + 2)
                    e.wait_ge(s_ex, i)
                    e.tensor_scalar(nbias[:, :], full_max[:, :], -1.0, one(qbk, i), ALU.mult, ALU.add
                                    ).then_inc(s_mx, 1)
                    queries(i + 1, 1 - r)
                if live(2):
                    e.wait_ge(s_wv, i - 1)
                    dst = k.x[:, i - 2, :] if isinstance(i, int) else k.x[:, bass.ds(i - 2, 1), :].squeeze(1)
                    e.tensor_tensor(dst, dst, X[:, D:2 * D], ALU.add).then_inc(s_xa, 1)
                if live(1):
                    q = 1 - r
                    for g in (2, 3):
                        evacuate(i, g)
                    e.reciprocal(rinv[:, :], total[q][:, :]).then_inc(s_ri, 1)
                    e.wait_ge(s_ri, i)
                    e.wait_ge(s_pv, i)
                    e.tensor_scalar(on[q][:, :], O[:, 0:D], rinv[:, :], None, ALU.mult).then_inc(s_on, 1)

            pipeline(e, sub)


def mamba_front(nc, k, m):
    with ExitStack() as ctx:
        sb, ps, sem = tools(nc, ctx)
        BH = HALF // L
        xpad = [sb(f"xpad{r}", [P, BH, L + KC - 1]) for r in range(2)]
        acc = [sb(f"acc{r}", [P, BH, L]) for r in range(2)]
        expA = sb("expA", [P, CH * DS])
        dtr = sb("dtr", [DTR, TOK])
        bc = sb("bc", [64, TOK])
        az = [sb(f"az{r}", [P, HALF]) for r in range(2)]
        ez = [sb(f"ez{r}", [P, HALF]) for r in range(2)]
        lz = [sb(f"lz{r}", [P, HALF]) for r in range(2)]
        rz = [sb(f"rz{r}", [P, HALF]) for r in range(2)]
        zp = [ps(f"zp{i}") for i in range(4)]
        xq = [ps(f"xq{i}") for i in range(2)]
        dq = [ps(f"dq{i}") for i in range(2)]
        s_in = sem("m_in")
        s_xp = sem("m_xp")
        s_pad = sem("m_pad")
        s_cv = sem("m_cv")
        s_u = sem("m_u")
        s_rs = sem("m_rs")
        s_xj = sem("m_xj")
        s_xe = sem("m_xe")
        s_dt = sem("m_dt")
        s_az = sem("m_az")
        s_rz = sem("m_rz")
        s_dl = sem("m_dl")
        s_bc = sem("m_bc")
        s_a = sem("m_a")
        block = ctx.enter_context(nc.Block())
        xblocks = [(c, h) for h in range(2) for c in range(CH)]

        @block.tensor
        def _(e):
            e.wait_ge(k.s_w2, k.n_w2)
            n = 0
            for part in range(2):
                for c, h in xblocks:
                    if n >= 4:
                        e.wait_ge(s_xp, min(n - 3, 8))
                        if n - 3 > 8:
                            e.wait_ge(s_rs, n - 3 - 8)
                    for kt in range(KD):
                        i = e.matmul(zp[n % 4][:, :], k.w_in[:, kt, (part * CH + c) * P:(part * CH + c + 1) * P],
                                     k.xT[:, kt, h * HALF:(h + 1) * HALF], start=kt == 0, stop=kt == 1)
                    i.then_inc(s_in, 1)
                    n += 1
            for h in range(2):
                e.wait_ge(s_u, CH * (h + 1))
                for c in range(CH):
                    i = e.matmul(xq[h][0:64, :], k.w_xp[:, c, :], m.u[:, c, h * HALF:(h + 1) * HALF],
                                 start=c == 0, stop=c == CH - 1)
                i.then_inc(s_xj, 1)
            for n, (c, h) in enumerate(xblocks):
                e.wait_ge(s_xe, h + 1)
                if n >= 2:
                    e.wait_ge(s_az, 3 * (n - 2) + 1)
                    e.wait_ge(s_rz, n - 1)
                e.matmul(dq[n % 2][:, :], k.w_dt[:, c * P:(c + 1) * P], dtr[:, h * HALF:(h + 1) * HALF],
                         start=True, stop=True).then_inc(s_dt, 1)

        @block.scalar
        def _(e):
            def gate(n):
                c, h = xblocks[n]
                e.wait_ge(s_in, 8 + n + 1)
                e.activation(m.sres[:, c, h * HALF:(h + 1) * HALF], zp[n % 4][:, :], ACT.Silu,
                             bias=col(k, "inb", CH + c)).then_inc(s_rs, 1)

            def silu_u(n):
                c, h = xblocks[n]
                e.wait_ge(s_cv, 4 * n + 4)
                e.activation(m.u[:, c, h * HALF:(h + 1) * HALF].rearrange("p (b l) -> p b l", l=L),
                             acc[n % 2][:, :, :], ACT.Silu).then_inc(s_u, 1)

            e.wait_ge(s_pad, 1)
            for n, (c, h) in enumerate(xblocks):
                e.wait_ge(s_in, n + 1)
                if n >= 2:
                    e.wait_ge(s_cv, 4 * (n - 2) + 4)
                e.activation(xpad[n % 2][:, :, KC - 1:], zp[n % 4][:, :].rearrange("p (b l) -> p b l", l=L),
                             ACT.Identity, bias=col(k, "inb", c)).then_inc(s_xp, 1)
                if n >= 1:
                    silu_u(n - 1)
            silu_u(7)
            for n in range(8):
                gate(n)
            for n, (c, h) in enumerate(xblocks):
                r = n % 2
                e.wait_ge(s_dt, n + 1)
                e.activation(az[r][:, :], dq[r][:, :], ACT.Abs, bias=col(k, "dtb", c)).then_inc(s_az, 1)
                e.wait_ge(s_az, 3 * n + 1)
                e.activation(ez[r][:, :], az[r][:, :], ACT.Exp, scale=-1.0).then_inc(s_az, 1)
                e.wait_ge(s_az, 3 * n + 2)
                if n >= 2:
                    e.wait_ge(s_dl, 2 * (n - 2) + 1)
                e.activation(lz[r][:, :], ez[r][:, :], ACT.Ln, bias=1.0).then_inc(s_az, 1)
            a0, aw = COLS["alog"]
            e.activation(expA[:, :], k.cols[:, a0:a0 + aw], ACT.Exp).then_inc(s_a, 1)
            e.wait_ge(s_a, 1)
            e.mul(m.negA[:, :, :].rearrange("p c n -> p (c n)"), expA[:, :], -1.0)

        @block.vector
        def _(e):
            for r in range(2):
                i = e.memset(xpad[r][:, :, 0:KC - 1], 0.0)
            i.then_inc(s_pad, 1)
            for n, (c, h) in enumerate(xblocks):
                r = n % 2
                e.wait_ge(s_xp, n + 1)
                if n >= 2:
                    e.wait_ge(s_u, n - 1)
                for j in range(KC):
                    tap = col(k, "convw", c * KC + j)
                    if j == 0:
                        e.tensor_scalar(acc[r][:, :, :], xpad[r][:, :, 0:L], tap, col(k, "convb", c),
                                        ALU.mult, ALU.add).then_inc(s_cv, 1)
                    else:
                        e.wait_ge(s_cv, 4 * n + j)
                        e.scalar_tensor_tensor(acc[r][:, :, :], xpad[r][:, :, j:j + L], tap, acc[r][:, :, :],
                                               ALU.mult, ALU.add).then_inc(s_cv, 1)
            for h in range(2):
                hs = slice(h * HALF, (h + 1) * HALF)
                e.wait_ge(s_xj, h + 1)
                e.tensor_copy(dtr[:, hs], xq[h][0:DTR, :])
                e.tensor_copy(bc[32:64, hs], xq[h][32:64, :]).then_inc(s_xe, 1)
            for n, (c, h) in enumerate(xblocks):
                r = n % 2
                hs = slice(h * HALF, (h + 1) * HALF)
                e.wait_ge(s_dt, n + 1)
                e.wait_ge(s_az, 3 * n + 1)
                e.tensor_scalar(rz[r][:, :], dq[r][:, :], col(k, "dtb", c), 0.0, ALU.add, ALU.max
                                ).then_inc(s_rz, 1)
                e.wait_ge(s_rz, n + 1)
                e.wait_ge(s_az, 3 * n + 3)
                e.tensor_tensor(m.delta[:, c, hs], rz[r][:, :], lz[r][:, :], ALU.add).then_inc(s_dl, 1)
                e.wait_ge(s_dl, 2 * n + 1)
                e.tensor_tensor(m.du[:, c, hs], m.delta[:, c, hs], m.u[:, c, hs], ALU.mult).then_inc(s_dl, 1)
            for c in range(CH):
                i = e.tensor_scalar(m.diagD[:, c, :], k.ident[:, :], col(k, "dpar", c), None, ALU.mult)
            e.tensor_tensor(k.x[:, :, :], k.x[:, :, :],
                            rowvec(k, "outb").unsqueeze(1).to_broadcast([P, TILES, D]), ALU.add)

        @block.sync
        def _(e):
            e.wait_ge(s_xe, 2)
            e.dma_start(m.bc_dram, bc[32:64, :]).then_inc(s_bc, 16)
            e.wait_ge(s_bc, 16)


def mamba_scan(nc, k, m):
    with ExitStack() as ctx:
        sb, ps, sem = tools(nc, ctx)
        ND = 4
        Bb = [sb(f"Bb{i}", [P, TOK]) for i in range(2)]
        Cb = [sb(f"Cb{i}", [P, TOK]) for i in range(2)]
        A = [k.xn[:, 4 * i:4 * i + 4, :].rearrange("p t d -> p (t d)") for i in range(2)]
        dbu = [sb(f"dbu{i}", [P, TOK]) for i in range(ND)]
        hh = [sb(f"hh{i}", [P, TOK]) for i in range(2)]
        hc = [sb(f"hc{i}", [P, TOK]) for i in range(2)]
        Y = ps("Y", [P, CH, TOK])
        s_bl = [sem(f"n_bl{i}") for i in range(2)]
        s_cl = [sem(f"n_cl{i}") for i in range(2)]
        s_A = sem("n_A")
        s_bu = sem("n_bu")
        s_h = sem("n_h")
        s_hc = sem("n_hc")
        s_y = sem("n_y")
        s_yg = sem("n_yg")
        s_o = sem("n_o")
        block = ctx.enter_context(nc.Block())
        STEPS = DS * CH

        def steps(e, body):
            with e.Fori(0, DS // 2) as j:
                for q in range(2):
                    for c in range(CH):
                        body(j * 2 + q, q, c, j * (2 * CH) + (q * CH + c))

        @block.sync
        def _(e):
            def load(n, buf, row, s):
                src = m.bc_dram[row + n:row + n + 1, :] if isinstance(n, int) else m.bc_dram[bass.ds(n + row, 1), :]
                e.dma_start(buf[:, :], src.to_broadcast([P, TOK])).then_inc(s, 16)

            for q in range(2):
                load(q, Bb[q], 0, s_bl[q])
                load(q, Cb[q], DS, s_cl[q])
            with e.Fori(1, DS // 2) as j:
                for q in range(2):
                    e.wait_ge(s_bu, j * (2 * CH) + (q - 1) * CH)
                    load(j * 2 + q, Bb[q], 0, s_bl[q])
                    e.wait_ge(s_hc, j * (2 * CH) + ((q - 1) * CH + 2))
                    load(j * 2 + q, Cb[q], DS, s_cl[q])

        @block.scalar
        def _(e):
            def body(n, q, c, s):
                by_batch = lambda a: a.rearrange("p (b l) -> p b l", l=L)[:, :, 1:L]
                e.wait_ge(s_h, s + 3)
                e.activation(by_batch(A[c % 2]), by_batch(m.delta[:, c, :]), ACT.Exp,
                             scale=m.negA[:, c, :][:, bass.ds(n, 1)]).then_inc(s_A, 1)

            steps(e, body)

        @block.gpsimd
        def _(e):
            def body(n, q, c, s):
                if c == 0:
                    e.wait_ge(s_bl[q], n * 8 + (16 - 8 * q))
                e.wait_ge(s_h, s + 1)
                e.tensor_tensor(dbu[c % ND][:, :], m.du[:, c, :], Bb[q][:, :], ALU.mult).then_inc(s_bu, 1)

            steps(e, body)

        @block.vector
        def _(e):
            for r in range(2):
                zero = A[r].rearrange("p (b l) -> p b l", l=L)[:, :, 0]
                for b in range(0, B, B // 2):
                    e.memset(zero[:, b:b + B // 2], 0.0).then_inc(s_h, 1)
                e.memset(hc[r][:, 0:1], 0.0).then_inc(s_hc, 1)

            def emit_hc(n, q, c, s):
                if c == 0:
                    e.wait_ge(s_cl[q], n * 8 + (16 - 8 * q))
                e.wait_ge(s_h, s + 5)
                e.wait_ge(s_y, s + 1)
                e.tensor_tensor(hc[c % 2][:, :], hh[c % 2][:, :], Cb[q][:, :], ALU.mult).then_inc(s_hc, 1)

            def body(n, q, c, s):
                e.wait_ge(s_A, s + 1)
                e.wait_ge(s_bu, s + 1)
                e.wait_ge(s_hc, s + 1)
                e.tensor_tensor_scan(hh[c % 2][:, :], A[c % 2], dbu[c % ND][:, :], 0.0,
                                     ALU.mult, ALU.add).then_inc(s_h, 1)
                if c:
                    emit_hc(n, q, c - 1, s - 1)
                if c == CH - 1:
                    emit_hc(n, q, c, s)

            steps(e, body)
            e.wait_ge(s_y, STEPS + 2)
            for c in range(CH):
                e.tensor_tensor(m.sres[:, c, :], Y[:, c, :], m.sres[:, c, :], ALU.mult).then_inc(s_yg, 1)
            for g in range(TILES // 2):
                e.wait_ge(s_o, g + 1)
                x = k.x[:, 2 * g:2 * g + 2, :].rearrange("p t d -> p (t d)")
                e.tensor_tensor(x, x, Y[:, g, 0:2 * D], ALU.add)

        @block.tensor
        def _(e):
            for c in range(CH):
                for h in range(2):
                    i = e.matmul(Y[:, c, h * HALF:(h + 1) * HALF], m.diagD[:, c, :],
                                 m.u[:, c, h * HALF:(h + 1) * HALF], start=True, stop=False,
                                 skip_group_check=True)
                if c >= CH - 2:
                    i.then_inc(s_y, 1)

            def body(n, q, c, s):
                e.wait_ge(s_hc, s + 3)
                for h in range(2):
                    i = e.matmul(Y[:, c, h * HALF:(h + 1) * HALF], k.ident[:, :],
                                 hc[c % 2][:, h * HALF:(h + 1) * HALF], start=False, stop=True,
                                 skip_group_check=True)
                i.then_inc(s_y, 1)

            steps(e, body)
            e.wait_ge(s_yg, CH)
            for t in range(TILES):
                for c in range(CH):
                    i = e.matmul(Y[:, t // 2, (t % 2) * D:(t % 2 + 1) * D], m.sres[:, c, t * P:(t + 1) * P],
                                 k.w_out[:, c, :], start=c == 0, stop=c == CH - 1)
                if t % 2:
                    i.then_inc(s_o, 1)


def spiking_ffn(nc, k):
    beta, thr, steps = 0.9, 1.0, 5
    with ExitStack() as ctx:
        sb, ps, sem = tools(nc, ctx)
        r_sb = [sb(f"r{i}", [P, HALF]) for i in range(2)]
        hT = sb("hT", [P, FM, TOK])
        y = [sb(f"y{i}", [P, 2 * D]) for i in range(2)]
        mem = [sb(f"mem{i}", [P, 2 * D]) for i in range(2)]
        drive = sb("drive", [P, 2 * D])
        cnt = sb("cnt", [P, 2 * D])
        fp = [ps(f"fp{i}") for i in range(4)]
        yp = [ps(f"yp{i}") for i in range(2)]
        s_fc = sem("f_fc")
        s_re = sem("f_re")
        s_h = sem("f_h")
        s_pr = sem("f_pr")
        s_y = sem("f_y")
        s_d = sem("f_d")
        block = ctx.enter_context(nc.Block())
        blocks = [(m, h) for h in range(2) for m in range(FM)]

        @block.tensor
        def _(e):
            e.wait_ge(k.s_w3, k.n_w3)
            for n, (m, h) in enumerate(blocks):
                if n >= 4:
                    e.wait_ge(s_re, n - 3)
                for kt in range(KD):
                    i = e.matmul(fp[n % 4][:, :], k.w_fc[:, kt, m * P:(m + 1) * P],
                                 k.xT[:, kt, h * HALF:(h + 1) * HALF], start=kt == 0, stop=kt == 1)
                i.then_inc(s_fc, 1)
            for g in range(TILES // 2):
                e.wait_ge(s_h, FM * (g // 2 + 1))
                if g >= 2:
                    e.wait_ge(s_y, g - 1)
                for u in range(2):
                    t = 2 * g + u
                    for m in range(FM):
                        i = e.matmul(yp[g % 2][:, u * D:(u + 1) * D], hT[:, m, t * P:(t + 1) * P],
                                     k.w_pr[:, m, :], start=m == 0, stop=m == FM - 1)
                i.then_inc(s_pr, 1)

        @block.scalar
        def _(e):
            for n in range(len(blocks)):
                e.wait_ge(s_fc, n + 1)
                if n >= 2:
                    e.wait_ge(s_h, n - 1)
                e.activation(r_sb[n % 2][:, :], fp[n % 4][:, :], ACT.Relu).then_inc(s_re, 1)
            for g in range(TILES // 2):
                e.wait_ge(s_pr, g + 1)
                if g >= 2:
                    e.wait_ge(s_d, 14 * (g - 1))
                e.activation(y[g % 2][:, :], yp[g % 2][:, :], ACT.Copy).then_inc(s_y, 1)

        @block.vector
        def _(e):
            for n, (m, h) in enumerate(blocks):
                e.wait_ge(s_re, n + 1)
                r = r_sb[n % 2]
                e.tensor_tensor(hT[:, m, h * HALF:(h + 1) * HALF], r[:, :], r[:, :], ALU.mult).then_inc(s_h, 1)
            n = 0

            def chain(ins):
                nonlocal n
                n += 1
                ins.then_inc(s_d, 1)
                e.wait_ge(s_d, n)

            for g in range(TILES // 2):
                e.wait_ge(s_y, g + 1)
                yg = y[g % 2][:, :]
                cur = yg
                chain(e.tensor_scalar(cnt[:, :], cur, thr, None, ALU.is_gt))
                for s in range(1, steps):
                    nxt = mem[s % 2][:, :]
                    chain(e.scalar_tensor_tensor(drive[:, :], cur, beta, yg, ALU.mult, ALU.add))
                    chain(e.scalar_tensor_tensor(nxt, cur, thr, drive[:, :], ALU.is_gt, ALU.subtract,
                                                 reverse1=True))
                    cur = nxt
                    chain(e.scalar_tensor_tensor(cnt[:, :], cur, thr, cnt[:, :], ALU.is_gt, ALU.add))
                x = k.x[:, 2 * g:2 * g + 2, :].rearrange("p t d -> p (t d)")
                chain(e.scalar_tensor_tensor(x, cnt[:, :], 1.0 / steps, x, ALU.mult, ALU.add))


def windowed_attention(nc, k):
    with ExitStack() as ctx:
        sb, _, _ = tools(nc, ctx)
        qT = sb("q4T", [P, TILES, KD, P])
        kT = sb("k4T", [P, TILES, KD, P])
        vx = sb("vx", [P, TILES, H, DV])
        windowed_projections(nc, k, qT, kT, vx)
        windowed_heads(nc, k, qT, kT, vx)


def windowed_projections(nc, k, qT, kT, vx):
    with ExitStack() as ctx:
        sb, ps, sem = tools(nc, ctx)
        qk = [sb(f"qk{i}", [P, 2 * H, DH]) for i in range(2)]
        t2 = [sb(f"t2{i}", [P, 2 * H, DH]) for i in range(2)]
        t1 = [sb(f"t1{i}", [P, 2 * H, DH]) for i in range(2)]
        rot = [sb(f"rot{i}", [P, 2 * H, DH]) for i in range(2)]
        QK = [ps(f"QK{i}") for i in range(2)]
        V = [ps(f"V{i}") for i in range(2)]
        TQ = [ps(f"TQ{i}") for i in range(2)]
        s_pj = sem("w_pj")
        s_vj = sem("w_vj")
        s_b = sem("w_b")
        s_v = sem("w_v")
        s_sn = sem("w_sn")
        s_cs = sem("w_cs")
        s_rt = sem("w_rt")
        s_tq = sem("w_tq")
        s_qe = sem("w_qe")
        with nc.Block() as block:
            @block.tensor
            def _(e):
                e.wait_ge(k.s_w4, k.n_w4)

                def turn(t):
                    e.wait_ge(s_rt, t + 1)
                    if t >= 2:
                        e.wait_ge(s_qe, t - 1)
                    for c in range(2 * KD):
                        i = e.transpose(TQ[t % 2][:, c * P:(c + 1) * P],
                                        rot[t % 2][:, c * HG:(c + 1) * HG, :].rearrange("p h d -> p (h d)"),
                                        k.ident[:, :])
                    i.then_inc(s_tq, 1)

                for t in range(TILES):
                    if t >= 2:
                        e.wait_ge(s_b, t - 1)
                        e.wait_ge(s_v, t - 1)
                    tok = slice(t * P, (t + 1) * P)
                    for src, w, dst in ((k.xT, k.w4[0], QK[t % 2][:, 0:D]), (k.c0T, k.w4[1], QK[t % 2][:, D:2 * D]),
                                        (k.c0T, k.w4[2], V[t % 2][:, 0:D])):
                        for c in range(KD):
                            i = e.matmul(dst, src[:, c, tok], w[:, c, :], start=c == 0, stop=c == 1)
                        if w is not k.w4[0]:
                            i.then_inc(s_pj if w is k.w4[1] else s_vj, 1)
                    if t:
                        turn(t - 1)
                turn(TILES - 1)

            @block.scalar
            def _(e):
                for t in range(TILES):
                    e.wait_ge(s_tq, t + 1)
                    src = TQ[t % 2][:, :].rearrange("p (c n) -> p c n", n=P)
                    e.activation(qT[:, t, :, :], src[:, 0:KD, :], ACT.Copy)
                    e.activation(kT[:, t, :, :], src[:, KD:2 * KD, :], ACT.Copy).then_inc(s_qe, 1)

            @block.gpsimd
            def _(e):
                e.wait_ge(k.s_w4, k.n_w4)
                e.memset(vx[:, :, :, DH:DV], 1.0)

                for t in range(TILES):
                    e.wait_ge(s_b, t + 1)
                    if t >= 2:
                        e.wait_ge(s_rt, t - 1)
                    hd = DH // 2
                    sn = [k.trig[:, 1, i * hd:(i + 1) * hd].unsqueeze(1).to_broadcast([P, 2 * H, hd]) for i in range(2)]
                    e.tensor_tensor(t2[t % 2][:, :, 0:hd], qk[t % 2][:, :, hd:DH], sn[0], ALU.mult)
                    e.tensor_tensor(t2[t % 2][:, :, hd:DH], qk[t % 2][:, :, 0:hd], sn[1], ALU.mult).then_inc(s_sn, 1)

            @block.vector
            def _(e):
                e.wait_ge(k.s_w4, k.n_w4)
                bias = k.rows[:, ROWV["bq4"]:ROWV["bq4"] + 2, :].rearrange("p r (h d) -> p (r h) d", d=DH)

                for t in range(TILES):
                    r = t % 2
                    e.wait_ge(s_pj, t + 1)
                    e.wait_ge(s_sn, t - 1) if t >= 2 else None
                    e.tensor_tensor(qk[r][:, :, :], QK[r][:, :].rearrange("p (h d) -> p h d", d=DH), bias, ALU.add
                                    ).then_inc(s_b, 1)
                    e.wait_ge(s_vj, t + 1)
                    e.tensor_tensor(vx[:, t, :, 0:DH], V[r][:, 0:D].rearrange("p (h d) -> p h d", d=DH),
                                    rowvec(k, "bv4").rearrange("p (h d) -> p h d", d=DH), ALU.add
                                    ).then_inc(s_v, 1)
                    e.wait_ge(s_b, t + 1)
                    cs = k.trig[:, 0, :].unsqueeze(1).to_broadcast([P, 2 * H, DH])
                    e.tensor_tensor(t1[r][:, :, :], qk[r][:, :, :], cs, ALU.mult).then_inc(s_cs, 1)
                    e.wait_ge(s_cs, t + 1)
                    e.wait_ge(s_sn, t + 1)
                    if t >= 2:
                        e.wait_ge(s_tq, t - 1)
                    e.tensor_tensor(rot[r][:, :, :], t1[r][:, :, :], t2[r][:, :, :], ALU.add).then_inc(s_rt, 1)
                e.tensor_tensor(k.x[:, :, :], k.x[:, :, :],
                                rowvec(k, "bo4").unsqueeze(1).to_broadcast([P, TILES, D]), ALU.add)


def windowed_heads(nc, k, qT, kT, vx):
    scale = float(DH) ** -0.5
    with ExitStack() as ctx:
        sb, ps, sem = tools(nc, ctx)
        qs = [sb(f"hqs{i}", [P, KD, P]) for i in range(2)]
        kb = [sb(f"hkb{i}", [P, 2, KD, HG * L]) for i in range(2)]
        mx = [sb(f"hmx{i}", [P, H]) for i in range(2)]
        sm = [sb(f"hsm{i}", [P, H, L]) for i in range(2)]
        pb = [sb(f"hpb{i}", [P, H, P]) for i in range(2)]
        pT = sb("hpT", [P, H, P])
        ri = sb("hri", [P, H])
        on = [sb(f"hon{i}", [P, D]) for i in range(2)]
        onT = sb("honT", [P, KD, P])
        S = ps("hS", [P, 2 * HALF])
        TP = [ps(f"hTP{i}") for i in range(2)]
        O = ps("hO")
        X = ps("hX")
        s_z = sem("h_z")
        s_qs = sem("h_qs")
        s_sc = sem("h_sc")
        s_mx = sem("h_mx")
        s_sm = sem("h_sm")
        s_ex = sem("h_ex")
        s_tp = sem("h_tp")
        s_te = sem("h_te")
        s_to = sem("h_to")
        s_pv = sem("h_pv")
        s_ri = sem("h_ri")
        s_on = sem("h_on")
        s_ot = sem("h_ot")
        s_oe = sem("h_oe")
        s_wo = sem("h_wo")
        s_xa = sem("h_xa")
        block = ctx.enter_context(nc.Block())

        def pipeline(e, sub):
            for i in range(2):
                sub(i, i % 2, lambda d, i=i: i - d >= 0)
            with e.Fori(1, TILES // 2) as j:
                sub(j * 2, 0, lambda d: True)
                sub(j * 2 + 1, 1, lambda d: True)
            for i in range(TILES, TILES + 2):
                sub(i, i % 2, lambda d, i=i: i - d < TILES)

        def at(a, i):
            return a[:, i] if isinstance(i, int) else a[:, bass.ds(i, 1)].squeeze(1)

        @block.tensor
        def _(e):
            def sub(i, r, live):
                if live(2):
                    e.wait_ge(s_on, i - 1)
                    if not isinstance(i, int) or i > 2:
                        e.wait_ge(s_xa, i - 2)
                    for c in range(KD):
                        j = e.transpose(X[:, c * P:(c + 1) * P], on[r][:, c * P:(c + 1) * P], k.ident[:, :])
                    j.then_inc(s_ot, 1)
                if live(0):
                    e.wait_ge(s_qs, i + 1)
                    e.wait_ge(s_sm, i)
                    for c in range(KD):
                        e.matmul(S[:, c * HALF:(c + 1) * HALF], k.ident_bf[:, :], k.causal_bf[:, :],
                                 start=True, stop=True)
                        for b in range(2):
                            j = e.matmul(S[64 * b:64 * b + 64, c * HALF:(c + 1) * HALF],
                                         qs[r][:, c, 64 * b:64 * b + 64], kb[r][:, b, c, :],
                                         start=False, stop=True, skip_group_check=True)
                    j.then_inc(s_sc, 1)
                if live(2):
                    e.wait_ge(s_oe, i - 1)
                    for c in range(KD):
                        j = e.matmul(X[:, D:2 * D], onT[:, c, :], k.w4[3][:, c, :], start=c == 0, stop=c == 1)
                    j.then_inc(s_wo, 1)
                if live(1):
                    q = 1 - r
                    e.wait_ge(s_ex, i * 2)

                    def pv(g):
                        e.wait_ge(s_te if g % 2 == 0 else s_to, (i - 1) * 2 + g // 2 + 1)
                        if g == 0:
                            e.wait_ge(s_on, i - 1)
                        v = at(vx, i - 1)
                        for h in range(4 * g, 4 * g + 4):
                            j = e.matmul(O[:, h * DV:(h + 1) * DV], pT[:, h, :], v[:, h, :], start=True, stop=True)
                        return j

                    for g in range(4):
                        if g >= 2:
                            e.wait_ge(s_te if g % 2 == 0 else s_to, (i - 1) * 2 + g // 2)
                        for u in range(4):
                            j = e.transpose(TP[g % 2][:, u * P:(u + 1) * P], pb[q][:, 4 * g + u, :], k.ident[:, :])
                        j.then_inc(s_tp, 1)
                        if g:
                            pv(g - 1)
                    pv(3).then_inc(s_pv, 1)

            pipeline(e, sub)

        def evac(e, i, g):
            e.wait_ge(s_tp, (i - 1) * 4 + g + 1)
            if g < 2:
                e.wait_ge(s_pv, i - 1)
            src = TP[g % 2][:, :].rearrange("p (u n) -> p u n", n=P)
            if g % 2 == 0:
                e.tensor_copy(pT[:, 4 * g:4 * g + 4, :], src).then_inc(s_te, 1)
            else:
                e.activation(pT[:, 4 * g:4 * g + 4, :], src, ACT.Copy).then_inc(s_to, 1)

        @block.scalar
        def _(e):
            e.wait_ge(s_z, 2)

            def sub(i, r, live):
                if live(2):
                    e.wait_ge(s_ot, i - 1)
                    if not isinstance(i, int) or i > 2:
                        e.wait_ge(s_wo, i - 2)
                    e.activation(onT[:, :, :], X[:, 0:D].rearrange("p (c n) -> p c n", c=KD), ACT.Copy
                                 ).then_inc(s_oe, 1)
                if live(1):
                    evac(e, i, 1)
                    evac(e, i, 3)
                if live(0):
                    if not isinstance(i, int) or i >= 2:
                        e.wait_ge(s_tp, (i - 1) * 4)
                    e.wait_ge(s_sm, i + 1)
                    for b in range(2):
                        rows = slice(64 * b, 64 * b + 64)
                        e.activation(pb[r][rows, :, 64 * b:64 * b + 64], sm[r][rows, :, :], ACT.Exp, scale=scale
                                     ).then_inc(s_ex, 1)

            pipeline(e, sub)

        @block.gpsimd
        def _(e):
            for r in range(2):
                e.memset(pb[r][:, :, :], 0.0).then_inc(s_z, 1)

            def sub(i, r, live):
                if live(0):
                    if not isinstance(i, int) or i >= 2:
                        e.wait_ge(s_sc, i - 1)
                    e.tensor_copy(qs[r][:, :, :], at(qT, i))
                    keys = at(kT, i)
                    for b in range(2):
                        for c in range(KD):
                            j = e.tensor_tensor(kb[r][:, b, c, :].rearrange("p (h n) -> p h n", n=L),
                                                keys[:, c, b * L:(b + 1) * L].unsqueeze(1).to_broadcast([P, HG, L]),
                                                k.own_head[:, :].unsqueeze(2).to_broadcast([P, HG, L]), ALU.mult)
                    j.then_inc(s_qs, 1)

            pipeline(e, sub)

        @block.vector
        def _(e):
            def sub(i, r, live):
                if live(0):
                    e.wait_ge(s_sc, i + 1)
                    Sv = S[:, :].rearrange("p (h n) -> p h n", n=L)
                    e.reduce_max(mx[r][:, :], Sv, AX.X).then_inc(s_mx, 1)
                    e.wait_ge(s_mx, i + 1)
                    if not isinstance(i, int) or i >= 2:
                        e.wait_ge(s_ex, (i - 1) * 2)
                    e.tensor_tensor(sm[r][:, :, :], Sv, mx[r][:, :].unsqueeze(2).to_broadcast([P, H, L]),
                                    ALU.subtract).then_inc(s_sm, 1)
                if live(2):
                    e.wait_ge(s_wo, i - 1)
                    x = at(k.x, i - 2)
                    e.tensor_tensor(x, x, X[:, D:2 * D], ALU.add).then_inc(s_xa, 1)
                if live(1):
                    evac(e, i, 0)
                    evac(e, i, 2)
                    e.wait_ge(s_pv, i)
                    Ov = O[:, 0:H * DV].rearrange("p (h d) -> p h d", d=DV)
                    e.reciprocal(ri[:, :], Ov[:, :, DH]).then_inc(s_ri, 1)
                    e.wait_ge(s_ri, i)
                    e.tensor_tensor(on[1 - r][:, :].rearrange("p (h d) -> p h d", d=DH), Ov[:, :, 0:DH],
                                    ri[:, :].unsqueeze(2).to_broadcast([P, H, DH]), ALU.mult).then_inc(s_on, 1)

            pipeline(e, sub)


def phase_attention(nc, k):
    scale = 1.0 / float(D) ** 0.5
    n_pairs = float(L * L)
    with ExitStack() as ctx:
        sb, ps, sem = tools(nc, ctx)
        qT = sb("q5T", [P, KD, TOK])
        kT = sb("k5T", [P, KD, TOK])
        v = sb("v5", [P, TILES, D])
        qp = sb("qp", [P, TILES, 2])
        diag = sb("diag", [P, 2, TILES, L])
        dd = sb("dd", [P, 2, TILES, L])
        dq = sb("dq", [P, 2, TILES, L])
        dist = sb("dist", [P, TILES, L])
        dev = sb("dev", [P, TILES, L])
        small = sb("small", [P, 8, TILES])
        rowsum, mean, rowsq, var, std, thr, mx, tot = (small[:, i, :] for i in range(8))
        ri = sb("ri5", [P, TILES])
        ok = sb("ok", [P, TILES, L])
        ady = sb("ady", [P, TILES, L])
        sm = sb("sm5", [P, TILES, L])
        pb = sb("pb5", [P, TILES, P])
        pT = sb("p5T", [P, TILES, P])
        cn = sb("cn", [P, TILES, D])
        cnT = sb("cnT", [P, KD, TOK])
        nrm = sb("nrm", [P, 2, TILES])
        qsq = sb("qsq", [P, TILES, 2])
        re = sb("re", [P, TILES, 2])
        reT = sb("reT", [2, TOK])
        bias = sb("bias5", [P, D])
        BK = [ps(f"BK{i}") for i in range(8)]
        s_pe = sem("p_pe")
        s_ac = sem("p_ac")
        s_ve = sem("p_ve")
        s_z = sem("p_z")
        block = ctx.enter_context(nc.Block())
        pe_at, ac_at, ve_at = {}, {}, {}
        pe_steps = (["qp"] + [("qk", n) for n in range(8)] + ["row"] + [("v", g) for g in range(4)] + ["sum"]
                    + ["scores", "sumsq", "reT"] + [("pT", g) for g in range(2)] + [("pv", g) for g in range(4)]
                    + [("cT", g) for g in range(4)] + [("o", g) for g in range(4)])
        for n, name in enumerate(pe_steps):
            pe_at[name] = n + 1
        ac_steps = ([("qk", n) for n in range(8)] + [("v", g) for g in range(4)] + ["nrm", "std", "exp0", "exp", "reT"]
                    + [("pT", 1)] + [("cT", g) for g in range(4)])
        for n, name in enumerate(ac_steps):
            ac_at[name] = n + 1
        ve_steps = ["qp", "qsq", "nrm2", "diag", "dd", "dq", "dist", "rowsum", "mean", "dev", "devsq", "rowsq",
                    "var", "nrmx", "nri", "re", "bias", "ady0", "ady", "ok", "okc", "thr", "in", "ok2", "add", "masked",
                    "mx", "sub", "den", "ri", ("pT", 0)] + [("cn", g) for g in range(4)] + ["xadd0", "xadd"] + [("x", g) for g in range(4)]
        for n, name in enumerate(ve_steps):
            ve_at[name] = n + 1
        made = {"pe": 0, "ac": 0, "ve": 0}

        def mark(ins, table, who, sem_, name):
            made[who] += 1
            assert table[name] == made[who], (name, made[who])
            ins.then_inc(sem_, 1)

        @block.tensor
        def _(e):
            done = lambda ins, name: mark(ins, pe_at, "pe", s_pe, name)
            ac = lambda name: e.wait_ge(s_ac, ac_at[name])
            ve = lambda name: e.wait_ge(s_ve, ve_at[name])
            e.wait_ge(k.s_w5, k.n_w5)
            for t in range(TILES):
                for c in range(KD):
                    i = e.matmul(BK[6][:, 2 * t:2 * t + 2], k.xT[:, c, t * P:(t + 1) * P], k.wtq[:, c, :],
                                 start=c == 0, stop=c == 1)
            done(i, "qp")
            n = 0
            for w, m in ((0, 0), (0, 1), (1, 0), (1, 1)):
                for h in range(2):
                    if n >= 4:
                        ac(("qk", n - 4))
                    for c in range(KD):
                        i = e.matmul(BK[n % 4][:, :], k.w5[w][:, c, m * P:(m + 1) * P],
                                     k.xT[:, c, h * HALF:(h + 1) * HALF], start=c == 0, stop=c == 1)
                    done(i, ("qk", n))
                    n += 1
            ve("diag")
            for g in range(2):
                i = e.matmul(BK[4 + g][:, :], k.same_batch[:, :], diag[:, g, :, :].rearrange("p t n -> p (t n)"),
                             start=True, stop=True)
            done(i, "row")
            for g in range(4):
                ac(("qk", 4 + g))
                for u in range(2):
                    t = 2 * g + u
                    for c in range(KD):
                        i = e.matmul(BK[g][:, u * D:(u + 1) * D], k.xT[:, c, t * P:(t + 1) * P], k.w5[2][:, c, :],
                                     start=c == 0, stop=c == 1)
                done(i, ("v", g))
            ve("rowsum")
            done(e.matmul(BK[6][:, 64:64 + TILES], k.same_batch[:, :], rowsum, start=True, stop=True), "sum")
            for t in range(TILES):
                for c in range(KD):
                    for b in range(2):
                        q = slice(t * P + 64 * b, t * P + 64 * b + 64)
                        i = e.matmul(BK[7][64 * b:64 * b + 64, t * L:(t + 1) * L], qT[:, c, q], kT[:, c, q],
                                     start=c == 0, stop=c == 1)
            done(i, "scores")
            ve("rowsq")
            done(e.matmul(BK[6][:, 128:128 + TILES], k.same_batch[:, :], rowsq, start=True, stop=True), "sumsq")
            ve("re")
            ac(("v", 3))
            for t in range(TILES):
                i = e.transpose(BK[t // 4][0:2, (t % 4) * P:(t % 4 + 1) * P], re[:, t, :], k.ident[:, :])
            done(i, "reT")
            ve("ri")
            ac("exp")
            ac("reT")
            for g in range(2):
                for u in range(4):
                    i = e.transpose(BK[4 + g][:, u * P:(u + 1) * P], pb[:, 4 * g + u, :], k.ident[:, :])
                done(i, ("pT", g))
            ve(("pT", 0))
            ac(("pT", 1))
            for g in range(4):
                for u in range(2):
                    t = 2 * g + u
                    i = e.matmul(BK[g][:, u * D:(u + 1) * D], pT[:, t, :], v[:, t, :], start=True, stop=True)
                done(i, ("pv", g))
            for g in range(4):
                ve(("cn", g))
                for u in range(2):
                    for c in range(KD):
                        i = e.transpose(BK[4 + g][:, (2 * u + c) * P:(2 * u + c + 1) * P],
                                        cn[:, 2 * g + u, c * P:(c + 1) * P], k.ident[:, :])
                done(i, ("cT", g))
            for g in range(4):
                ac(("cT", g))
                for u in range(2):
                    t = 2 * g + u
                    for c in range(KD):
                        e.matmul(BK[g][:, u * D:(u + 1) * D], cnT[:, c, t * P:(t + 1) * P], k.w5[3][:, c, :],
                                 start=c == 0, stop=False)
                    i = e.matmul(BK[g][:, u * D:(u + 1) * D], reT[:, t * P:(t + 1) * P], k.wfq[:, :],
                                 start=False, stop=True)
                done(i, ("o", g))

        @block.scalar
        def _(e):
            done = lambda ins, name: mark(ins, ac_at, "ac", s_ac, name)
            pe = lambda name: e.wait_ge(s_pe, pe_at[name])
            ve = lambda name: e.wait_ge(s_ve, ve_at[name])
            n = 0
            for dst, b in ((qT, "bq5"), (kT, "bk5")):
                for m in range(KD):
                    for h in range(2):
                        pe(("qk", n))
                        done(e.activation(dst[:, m, h * HALF:(h + 1) * HALF], BK[n % 4][:, :], ACT.Identity,
                                          bias=col(k, b, m)), ("qk", n))
                        n += 1
            for g in range(4):
                pe(("v", g))
                done(e.activation(v[:, 2 * g:2 * g + 2, :].rearrange("p t d -> p (t d)"), BK[g][:, :], ACT.Copy),
                     ("v", g))
            ve("nrm2")
            done(e.activation(nrm[:, 1, :], nrm[:, 0, :], ACT.Sqrt), "nrm")
            ve("var")
            done(e.activation(std, var, ACT.Sqrt), "std")
            e.wait_ge(s_z, 1)
            ve("sub")
            for b in range(2):
                rows = slice(64 * b, 64 * b + 64)
                done(e.activation(pb[rows, :, 64 * b:64 * b + 64], sm[rows, :, :], ACT.Exp, scale=scale),
                     "exp0" if b == 0 else "exp")
            pe("reT")
            for g in range(2):
                i = e.activation(reT[:, g * HALF:(g + 1) * HALF], BK[g][0:2, :], ACT.Copy)
            done(i, "reT")
            pe(("pT", 1))
            done(e.activation(pT[:, 4:8, :], BK[5][:, :].rearrange("p (t n) -> p t n", n=P), ACT.Copy), ("pT", 1))
            for g in range(4):
                pe(("cT", g))
                src = BK[4 + g][:, :].rearrange("p (u c n) -> p c u n", u=2, c=KD)
                dst = cnT[:, :, 2 * g * P:(2 * g + 2) * P].rearrange("p c (u n) -> p c u n", u=2)
                done(e.activation(dst, src, ACT.Copy), ("cT", g))

        @block.gpsimd
        def _(e):
            e.memset(pb[:, :, :], 0.0).then_inc(s_z, 1)

        @block.vector
        def _(e):
            pe = lambda name: e.wait_ge(s_pe, pe_at[name])
            ac = lambda name: e.wait_ge(s_ac, ac_at[name])

            def done(ins, name):
                mark(ins, ve_at, "ve", s_ve, name)

            def chain(ins, name):
                done(ins, name)
                e.wait_ge(s_ve, ve_at[name])

            wide = lambda a: a.unsqueeze(2).to_broadcast([P, TILES, L])
            e.wait_ge(k.s_w5, k.n_w5)
            pe("qp")
            chain(e.tensor_tensor(qp[:, :, :], BK[6][:, 0:2 * TILES].rearrange("p (t w) -> p t w", w=2),
                                  k.btq[:, :].unsqueeze(1).to_broadcast([P, TILES, 2]), ALU.add), "qp")
            chain(e.tensor_tensor(qsq[:, :, :], qp[:, :, :], qp[:, :, :], ALU.mult), "qsq")
            chain(e.tensor_tensor(nrm[:, 0, :], qsq[:, :, 0], qsq[:, :, 1], ALU.add), "nrm2")
            for g in range(2):
                i = e.tensor_tensor(diag[:, g, :, :], wide(qp[:, :, g]),
                                    k.diag64[:, :].unsqueeze(1).to_broadcast([P, TILES, L]), ALU.mult)
            chain(i, "diag")
            pe("row")
            for g in range(2):
                i = e.tensor_tensor(dd[:, g, :, :], wide(qp[:, :, g]),
                                    BK[4 + g][:, :].rearrange("p (t n) -> p t n", n=L), ALU.subtract)
            chain(i, "dd")
            chain(e.tensor_tensor(dq[:, :, :, :].rearrange("p g t n -> p (g t n)"),
                                  dd[:, :, :, :].rearrange("p g t n -> p (g t n)"),
                                  dd[:, :, :, :].rearrange("p g t n -> p (g t n)"), ALU.mult), "dq")
            chain(e.tensor_tensor(dist[:, :, :], dq[:, 0, :, :], dq[:, 1, :, :], ALU.add), "dist")
            chain(e.reduce_sum(rowsum, dist[:, :, :], AX.X), "rowsum")
            pe("sum")
            chain(e.tensor_scalar(mean, BK[6][:, 64:64 + TILES], 1.0 / n_pairs, None, ALU.mult), "mean")
            chain(e.tensor_tensor(dev[:, :, :], dist[:, :, :], wide(mean), ALU.subtract), "dev")
            chain(e.tensor_tensor(dev[:, :, :], dev[:, :, :], dev[:, :, :], ALU.mult), "devsq")
            chain(e.reduce_sum(rowsq, dev[:, :, :], AX.X), "rowsq")
            pe("sumsq")
            done(e.tensor_scalar(var, BK[6][:, 128:128 + TILES], 1.0 / (n_pairs - 1.0), None, ALU.mult), "var")
            ac("nrm")
            chain(e.tensor_scalar(nrm[:, 0, :], nrm[:, 1, :], 1e-12, None, ALU.max), "nrmx")
            chain(e.reciprocal(nrm[:, 1, :], nrm[:, 0, :]), "nri")
            done(e.scalar_tensor_tensor(re[:, :, :], qp[:, :, :], 0.1,
                                        nrm[:, 1, :].unsqueeze(2).to_broadcast([P, TILES, 2]), ALU.mult, ALU.mult),
                 "re")
            done(e.scalar_tensor_tensor(bias[:, :], rowvec(k, "bfq"), 0.1, rowvec(k, "bo5"), ALU.mult, ALU.add),
                 "bias")
            chain(e.tensor_scalar(ady[:, :, :], dd[:, 1, :, :], -4096.0, None, ALU.mult), "ady0")
            chain(e.scalar_tensor_tensor(ady[:, :, :], dd[:, 1, :, :], 4096.0, ady[:, :, :], ALU.mult, ALU.max), "ady")
            chain(e.scalar_tensor_tensor(ok[:, :, :], dd[:, 0, :, :], -1.0, ady[:, :, :], ALU.mult, ALU.is_le), "ok")
            chain(e.tensor_tensor(ok[:, :, :], ok[:, :, :], k.causal[:, :].unsqueeze(1).to_broadcast([P, TILES, L]),
                                  ALU.mult), "okc")
            ac("std")
            chain(e.scalar_tensor_tensor(thr, std, 1.25, mean, ALU.mult, ALU.add), "thr")
            chain(e.tensor_tensor(dev[:, :, :], dist[:, :, :], wide(thr), ALU.is_le), "in")
            chain(e.tensor_tensor(ok[:, :, :], ok[:, :, :], dev[:, :, :], ALU.mult), "ok2")
            chain(e.tensor_scalar(ok[:, :, :], ok[:, :, :], -NEG, NEG, ALU.mult, ALU.add), "add")
            pe("scores")
            chain(e.tensor_tensor(sm[:, :, :], BK[7][:, :].rearrange("p (t n) -> p t n", n=L), ok[:, :, :], ALU.add),
                  "masked")
            chain(e.reduce_max(mx, sm[:, :, :], AX.X), "mx")
            done(e.tensor_tensor(sm[:, :, :], sm[:, :, :], wide(mx), ALU.subtract), "sub")
            ac("exp")
            for b in range(2):
                rows = slice(64 * b, 64 * b + 64)
                i = e.reduce_sum(tot[rows], pb[rows, :, 64 * b:64 * b + 64], AX.X)
            chain(i, "den")
            done(e.reciprocal(ri[:, :], tot), "ri")
            pe(("pT", 0))
            done(e.tensor_copy(pT[:, 0:4, :], BK[4][:, :].rearrange("p (t n) -> p t n", n=P)), ("pT", 0))
            for g in range(4):
                pe(("pv", g))
                for u in range(2):
                    t = 2 * g + u
                    i = e.scalar_tensor_tensor(cn[:, t, :], BK[g][:, u * D:(u + 1) * D], ri[:, t:t + 1],
                                               rowvec(k, "bv5"), ALU.mult, ALU.add)
                done(i, ("cn", g))
            chain(e.tensor_tensor(k.x[:, :, :].rearrange("p t d -> p (t d)"), k.x[:, :, :].rearrange("p t d -> p (t d)"),
                                  k.xn[:, :, :].rearrange("p t d -> p (t d)"), ALU.add), "xadd0")
            chain(e.tensor_tensor(k.x[:, :, :], k.x[:, :, :], bias[:, :].unsqueeze(1).to_broadcast([P, TILES, D]),
                                  ALU.add), "xadd")
            for g in range(4):
                pe(("o", g))
                x = k.x[:, 2 * g:2 * g + 2, :].rearrange("p t d -> p (t d)")
                done(e.tensor_tensor(x, x, BK[g][:, :], ALU.add), ("x", g))


def experts(nc, k, t_w1, t_w2):
    with ExitStack() as ctx:
        sb, ps, sem = tools(nc, ctx)
        score = sb("score", [P, TILES, E])
        top = sb("top", [P, TILES, 8])
        idx = sb("idx", [P, TILES, 8], U32)
        idf = sb("idf", [P, TILES, 8])
        pick = [sb(f"pick{i}", [P, TILES, E]) for i in range(TOPK)]
        comb = sb("comb", [P, TILES, E])
        combT = sb("combT", [E, TOK])
        w1 = [sb(f"ew1{i}", [P, KD, D]) for i in range(2)]
        w2 = [sb(f"ew2{i}", [P, KD, D]) for i in range(2)]
        b1 = [sb(f"eb1{i}", [P, 2]) for i in range(2)]
        hT = [sb(f"ehT{i}", [P, KD, TOK]) for i in range(2)]
        HB = [ps(f"HB{i}") for i in range(4)]
        OB = [ps(f"OB{i}") for i in range(4)]
        s_g = sem("e_g")
        s_t = sem("e_t")
        s_ct = sem("e_ct")
        s_w = [sem(f"e_w{i}") for i in range(2)]
        s_b1 = sem("e_b1")
        s_h = sem("e_h")
        s_r = sem("e_r")
        s_o = sem("e_o")
        s_a = sem("e_a")
        block = ctx.enter_context(nc.Block())
        blocks = [(m, h) for h in range(2) for m in range(KD)]

        def per_expert(e, body):
            with e.Fori(0, E // 2) as j:
                for r in range(2):
                    body(j * 2 + r, r, j)

        @block.sync
        def _(e):
            def load(x, r):
                if isinstance(x, int):
                    a, b = t_w1[x], t_w2[x]
                else:
                    a, b = t_w1[bass.ds(x, 1)].squeeze(0), t_w2[bass.ds(x, 1)].squeeze(0)
                e.dma_start(w1[r][:, :, :], a.rearrange("(c p) n -> p c n", p=P)).then_inc(s_w[r], 16)
                e.dma_start(w2[r][:, :, :], b.rearrange("(c p) n -> p c n", p=P)).then_inc(s_w[r], 16)

            for x in range(2):
                load(x, x)
            with e.Fori(1, E // 2) as j:
                for r in range(2):
                    e.wait_ge(s_o, j * 8 + (4 * r - 3))
                    load(j * 2 + r, r)

        @block.tensor
        def _(e):
            e.wait_ge(k.s_w6, k.n_w6)
            for t in range(TILES):
                for c in range(KD):
                    i = e.matmul(OB[0][:, t * E:(t + 1) * E], k.xT[:, c, t * P:(t + 1) * P], k.wg[:, c, :],
                                 start=c == 0, stop=c == 1)
            i.then_inc(s_g, 1)

            def body(x, r, j):
                e.wait_ge(s_w[r], j * 32 + 32)
                for n, (m, h) in enumerate(blocks):
                    s = x * 4 + n
                    e.wait_ge(s_r, s + 1)
                    for c in range(KD):
                        i = e.matmul(HB[n][:, :], w1[r][:, c, m * P:(m + 1) * P],
                                     k.xT[:, c, h * HALF:(h + 1) * HALF], start=c == 0, stop=c == 1)
                    i.then_inc(s_h, 1)
                for g in range(4):
                    if g % 2 == 0:
                        e.wait_ge(s_r, x * 4 + (4 + 2 * (g // 2) + 2))
                    e.wait_ge(s_a, x * 4 + (g + 1))
                    for u in range(2):
                        t = 2 * g + u
                        for c in range(KD):
                            i = e.matmul(OB[g][:, u * D:(u + 1) * D], hT[r][:, c, t * P:(t + 1) * P], w2[r][:, c, :],
                                         start=c == 0, stop=c == 1)
                    i.then_inc(s_o, 1)

            e.wait_ge(s_t, 7)
            e.transpose(OB[3][:, 0:P], k.ident[:, :], k.ident[:, :]).then_inc(s_o, 1)
            for t in range(TILES):
                i = e.transpose(OB[1 + t // 4][0:E, (t % 4) * P:(t % 4 + 1) * P], comb[:, t, :], k.ident[:, :])
            i.then_inc(s_g, 1)
            e.wait_ge(s_ct, 2)
            for g in range(4):
                for u in range(2):
                    t = 2 * g + u
                    i = e.matmul(OB[g][:, u * D:(u + 1) * D], combT[:, t * P:(t + 1) * P], k.b2[:, :],
                                 start=True, stop=True)
                i.then_inc(s_g, 1)
            per_expert(e, body)

        @block.scalar
        def _(e):
            for n in range(4):
                e.activation(hT[n % 2][:, 0, n:n + 1], k.ident[:, 0:1], ACT.Copy).then_inc(s_r, 1)
            e.wait_ge(s_g, 2)
            for n in range(2):
                e.activation(combT[:, n * HALF:(n + 1) * HALF], OB[1 + n][0:E, :], ACT.Copy).then_inc(s_ct, 1)
            e.wait_ge(s_r, 4)

            def body(x, r, j):
                e.wait_ge(s_b1, x + 1)
                for n, (m, h) in enumerate(blocks):
                    e.wait_ge(s_h, x * 4 + (n + 1))
                    if n == 0:
                        e.wait_ge(s_o, j * 8 + 1)
                    e.activation(hT[r][:, m, h * HALF:(h + 1) * HALF], HB[n][:, :], ACT.Relu, bias=b1[r][:, m:m + 1]
                                 ).then_inc(s_r, 1)

            per_expert(e, body)

        @block.gpsimd
        def _(e):
            a0, _ = COLS["b1"]

            def body(x, r, j):
                e.wait_ge(s_r, x * 4 + 1)
                e.tensor_copy(b1[r][:, :], k.cols[:, bass.ds(x * 2 + a0, 2)]).then_inc(s_b1, 1)

            per_expert(e, body)

        @block.vector
        def _(e):
            e.wait_ge(k.s_w6, k.n_w6)
            n = 0

            def chain(ins):
                nonlocal n
                n += 1
                ins.then_inc(s_t, 1)
                e.wait_ge(s_t, n)

            e.wait_ge(s_g, 1)
            chain(e.tensor_tensor(score[:, :, :], OB[0][:, 0:TILES * E].rearrange("p (t x) -> p t x", x=E),
                                  k.gateb[:, :].unsqueeze(1).to_broadcast([P, TILES, E]), ALU.add))
            for t in range(TILES):
                i = e.max(top[:, t, :], score[:, t, :])
            chain(i)
            for t in range(TILES):
                i = e.max_index(idx[:, t, :], top[:, t, :], score[:, t, :])
            chain(i)
            chain(e.tensor_copy(idf[:, :, :], idx[:, :, :]))
            for i in range(TOPK):
                ins = e.tensor_tensor(pick[i][:, :, :], k.iota8[:, :].unsqueeze(1).to_broadcast([P, TILES, E]),
                                      idf[:, :, i:i + 1].to_broadcast([P, TILES, E]), ALU.is_equal)
            chain(ins)
            for i in range(TOPK):
                ins = e.tensor_tensor(pick[i][:, :, :], pick[i][:, :, :], top[:, :, i:i + 1].to_broadcast([P, TILES, E]),
                                      ALU.mult)
            chain(ins)
            chain(e.tensor_tensor(comb[:, :, :], pick[0][:, :, :], pick[1][:, :, :], ALU.add))
            for g in range(4):
                e.wait_ge(s_g, 3 + g)
                x = k.x[:, 2 * g:2 * g + 2, :].rearrange("p t d -> p (t d)")
                e.tensor_tensor(x, x, OB[g][:, :], ALU.add).then_inc(s_a, 1)

            def body(x, r, j):
                for g in range(4):
                    e.wait_ge(s_o, x * 4 + (g + 2))
                    e.wait_ge(s_a, x * 4 + (g + 1))
                    for u in range(2):
                        t = 2 * g + u
                        i = e.scalar_tensor_tensor(k.x[:, t, :], OB[g][:, u * D:(u + 1) * D],
                                                   comb[:, t, :][:, bass.ds(x, 1)], k.x[:, t, :], ALU.mult, ALU.add)
                    i.then_inc(s_a, 1)

            per_expert(e, body)


def perceiver(nc, t, out):
    with ExitStack() as ctx:
        sb, ps, sem = tools(nc, ctx)
        k = Names()
        k.ctx, k.ctxT = t["ctx"], t["ctxT"]
        k.x = sb("x", [P, TILES, D])
        k.xn = sb("xn", [P, TILES, D])
        k.xT = sb("xT", [P, KD, TOK])
        k.ident = sb("ident", [P, P])
        k.cols = sb("cols", [P, NCOLS])
        k.rows = sb("rows", [P, NROWS, D])
        k.bc_dram = nc.dram_tensor("bc_rows", (2 * DS, TOK), F32, kind="Internal").ap()
        k.trig = sb("trig", [P, 2, DH])
        k.own_head = sb("own_head", [P, HG])
        k.causal = sb("causal", [P, L])
        k.ident_bf = sb("ident_bf", [P, P], BF16)
        k.causal_bf = sb("causal_bf", [P, HG * L], BF16)
        k.same_batch = sb("same_batch", [P, P])
        k.diag64 = sb("diag64", [P, L])
        k.iota8 = sb("iota8", [P, E])
        k.wtq = sb("wtq", [P, KD, 2])
        k.wfq = sb("wfq", [2, D])
        k.btq = sb("btq", [P, 2])
        k.wg = sb("wg", [P, KD, E])
        k.gateb = sb("gateb", [P, E])
        k.b2 = sb("b2", [E, D])
        k.s_w5, k.s_w6 = sem("s_w5"), sem("s_w6")
        k.n_w5 = 16 * 7
        k.n_w6 = 16 * 3
        k.s_w3, k.s_w4 = sem("s_w3"), sem("s_w4")
        k.n_w3 = 32
        k.n_w4 = 16 * (5 + KD)
        k.s_w2 = sem("s_w2")
        k.n_w2 = 80 + 1
        k.s_x, k.s_rows, k.s_const, k.s_w0, s_out = (sem(n) for n in ("s_x", "s_rows", "s_const", "s_w0", "s_out"))
        k.n_ident = k.n_const = 8 + 3 + 3 + E
        k.n_w0 = 64

        ctx1 = ctx.enter_context(ExitStack())
        sb1, _, _ = tools(nc, ctx1)
        k.wq0, k.wk0T, k.wv0 = (sb1(n, [P, KD, D]) for n in ("wq0", "wk0T", "wv0"))
        k.cT = [sb1(f"cT{r}", [P, 2, KD, LK]) for r in range(2)]
        k.cN = [sb1(f"cN{r}", [FULL + 1, 2, ROWS, D]) for r in range(2)]
        k.s_dT = [sem(f"a_dT{r}") for r in range(2)]
        k.s_dN = [sem(f"a_dN{r}") for r in range(2)]
        with nc.Block() as block:
            @block.sync
            def _(e):
                e.dma_start(k.x[:, :, :], t["x"].rearrange("b l d -> (b l) d").rearrange("(t p) d -> p t d", p=P)
                            ).then_inc(k.s_x, 16)
                e.dma_start(k.cols[:, :], t["cols"]).then_inc(k.s_w0, 16)
                for n, w in (("wq0", k.wq0), ("wk0T", k.wk0T), ("wv0", k.wv0)):
                    e.dma_start(w[:, :, :], t[n].rearrange("(c p) n -> p c n", p=P)).then_inc(k.s_w0, 16)
                e.dma_start(k.rows[:, :, :].rearrange("p r d -> p (r d)"),
                            t["rows"].rearrange("r d -> (r d)").unsqueeze(0).to_broadcast([P, NROWS * D])
                            ).then_inc(k.s_rows, 16)
                load_columns(e, k, 0, 0)
                load_rows(e, k, 0, 0)
                load_columns(e, k, 1, 1)
                load_rows(e, k, 1, 1)
                e.dma_start(k.trig[:, :, :], t["trig"]).then_inc(k.s_w4, 16)
                e.dma_start(k.wtq[:, :, :], t["wtq"].rearrange("(c p) n -> p c n", p=P)).then_inc(k.s_w5, 16)
                e.dma_start(k.wfq[:, :], t["wfq"]).then_inc(k.s_w5, 16)
                e.dma_start(k.btq[:, :], t["btq"].unsqueeze(0).to_broadcast([P, 2])).then_inc(k.s_w5, 16)
                e.dma_start(k.wg[:, :, :], t["wg"].rearrange("(c p) n -> p c n", p=P)).then_inc(k.s_w6, 16)
                e.dma_start(k.gateb[:, :], t["gateb"].unsqueeze(0).to_broadcast([P, E])).then_inc(k.s_w6, 16)
                e.dma_start(k.b2[:, :], t["b2"]).then_inc(k.s_w6, 16)

            @block.vector
            def _(e):
                e.wait_ge(k.s_const, k.n_const)
                e.tensor_copy(k.ident_bf[:, :], k.ident[:, :])
                e.tensor_scalar(k.causal_bf[:, :].rearrange("p (h n) -> p h n", n=L),
                                k.causal[:, :].unsqueeze(1).to_broadcast([P, HG, L]), -NEG, NEG,
                                ALU.mult, ALU.add)

            @block.gpsimd
            def _(e):
                n = 0

                def chain(ins):
                    nonlocal n
                    n += 1
                    ins.then_inc(k.s_const, 1)
                    e.wait_ge(k.s_const, n)

                def keep(m, op, fill, base, pattern, mult):
                    chain(e.affine_select(out=m, in_=m, compare_op=op, fill=fill, base=base,
                                          pattern=pattern, channel_multiplier=mult))

                chain(e.memset(k.ident[:, :], 0.0))
                keep(k.ident[:, :], ALU.not_equal, 1.0, 0, [[-1, P]], 1)
                chain(e.memset(k.causal[:, :], 1.0))
                for b in range(2):
                    keep(k.causal[64 * b:64 * b + 64, :], ALU.is_ge, 0.0, 0, [[-1, L]], 1)
                chain(e.memset(k.own_head[:, :], 1.0))
                keep(k.own_head[:, :], ALU.is_ge, 0.0, 0, [[-DH, HG]], 1)
                keep(k.own_head[:, :], ALU.is_ge, 0.0, DH - 1, [[DH, HG]], -1)
                chain(e.memset(k.diag64[:, :], 0.0))
                for b in range(2):
                    keep(k.diag64[64 * b:64 * b + 64, :], ALU.not_equal, 1.0, 0, [[-1, L]], 1)
                chain(e.memset(k.same_batch[:, :], 0.0))
                for b in range(2):
                    chain(e.memset(k.same_batch[64 * b:64 * b + 64, 64 * b:64 * b + 64], 1.0))
                for i in range(E):
                    chain(e.memset(k.iota8[:, i:i + 1], float(i)))

        layer_norm(nc, k, "ln0")
        cross_attention(nc, k)
        ctx1.close()
        ctx4, ctx3, ctx2 = (ctx.enter_context(ExitStack()) for _ in range(3))
        sb4, sb3, sb2 = (tools(nc, c)[0] for c in (ctx4, ctx3, ctx2))
        k.w5 = [sb4(f"w5{i}", [P, KD, D]) for i in range(4)]
        k.w4 = [sb4(f"w4{i}", [P, KD, D]) for i in range(4)]
        k.c0T = sb4("c0T", [P, KD, TOK])
        k.w_fc = sb3("w_fc", [P, KD, FF])
        k.w_pr = sb3("w_pr", [P, FM, D])
        k.w_in = sb2("w_in", [P, KD, 2 * DI])
        k.w_xp = sb2("w_xp", [P, CH, 64])
        k.w_dt = sb2("w_dt", [DTR, DI])
        k.w_out = sb2("w_out", [P, CH, D])

        def late_weights(block):
            @block.gpsimd
            def _(e):
                e.memset(k.w_xp[:, :, DTR:32], 0.0).then_inc(k.s_w2, 1)

            @block.sync
            def _(e):
                e.dma_start(k.w_in[:, :, :], t["w_in"].rearrange("(c p) n -> p c n", p=P)).then_inc(k.s_w2, 16)
                e.dma_start(k.w_xp[:, :, 0:DTR], t["w_xp"][:, 0:DTR].rearrange("(c p) n -> p c n", p=P)
                            ).then_inc(k.s_w2, 16)
                e.dma_start(k.w_xp[:, :, 32:64], t["w_xp"][:, DTR:DTR + 2 * DS].rearrange("(c p) n -> p c n", p=P)
                            ).then_inc(k.s_w2, 16)
                e.dma_start(k.w_dt[:, :], t["w_dt"]).then_inc(k.s_w2, 16)
                e.dma_start(k.w_out[:, :, :], t["w_out"].rearrange("(c p) n -> p c n", p=P)).then_inc(k.s_w2, 16)
                e.dma_start(k.w_fc[:, :, :], t["w_fc"].rearrange("(c p) n -> p c n", p=P)).then_inc(k.s_w3, 16)
                e.dma_start(k.w_pr[:, :, :], t["w_pr"].rearrange("(c p) n -> p c n", p=P)).then_inc(k.s_w3, 16)
                for i in range(4):
                    e.dma_start(k.w4[i][:, :, :], t[f"w4{i}"].rearrange("(c p) n -> p c n", p=P)).then_inc(k.s_w4, 16)
                for i in range(4):
                    e.dma_start(k.w5[i][:, :, :], t[f"w5{i}"].rearrange("(c p) n -> p c n", p=P)).then_inc(k.s_w5, 16)
                for c in range(KD):
                    e.dma_start(k.c0T[:, c, :].rearrange("p (b n) -> p b n", n=L),
                                t["ctxT"][:, c * P:(c + 1) * P, 0:L].rearrange("b p n -> p b n")).then_inc(k.s_w4, 16)

        layer_norm(nc, k, "ln1", late_weights)
        with ExitStack() as mctx:
            sb, _, _ = tools(nc, mctx)
            m = Names()
            m.bc_dram = k.bc_dram
            m.u, m.sres, m.delta, m.du = (sb(n, [P, CH, TOK]) for n in ("u", "sres", "delta", "du"))
            m.diagD = sb("diagD", [P, CH, P])
            m.negA = sb("negA", [P, CH, DS])
            mamba_front(nc, k, m)
            mamba_scan(nc, k, m)
        ctx2.close()
        layer_norm(nc, k, "ln2")
        spiking_ffn(nc, k)
        ctx3.close()
        layer_norm(nc, k, "ln3")
        windowed_attention(nc, k)
        layer_norm(nc, k, "ln4")
        phase_attention(nc, k)
        ctx4.close()
        layer_norm(nc, k, "ln5")
        experts(nc, k, t["w1"], t["w2"])

        with nc.Block() as block:
            @block.sync
            def _(e):
                e.dma_start(out.rearrange("b l d -> (b l) d").rearrange("(t p) d -> p t d", p=P), k.x[:, :, :]
                            ).then_inc(s_out, 16)
                e.wait_ge(s_out, 16)




def rotary():
    half = DH // 2
    inv = (1.0 / 10000.0 ** (np.arange(half, dtype=np.float32) / half)).astype(np.float32)
    ang = np.arange(L, dtype=np.float32)[:, None] * inv[None, :]
    cos, sin = np.cos(ang), np.sin(ang)
    table = np.stack([np.concatenate([cos, cos], 1), np.concatenate([-sin, sin], 1)], 1)
    return np.concatenate([table, table], 0).astype(np.float32)


def layout(inputs):
    a = {n: np.asarray(v) for n, v in inputs.items()}
    T = np.transpose
    cols = [T(a["L0_xattn_bq"].reshape(2, P)), T(a["L0_xattn_bk"].reshape(2, P)),
            T(a["L0_attn_in_proj_b"].reshape(8, P)),
            T(a["L0_attn_conv_w"].reshape(4, P, 4), (1, 0, 2)).reshape(P, 16),
            T(a["L0_attn_conv_b"].reshape(4, P)), T(a["L0_attn_dt_proj_b"].reshape(4, P)),
            T(a["L0_attn_D_param"].reshape(4, P)),
            T(a["L0_attn_A_log"].reshape(4, P, 16), (1, 0, 2)).reshape(P, 64),
            T(a["L1_attn_bq"].reshape(2, P)), T(a["L1_attn_bk"].reshape(2, P)),
            T(a["L1_ffn_b1"].reshape(16, P))]
    rows = [a[n] for n in ("L0_xattn_bv", "L0_attn_out_proj_b", "L1_xattn_bq", "L1_xattn_bk", "L1_xattn_bv",
                           "L1_xattn_bo", "L1_attn_bv", "L1_attn_bo", "L1_attn_bfq")]
    return {
        "x": a["x"], "ctx": a["ctx_1024"], "ctxT": T(a["ctx_1024"], (0, 2, 1)),
        "cols": np.concatenate(cols, axis=1), "rows": np.stack(rows),
        "w_in": T(a["L0_attn_in_proj_w"]), "w_xp": T(a["L0_attn_x_proj_w"]),
        "w_dt": T(a["L0_attn_dt_proj_w"]), "w_out": T(a["L0_attn_out_proj_w"]),
        "w_fc": T(a["L0_ffn_W_fc"]), "w_pr": T(a["L0_ffn_W_proj"]),
        **{f"w4{i}": T(a[f"L1_xattn_W{c}"]) for i, c in enumerate("qkvo")}, "trig": rotary(),
        **{f"w5{i}": T(a[f"L1_attn_W{c}"]) for i, c in enumerate("qkvo")},
        "wtq": T(a["L1_attn_Wtq"]), "wfq": T(a["L1_attn_Wfq"]), "btq": a["L1_attn_btq"],
        "wg": a["L1_ffn_gate_w"], "gateb": a["L1_ffn_gate_b"], "b2": a["L1_ffn_b2"],
        "w1": a["L1_ffn_w1"], "w2": a["L1_ffn_w2"],
        "wq0": a["L0_xattn_Wq"], "wk0T": T(a["L0_xattn_Wk"]), "wv0": a["L0_xattn_Wv"],
    }


def kernel(**inputs):
    import concourse.bacc as _bacc
    from concourse.bass_utils import run_bass_kernel_spmd as _run

    nc = _bacc.Bacc("TRN2", target_bir_lowering=False, num_devices=1)
    arrays, args = {}, {}
    for name, v in layout(inputs).items():
        v = np.ascontiguousarray(v)
        arrays[f"in_{name}"] = v
        args[name] = nc.dram_tensor(f"in_{name}", v.shape, mybir.dt.from_np(v.dtype), kind="ExternalInput").ap()
    out = nc.dram_tensor("out_dram", (B, L, D), F32, kind="ExternalOutput").ap()
    perceiver(nc, args, out)
    r = _run(nc, [arrays], core_ids=[0])
    return r.results[0]["out_dram"]
```

```python
from contextlib import ExitStack

import numpy as np
import concourse.bass as bass
from concourse import mybir

F32 = mybir.dt.float32
F32R = mybir.dt.float32r
BF16 = mybir.dt.bfloat16
U32 = mybir.dt.uint32
ALU = mybir.AluOpType
ACT = mybir.ActivationFunctionType
AX = mybir.AxisListType

P = 128
B, L, D = 16, 64, 256
LK = 1601
TOK = B * L
TILES = TOK // P
KD = D // P
HALF = 512
EPS = 1e-5
NEG = -3.0e38

ROWS = 13
FULL = LK // ROWS
LAST = LK - FULL * ROWS
SC_W = [min(HALF, LK - c * HALF) for c in range(4)]

DI, DS, DTR, KC = 512, 16, 16, 4
CH = DI // P
FF = 1024
FM = FF // P
H, DH = 16, 16
HG = P // DH
DV = DH + 1
E, TOPK = 8, 2

COLS = {}
_n = 0
for _name, _w in (("bq0", 2), ("bk0", 2), ("inb", 8), ("convw", 16), ("convb", 4), ("dtb", 4),
                  ("dpar", 4), ("alog", 64), ("bq5", 2), ("bk5", 2), ("b1", 16)):
    COLS[_name] = (_n, _w)
    _n += _w
NCOLS = _n
ROWV = {n: i for i, n in enumerate(("bv0", "outb", "bq4", "bk4", "bv4", "bo4", "bv5", "bo5", "bfq"))}
NROWS = len(ROWV)


class Names:
    pass


def tools(nc, ctx):
    def sb(name, shape, dt=F32):
        return ctx.enter_context(nc.sbuf_tensor(name, shape, dt))

    def ps(name, shape=(P, HALF), dt=F32):
        return ctx.enter_context(nc.psum_tensor(name, list(shape), dt))

    def sem(name):
        return ctx.enter_context(nc.semaphore(name))

    return sb, ps, sem


def col(k, name, i=0):
    a, _ = COLS[name]
    return k.cols[:, a + i:a + i + 1]


def rowvec(k, name):
    return k.rows[:, ROWV[name], :]


def layer_norm(nc, k, tag, loads=None, split=None):
    with ExitStack() as ctx:
        sb, ps, sem = tools(nc, ctx)
        mv = sb(f"{tag}_mv", [P, TILES, 2])
        veps = sb(f"{tag}_veps", [P, TILES])
        sd = sb(f"{tag}_sd", [P, TILES])
        rstd = sb(f"{tag}_rstd", [P, TILES])
        tp = [ps(f"{tag}_tp{i}") for i in range(4)]
        s_dve = sem(f"{tag}_dve")
        s_sd = sem(f"{tag}_sd_ready")
        s_xn = sem(f"{tag}_xn")
        s_tp = sem(f"{tag}_tp_done")
        s_ev = sem(f"{tag}_ev")
        block = ctx.enter_context(nc.Block())
        if loads:
            loads(block)

        @block.vector
        def _(e):
            if tag == "ln0":
                e.wait_ge(k.s_x, 16)
            if tag == "ln0":
                for t in range(TILES):
                    i = e.bn_stats(k.stats[:, t, :], k.x[:, t, :])
                i.then_inc(s_dve, 1)
                e.wait_ge(s_dve, 1)
            base = 1 if tag == "ln0" else 0
            for t in range(TILES):
                i = e.bn_aggr(mv[:, t, :], k.stats[:, t, :])
            i.then_inc(s_dve, 1)
            e.wait_ge(s_dve, base + 1)
            e.tensor_scalar(veps[:, :], mv[:, :, 1], EPS, None, ALU.add).then_inc(s_dve, 1)
            e.wait_ge(s_sd, 1)
            e.reciprocal(rstd[:, :], sd[:, :]).then_inc(s_dve, 1)
            e.wait_ge(s_dve, base + 3)
            for t in range(TILES):
                e.tensor_scalar(k.xn[:, t, :], k.x[:, t, :], mv[:, t, 0:1], rstd[:, t:t + 1],
                                ALU.subtract, ALU.mult).then_inc(s_xn, 1)
            if split:
                for t in range(TILES):
                    tok = slice(t * P, (t + 1) * P)
                    e.wait_ge(s_ev, t + 1)
                    e.tensor_tensor(split[1][:, :, tok], k.xT[:, :, tok], split[0][:, :, tok].bitcast(F32),
                                    ALU.subtract)

        @block.scalar
        def _(e):
            e.wait_ge(s_dve, 3 if tag == "ln0" else 2)
            e.activation(sd[:, :], veps[:, :], ACT.Sqrt).then_inc(s_sd, 1)
            for t in range(TILES):
                e.wait_ge(s_tp, t + 1)
                if split:
                    e.activation(split[0][:, :, t * P:(t + 1) * P],
                                 tp[t % 4][:, 0:D].rearrange("p (c n) -> p c n", c=KD), ACT.Copy)
                e.activation(k.xT[:, :, t * P:(t + 1) * P],
                             tp[t % 4][:, 0:D].rearrange("p (c n) -> p c n", c=KD), ACT.Copy
                             ).then_inc(s_ev, 1)

        @block.tensor
        def _(e):
            if tag == "ln0":
                e.wait_ge(k.s_const, k.n_ident)
            for t in range(TILES):
                e.wait_ge(s_xn, t + 1)
                if t >= 4:
                    e.wait_ge(s_ev, t - 3)
                for c in range(KD):
                    i = e.transpose(tp[t % 4][:, c * P:(c + 1) * P], k.xn[:, t, c * P:(c + 1) * P],
                                    k.ident[:, :])
                i.then_inc(s_tp, 1)


def tile_stats(e, k, t):
    pick = (lambda a: a[:, t, :]) if isinstance(t, int) else (lambda a: a[:, bass.ds(t, 1), :].squeeze(1))
    return e.bn_stats(pick(k.stats), pick(k.x))


def load_columns(e, k, i, r):
    src = k.ctxT[2 * i:2 * i + 2] if isinstance(i, int) else k.ctxT[bass.ds(i * 2, 2), :, :]
    e.dma_start(k.cT[r][:, :, :, :], src.rearrange("b (c p) n -> p b c n", p=P)).then_inc(k.s_dT[r], 16)


def load_rows(e, k, i, r):
    src = k.ctx[2 * i:2 * i + 2] if isinstance(i, int) else k.ctx[bass.ds(i * 2, 2), :, :]
    e.dma_start(k.cN[r][0:FULL, :, :, :],
                src[:, 0:FULL * ROWS, :].rearrange("b (p c) d -> p b c d", c=ROWS)).then_inc(k.s_dN[r], 16)
    e.dma_start(k.cN[r][FULL:FULL + 1, :, 0:LAST, :],
                src[:, FULL * ROWS:LK, :].rearrange("b (p c) d -> p b c d", p=1)).then_inc(k.s_dN[r], 16)


def cross_attention(nc, k):
    scale = 1.0 / float(D) ** 0.5
    with ExitStack() as ctx:
        sb, ps, sem = tools(nc, ctx)
        qT = sb("qT", [P, KD, TOK])
        qkT = sb("qkT", [P, KD, TOK + P])
        qbk = sb("qbk", [P, TILES])
        qs = [sb(f"qs{r}", [P, KD, P]) for r in range(2)]
        cT, cN, s_dT, s_dN = k.cT, k.cN, k.s_dT, k.s_dN
        prob = [sb(f"prob{r}", [P, LK]) for r in range(2)]
        pT = sb("pT", [P, ROWS, P])
        mx = sb("mx", [P, 1])
        full_max = sb("full_max", [P, 1])
        nbias = sb("nbias", [P, 1])
        total = [sb(f"total{r}", [P, 1]) for r in range(2)]
        rinv = sb("rinv", [P, 1])
        on = [sb(f"on{r}", [P, D]) for r in range(2)]
        onT = sb("onT", [P, KD, P])
        S = ps("S", [P, 4 * HALF])
        tps = [ps(f"ptp{i}") for i in range(2)]
        O = ps("O")
        X = ps("X")
        s_pp = sem("a_pp")
        s_pe = sem("a_pe")
        s_qb = sem("a_qb")
        s_q0 = sem("a_q0")
        s_qs = sem("a_qs")
        s_sc = sem("a_sc")
        s_m1 = sem("a_m1")
        s_mx = sem("a_mx")
        s_ex = sem("a_ex")
        s_tp = sem("a_tp")
        s_te = sem("a_te")
        s_pv = sem("a_pv")
        s_ri = sem("a_ri")
        s_on = sem("a_on")
        s_ot = sem("a_ot")
        s_oe = sem("a_oe")
        s_wv = sem("a_wv")
        s_xa = sem("a_xa")
        block = ctx.enter_context(nc.Block())
        groups = [range(0, 4), range(4, 8), range(8, 12), range(12, 13)]

        def pipeline(e, sub):
            for i in range(2):
                sub(i, i % 2, lambda d, i=i: i - d >= 0)
            with e.Fori(1, TILES // 2) as j:
                sub(j * 2, 0, lambda d: True)
                sub(j * 2 + 1, 1, lambda d: True)
            for i in range(TILES, TILES + 2):
                sub(i, i % 2, lambda d, i=i: i - d < TILES)

        @block.sync
        def _(e):
            e.wait_ge(s_sc, 1)
            load_columns(e, k, 2, 0)
            e.wait_ge(s_sc, 2)
            load_columns(e, k, 3, 1)
            e.wait_ge(s_pv, 1)
            load_rows(e, k, 2, 0)
            with e.Fori(2, TILES // 2) as j:
                for r in range(2):
                    e.wait_ge(s_sc, j * 2 + (r - 1))
                    load_columns(e, k, j * 2 + r, r)
                    e.wait_ge(s_pv, j * 2 + (r - 2))
                    load_rows(e, k, j * 2 + (r - 1), 1 - r)
            e.wait_ge(s_pv, TILES - 2)
            load_rows(e, k, TILES - 1, 1)

        @block.tensor
        def _(e):
            e.wait_ge(k.s_w0, k.n_w0)
            n = 0
            for w, src in ((k.wq0, k.xT), (k.wk0T, qT)):
                for m in range(KD):
                    for h in range(2):
                        if n >= 2:
                            e.wait_ge(s_pe, n - 1 if n != 4 else 4)
                        for c in range(KD):
                            i = e.matmul(tps[n % 2][:, :], w[:, c, m * P:(m + 1) * P],
                                         src[:, c, h * HALF:(h + 1) * HALF], start=c == 0, stop=c == 1)
                        i.then_inc(s_pp, 1)
                        n += 1
            for t in range(TILES):
                for c in range(KD):
                    i = e.matmul(X[:, t:t + 1], qT[:, c, t * P:(t + 1) * P], col(k, "bk0", c),
                                 start=c == 0, stop=c == 1)
            i.then_inc(s_qb, 1)
            e.wait_ge(s_q0, 1)
            e.wait_ge(s_pe, 8)

            def turn(i, q, g):
                if g >= 2:
                    e.wait_ge(s_te, (i - 1) * 4 + g - 1)
                for c in groups[g]:
                    kc = FULL + (c < LAST)
                    j = e.transpose(tps[g % 2][0:kc, (c % 4) * P:(c % 4 + 1) * P],
                                    prob[q][:, c:c + (kc - 1) * ROWS + 1:ROWS], k.ident[:, :])
                j.then_inc(s_tp, 1)

            def sub(i, r, live):
                if live(1):
                    e.wait_ge(s_ex, i)
                    for g in range(2):
                        turn(i, 1 - r, g)
                if live(2):
                    e.wait_ge(s_on, i - 1)
                    for c in range(KD):
                        j = e.transpose(X[:, c * P:(c + 1) * P], on[r][:, c * P:(c + 1) * P], k.ident[:, :])
                    j.then_inc(s_ot, 1)
                if live(0):
                    e.wait_ge(s_qs, i + 1)
                    e.wait_ge(s_dT[r], 16 * (i // 2 + 1) if isinstance(i, int) else (i - r) * 8 + 16)
                    e.wait_ge(s_ex, i)
                    for c, w in enumerate(SC_W):
                        for kt in range(KD):
                            for b in range(2):
                                j = e.matmul(S[64 * b:64 * b + 64, c * HALF:c * HALF + w],
                                             qs[r][:, kt, 64 * b:64 * b + 64],
                                             cT[r][:, b, kt, c * HALF:c * HALF + w],
                                             start=kt == 0, stop=kt == 1)
                    j.then_inc(s_sc, 1)
                if live(2):
                    e.wait_ge(s_oe, i - 1)
                    for c in range(KD):
                        j = e.matmul(X[:, D:2 * D], onT[:, c, :], k.wv0[:, c, :], start=c == 0, stop=c == 1)
                    j.then_inc(s_wv, 1)
                if live(1):
                    q = 1 - r
                    e.wait_ge(s_dN[q], 32 * ((i - 1) // 2 + 1) if isinstance(i, int) else (i - 1 - q) * 16 + 32)

                    def pv(g):
                        e.wait_ge(s_te, (i - 1) * 4 + g + 1)
                        if g == 0:
                            e.wait_ge(s_on, i - 1)
                        for c in groups[g]:
                            kc = FULL + (c < LAST)
                            for b in range(2):
                                j = e.matmul(O[64 * b:64 * b + 64, 0:D], pT[0:kc, c, 64 * b:64 * b + 64],
                                             cN[q][0:kc, b, c, :], start=c == 0, stop=c == ROWS - 1)
                        return j

                    for g in range(2):
                        pv(g)
                        turn(i, q, g + 2)
                    pv(2)
                    pv(3).then_inc(s_pv, 1)

            pipeline(e, sub)

        @block.scalar
        def _(e):
            n = 0
            for b in ("bq0", None):
                for m in range(KD):
                    for h in range(2):
                        e.wait_ge(s_pp, n + 1)
                        dst = (qT if b else qkT)[:, m, h * HALF:(h + 1) * HALF]
                        if b:
                            e.activation(dst, tps[n % 2][:, :], ACT.Identity, bias=col(k, b, m)).then_inc(s_pe, 1)
                        else:
                            e.activation(dst, tps[n % 2][:, :], ACT.Copy).then_inc(s_pe, 1)
                        n += 1

            def sub(i, r, live):
                if live(2):
                    e.wait_ge(s_ot, i - 1)
                    if not isinstance(i, int) or i > 2:
                        e.wait_ge(s_wv, i - 2)
                    e.activation(onT[:, :, :], X[:, 0:D].rearrange("p (c n) -> p c n", c=KD), ACT.Copy
                                 ).then_inc(s_oe, 1)
                if live(0):
                    if not isinstance(i, int) or i >= 2:
                        e.wait_ge(s_tp, (i - 1) * 4)
                    e.wait_ge(s_mx, i + 1)
                    e.activation(prob[r][:, :], S[:, 0:LK], ACT.Exp, bias=nbias[:, :], scale=scale,
                                 accum_out=total[r][:, :]).then_inc(s_ex, 1)

            pipeline(e, sub)

        @block.vector
        def _(e):
            e.wait_ge(k.s_rows, 16)
            e.tensor_tensor(k.x[:, :, :], k.x[:, :, :],
                            rowvec(k, "bv0").unsqueeze(1).to_broadcast([P, TILES, D]), ALU.add)
            e.memset(qkT[:, :, TOK:TOK + P], 0.0)
            e.wait_ge(s_qb, 1)
            e.tensor_scalar(qbk[:, :], X[:, 0:TILES], scale, None, ALU.mult).then_inc(s_q0, 1)
            e.wait_ge(s_pe, 8)

            def queries(i, r):
                src = qkT[:, :, i * P:(i + 1) * P] if isinstance(i, int) else qkT[:, :, bass.ds(i * P, P)]
                e.tensor_copy(qs[r][:, :, :], src).then_inc(s_qs, 1)

            queries(0, 0)
            e.wait_ge(s_q0, 1)

            def evacuate(i, g):
                e.wait_ge(s_tp, (i - 1) * 4 + g + 1)
                if g == 0:
                    e.wait_ge(s_pv, i - 1)
                n, c0 = len(groups[g]), groups[g][0]
                if c0 < LAST:
                    e.tensor_copy(pT[0:FULL + 1, 0:LAST, :],
                                  tps[0][0:FULL + 1, 0:LAST * P].rearrange("p (c n) -> p c n", n=P))
                    e.tensor_copy(pT[0:FULL, LAST:4, :],
                                  tps[0][0:FULL, LAST * P:4 * P].rearrange("p (c n) -> p c n", n=P)
                                  ).then_inc(s_te, 1)
                else:
                    e.tensor_copy(pT[0:FULL, c0:c0 + n, :],
                                  tps[g % 2][0:FULL, 0:n * P].rearrange("p (c n) -> p c n", n=P)
                                  ).then_inc(s_te, 1)

            def sub(i, r, live):
                if live(1):
                    for g in range(2):
                        evacuate(i, g)
                one = (lambda a, n: a[:, n:n + 1] if isinstance(n, int) else a[:, bass.ds(n, 1)])
                if live(0):
                    e.wait_ge(s_sc, i + 1)
                    e.reduce_max(mx[:, :], S[:, 0:LK], AX.X).then_inc(s_m1, 1)
                    e.wait_ge(s_m1, i * 2 + 1)
                    e.tensor_scalar(full_max[:, :], mx[:, :], scale, one(qbk, i), ALU.mult, ALU.add
                                    ).then_inc(s_m1, 1)
                    e.wait_ge(s_m1, i * 2 + 2)
                    e.wait_ge(s_ex, i)
                    e.tensor_scalar(nbias[:, :], full_max[:, :], -1.0, one(qbk, i), ALU.mult, ALU.add
                                    ).then_inc(s_mx, 1)
                    queries(i + 1, 1 - r)
                if live(2):
                    e.wait_ge(s_wv, i - 1)
                    dst = k.x[:, i - 2, :] if isinstance(i, int) else k.x[:, bass.ds(i - 2, 1), :].squeeze(1)
                    e.tensor_tensor(dst, dst, X[:, D:2 * D], ALU.add).then_inc(s_xa, 1)
                if live(1):
                    q = 1 - r
                    for g in (2, 3):
                        evacuate(i, g)
                if live(2):
                    e.wait_ge(s_xa, i - 1)
                    tile_stats(e, k, i - 2)
                if live(1):
                    e.reciprocal(rinv[:, :], total[q][:, :]).then_inc(s_ri, 1)
                    e.wait_ge(s_ri, i)
                    e.wait_ge(s_pv, i)
                    e.tensor_scalar(on[q][:, :], O[:, 0:D], rinv[:, :], None, ALU.mult).then_inc(s_on, 1)

            pipeline(e, sub)


def mamba_front(nc, k, m):
    with ExitStack() as ctx:
        sb, ps, sem = tools(nc, ctx)
        BH = HALF // L
        xpad = [sb(f"xpad{r}", [P, BH, L + KC - 1]) for r in range(2)]
        acc = [sb(f"acc{r}", [P, BH, L]) for r in range(2)]
        expA = sb("expA", [P, CH * DS])
        dtr = sb("dtr", [DTR, TOK])
        bc = sb("bc", [64, TOK])
        zp = [ps(f"zp{i}") for i in range(4)]
        xq = [ps(f"xq{i}") for i in range(2)]
        dq = [ps(f"dq{i}") for i in range(2)]
        s_in = sem("m_in")
        s_xp = sem("m_xp")
        s_pad = sem("m_pad")
        s_cv = sem("m_cv")
        s_u = sem("m_u")
        s_rs = sem("m_rs")
        s_xj = sem("m_xj")
        s_xe = sem("m_xe")
        s_dt = sem("m_dt")
        s_az = sem("m_az")
        s_ez = sem("m_ez")
        s_lz = sem("m_lz")
        s_rz = sem("m_rz")
        s_dl = sem("m_dl")
        s_bc = sem("m_bc")
        s_a = sem("m_a")
        block = ctx.enter_context(nc.Block())
        xblocks = [(c, h) for h in range(2) for c in range(CH)]

        @block.tensor
        def _(e):
            e.wait_ge(k.s_w2, k.n_w2)
            def project(n):
                if n >= 4:
                    e.wait_ge(s_xp, min(n - 3, 8))
                    if n - 3 > 8:
                        e.wait_ge(s_rs, n - 3 - 8)
                c, h = xblocks[n % 8]
                for kt in range(KD):
                    i = e.matmul(zp[n % 4][:, :], k.w_in[:, kt, (n // 8 * CH + c) * P:(n // 8 * CH + c + 1) * P],
                                 k.xT[:, kt, h * HALF:(h + 1) * HALF], start=kt == 0, stop=kt == 1)
                i.then_inc(s_in, 1)

            for n in range(12):
                project(n)
            for h in range(2):
                e.wait_ge(s_u, CH * (h + 1))
                for c in range(CH):
                    i = e.matmul(xq[h][0:64, :], k.w_xp[:, c, :], m.u[:, c, h * HALF:(h + 1) * HALF],
                                 start=c == 0, stop=c == CH - 1)
                i.then_inc(s_xj, 1)
                e.wait_ge(s_xe, h + 1)
                for n in range(CH * h, CH * (h + 1)):
                    c = n % CH
                    if n >= 2:
                        e.wait_ge(s_az, n - 1)
                        e.wait_ge(s_rz, n - 1)
                    e.matmul(dq[n % 2][:, :], k.w_dt[:, c * P:(c + 1) * P], dtr[:, h * HALF:(h + 1) * HALF],
                             start=True, stop=True).then_inc(s_dt, 1)
            for n in range(12, 16):
                project(n)

        @block.scalar
        def _(e):
            def gate(n):
                c, h = xblocks[n]
                e.wait_ge(s_in, 8 + n + 1)
                e.activation(m.sres[:, c, h * HALF:(h + 1) * HALF], zp[n % 4][:, :], ACT.Silu,
                             bias=col(k, "inb", CH + c)).then_inc(s_rs, 1)

            def silu_u(n):
                c, h = xblocks[n]
                e.wait_ge(s_cv, 4 * n + 4)
                e.activation(m.u[:, c, h * HALF:(h + 1) * HALF].rearrange("p (b l) -> p b l", l=L),
                             acc[n % 2][:, :, :], ACT.Silu).then_inc(s_u, 1)

            e.wait_ge(s_pad, 1)
            for n, (c, h) in enumerate(xblocks):
                e.wait_ge(s_in, n + 1)
                if n >= 2:
                    e.wait_ge(s_cv, 4 * (n - 2) + 4)
                e.activation(xpad[n % 2][:, :, KC - 1:], zp[n % 4][:, :].rearrange("p (b l) -> p b l", l=L),
                             ACT.Identity, bias=col(k, "inb", c)).then_inc(s_xp, 1)
                if n >= 1:
                    silu_u(n - 1)
            silu_u(7)
            for n in range(4):
                gate(n)
            for h in range(2):
                half = m.delta[:, :, h * HALF:(h + 1) * HALF]
                for n in range(CH * h, CH * (h + 1)):
                    e.wait_ge(s_dt, n + 1)
                    e.activation(half[:, n % CH, :], dq[n % 2][:, :], ACT.Abs, bias=col(k, "dtb", n % CH)
                                 ).then_inc(s_az, 1)
                e.wait_ge(s_az, CH * (h + 1))
                e.activation(half, half, ACT.Exp, scale=-1.0).then_inc(s_ez, 1)
                e.wait_ge(s_ez, h + 1)
                e.activation(half, half, ACT.Ln, bias=1.0).then_inc(s_lz, 1)
            for n in range(4, 8):
                gate(n)
            a0, aw = COLS["alog"]
            e.activation(expA[:, :], k.cols[:, a0:a0 + aw], ACT.Exp).then_inc(s_a, 1)
            e.wait_ge(s_a, 1)
            e.mul(m.negA[:, :, :].rearrange("p c n -> p (c n)"), expA[:, :], -1.0)

        @block.vector
        def _(e):
            for r in range(2):
                i = e.memset(xpad[r][:, :, 0:KC - 1], 0.0)
            i.then_inc(s_pad, 1)
            for n, (c, h) in enumerate(xblocks):
                r = n % 2
                e.wait_ge(s_xp, n + 1)
                if n >= 2:
                    e.wait_ge(s_u, n - 1)
                for j in range(KC):
                    tap = col(k, "convw", c * KC + j)
                    if j == 0:
                        e.tensor_scalar(acc[r][:, :, :], xpad[r][:, :, 0:L], tap, col(k, "convb", c),
                                        ALU.mult, ALU.add).then_inc(s_cv, 1)
                    else:
                        e.wait_ge(s_cv, 4 * n + j)
                        e.scalar_tensor_tensor(acc[r][:, :, :], xpad[r][:, :, j:j + L], tap, acc[r][:, :, :],
                                               ALU.mult, ALU.add).then_inc(s_cv, 1)
            for h in range(2):
                hs = slice(h * HALF, (h + 1) * HALF)
                e.wait_ge(s_xj, h + 1)
                e.tensor_copy(dtr[:, hs], xq[h][0:DTR, :])
                e.tensor_copy(bc[32:64, hs], xq[h][32:64, :]).then_inc(s_xe, 1)
                for n in range(CH * h, CH * (h + 1)):
                    e.wait_ge(s_dt, n + 1)
                    e.wait_ge(s_az, n + 1)
                    e.tensor_scalar(m.du[:, n % CH, hs], dq[n % 2][:, :], col(k, "dtb", n % CH), 0.0,
                                    ALU.add, ALU.max).then_inc(s_rz, 1)
            for h in range(2):
                hs = slice(h * HALF, (h + 1) * HALF)
                e.wait_ge(s_rz, CH * (h + 1))
                e.wait_ge(s_lz, h + 1)
                for c in range(CH):
                    e.tensor_tensor(m.delta[:, c, hs], m.delta[:, c, hs], m.du[:, c, hs], ALU.add
                                    ).then_inc(s_dl, 1)
            for c in range(CH):
                i = e.tensor_scalar(m.diagD[:, c, :], k.ident[:, :], col(k, "dpar", c), None, ALU.mult)
            e.tensor_tensor(k.x[:, :, :], k.x[:, :, :],
                            rowvec(k, "outb").unsqueeze(1).to_broadcast([P, TILES, D]), ALU.add)

        @block.gpsimd
        def _(e):
            for n, (c, h) in enumerate(xblocks):
                hs = slice(h * HALF, (h + 1) * HALF)
                e.wait_ge(s_dl, n + 1)
                e.tensor_tensor(m.du[:, c, hs], m.delta[:, c, hs], m.u[:, c, hs], ALU.mult)

        @block.sync
        def _(e):
            e.wait_ge(s_xe, 2)
            e.dma_start(m.bc_dram, bc[32:64, :]).then_inc(s_bc, 16)
            e.wait_ge(s_bc, 16)
            load_state(e, m, 0, m.Bb[0], 0, m.s_bl[0])
            for q in range(2):
                load_state(e, m, q, m.Cb[q], DS, m.s_cl[q])


def load_state(e, m, n, buf, row, s):
    src = m.bc_dram[row + n:row + n + 1, :] if isinstance(n, int) else m.bc_dram[bass.ds(n + row, 1), :]
    e.dma_start(buf, src.to_broadcast([P, TOK])).then_inc(s, 16)


def mamba_scan(nc, k, m):
    with ExitStack() as ctx:
        sb, ps, sem = tools(nc, ctx)
        ND = 4
        Bb, Cb, s_bl, s_cl = m.Bb, m.Cb, m.s_bl, m.s_cl
        A = [k.xn[:, 4 * i:4 * i + 4, :].rearrange("p t d -> p (t d)") for i in range(2)]
        dbu = [sb(f"dbu{i}", [P, TOK]) for i in range(ND)]
        hh = [sb(f"hh{i}", [P, TOK]) for i in range(ND)]
        Y = ps("Y", [P, CH, TOK])
        s_A = sem("n_A")
        s_bu = sem("n_bu")
        s_h = sem("n_h")
        s_hc = sem("n_hc")
        s_y = sem("n_y")
        s_yg = sem("n_yg")
        s_o = sem("n_o")
        s_xa = sem("n_xa")
        block = ctx.enter_context(nc.Block())
        STEPS = DS * CH

        def out(t, n):
            return Y[:, t // 4, (t % 4) * D:(t % 4 + n) * D]

        def steps(e, body):
            with e.Fori(0, DS // 2) as j:
                for q in range(2):
                    for c in range(CH):
                        body(j * 2 + q, q, c, j * (2 * CH) + (q * CH + c))

        @block.sync
        def _(e):
            load_state(e, m, 1, Bb[1], 0, s_bl[1])
            with e.Fori(1, DS // 2) as j:
                for q in range(2):
                    e.wait_ge(s_bu, j * (2 * CH) + (q - 1) * CH)
                    load_state(e, m, j * 2 + q, Bb[q], 0, s_bl[q])
                    e.wait_ge(s_hc, j * (2 * CH) + (q - 1) * CH)
                    load_state(e, m, j * 2 + q, Cb[q], DS, s_cl[q])

        @block.scalar
        def _(e):
            def body(n, q, c, s):
                by_batch = lambda a: a.rearrange("p (b l) -> p b l", l=L)[:, :, 1:L]
                e.wait_ge(s_h, s + 3)
                e.activation(by_batch(A[c % 2]), by_batch(m.delta[:, c, :]), ACT.Exp,
                             scale=m.negA[:, c, :][:, bass.ds(n, 1)]).then_inc(s_A, 1)

            steps(e, body)

        @block.gpsimd
        def _(e):
            def body(n, q, c, s):
                if c == 0:
                    e.wait_ge(s_bl[q], n * 8 + (16 - 8 * q))
                e.wait_ge(s_h, s + 1)
                e.tensor_tensor(dbu[c % ND][:, :], m.du[:, c, :], Bb[q], ALU.mult).then_inc(s_bu, 1)

            steps(e, body)

        @block.vector
        def _(e):
            for r in range(2):
                zero = A[r].rearrange("p (b l) -> p b l", l=L)[:, :, 0]
                for b in range(0, B, B // 2):
                    e.memset(zero[:, b:b + B // 2], 0.0).then_inc(s_h, 1)

            def emit_hc(n, q, c, s):
                if c == 0:
                    e.wait_ge(s_cl[q], n * 8 + (16 - 8 * q))
                e.wait_ge(s_h, s + 5)
                e.tensor_tensor(hh[c][:, :], hh[c][:, :], Cb[q], ALU.mult).then_inc(s_hc, 1)

            def body(n, q, c, s):
                e.wait_ge(s_A, s + 1)
                e.wait_ge(s_bu, s + 1)
                e.wait_ge(s_y, s + 1)
                e.tensor_tensor_scan(hh[c][:, :], A[c % 2], dbu[c][:, :], 0.0, ALU.mult, ALU.add
                                     ).then_inc(s_h, 1)
                if c:
                    emit_hc(n, q, c - 1, s - 1)
                if c == CH - 1:
                    emit_hc(n, q, c, s)

            steps(e, body)
            for c in range(CH):
                e.wait_ge(s_y, STEPS + 1 + c)
                e.tensor_tensor(m.sres[:, c, :], Y[:, c, :], m.sres[:, c, :], ALU.mult).then_inc(s_yg, 1)
            for g in range(TILES // 2):
                e.wait_ge(s_o, g + 1)
                x = k.x[:, 2 * g:2 * g + 2, :].rearrange("p t d -> p (t d)")
                e.tensor_tensor(x, x, out(2 * g, 2), ALU.add).then_inc(s_xa, 1)
                e.wait_ge(s_xa, g + 1)
                for t in (2 * g, 2 * g + 1):
                    tile_stats(e, k, t)

        @block.tensor
        def _(e):
            for c in range(CH):
                for h in range(2):
                    i = e.matmul(Y[:, c, h * HALF:(h + 1) * HALF], m.diagD[:, c, :],
                                 m.u[:, c, h * HALF:(h + 1) * HALF], start=True, stop=False,
                                 skip_group_check=True)
                i.then_inc(s_y, 1)

            def body(n, q, c, s):
                e.wait_ge(s_hc, s + 1)
                for h in range(2):
                    i = e.matmul(Y[:, c, h * HALF:(h + 1) * HALF], k.ident[:, :],
                                 hh[c][:, h * HALF:(h + 1) * HALF], start=False, stop=True,
                                 skip_group_check=True)
                i.then_inc(s_y, 1)

            steps(e, body)

            def out_proj(t, c):
                return e.matmul(out(t, 1), m.sres[:, c, t * P:(t + 1) * P], k.w_out[:, c, :],
                                start=c == 0 and t % 2 == 0, stop=True, skip_group_check=True)

            for c in range(CH):
                e.wait_ge(s_yg, c + 1)
                for t in range(TILES // 2):
                    i = out_proj(t, c)
                    if c == CH - 1 and t % 2:
                        i.then_inc(s_o, 1)
            for t in range(TILES // 2, TILES, 2):
                for c in range(CH):
                    for u in range(2):
                        i = out_proj(t + u, c)
                i.then_inc(s_o, 1)


def spiking_ffn(nc, k):
    beta, thr, steps = 0.9, 1.0, 5
    with ExitStack() as ctx:
        sb, ps, sem = tools(nc, ctx)
        r_sb = [sb(f"r{i}", [P, HALF]) for i in range(2)]
        hT = sb("hT", [P, FM, TOK])
        y = [sb(f"y{i}", [P, 2 * D]) for i in range(2)]
        mem = [sb(f"mem{i}", [P, 2 * D]) for i in range(2)]
        drive = sb("drive", [P, 2 * D])
        cnt = sb("cnt", [P, 2 * D])
        fp = [ps(f"fp{i}") for i in range(4)]
        yp = [ps(f"yp{i}") for i in range(2)]
        s_fc = sem("f_fc")
        s_re = sem("f_re")
        s_h = sem("f_h")
        s_pr = sem("f_pr")
        s_y = sem("f_y")
        s_d = sem("f_d")
        block = ctx.enter_context(nc.Block())
        blocks = [(m, h) for h in range(2) for m in range(FM)]

        @block.tensor
        def _(e):
            e.wait_ge(k.s_w3, k.n_w3)
            AHEAD = 3
            for h in range(2):
                for n in (range(FM + AHEAD), range(FM + AHEAD, 2 * FM))[h]:
                    m, hf = n % FM, n // FM
                    if n >= 4:
                        e.wait_ge(s_re, n - 3)
                    for kt in range(KD):
                        i = e.matmul(fp[n % 4][:, :], k.w_fc[:, kt, m * P:(m + 1) * P],
                                     k.xT[:, kt, hf * HALF:(hf + 1) * HALF], start=kt == 0, stop=kt == 1)
                    i.then_inc(s_fc, 1)
                e.wait_ge(s_h, FM * (h + 1))
                for g in (2 * h, 2 * h + 1):
                    if g >= 2:
                        e.wait_ge(s_y, g - 1)
                    for u in range(2):
                        t = 2 * g + u
                        for m in range(FM):
                            i = e.matmul(yp[g % 2][:, u * D:(u + 1) * D], hT[:, m, t * P:(t + 1) * P],
                                         k.w_pr[:, m, :], start=m == 0, stop=m == FM - 1)
                    i.then_inc(s_pr, 1)

        @block.scalar
        def _(e):
            for h in range(2):
                for n in range(FM * h, FM * (h + 1)):
                    m = n % FM
                    e.wait_ge(s_fc, n + 1)
                    if n >= 2:
                        e.wait_ge(s_h, n - 1)
                    e.activation(r_sb[n % 2][:, :], fp[n % 4][:, :], ACT.Relu).then_inc(s_re, 1)
                for g in (2 * h, 2 * h + 1):
                    e.wait_ge(s_pr, g + 1)
                    if g >= 2:
                        e.wait_ge(s_d, 14 * (g - 1))
                    e.activation(y[g % 2][:, :], yp[g % 2][:, :], ACT.Copy).then_inc(s_y, 1)

        @block.gpsimd
        def _(e):
            for n, (m, h) in enumerate(blocks):
                e.wait_ge(s_re, n + 1)
                r = r_sb[n % 2]
                e.tensor_tensor(hT[:, m, h * HALF:(h + 1) * HALF], r[:, :], r[:, :], ALU.mult).then_inc(s_h, 1)

        @block.vector
        def _(e):
            n = 0

            def chain(ins, wait=True):
                nonlocal n
                n += 1
                ins.then_inc(s_d, 1)
                if wait:
                    e.wait_ge(s_d, n)

            def count(cur, first):
                if first:
                    chain(e.tensor_scalar(cnt[:, :], cur, thr, None, ALU.is_gt), wait=False)
                else:
                    chain(e.scalar_tensor_tensor(cnt[:, :], cur, thr, cnt[:, :], ALU.is_gt, ALU.add), wait=False)
                e.wait_ge(s_d, n - 1)

            for g in range(TILES // 2):
                e.wait_ge(s_y, g + 1)
                yg = y[g % 2][:, :]
                cur = yg
                for s in range(1, steps):
                    nxt = mem[s % 2][:, :]
                    chain(e.scalar_tensor_tensor(drive[:, :], cur, beta, yg, ALU.mult, ALU.add), wait=False)
                    count(cur, s == 1)
                    chain(e.scalar_tensor_tensor(nxt, cur, thr, drive[:, :], ALU.is_gt, ALU.subtract,
                                                 reverse1=True))
                    cur = nxt
                count(cur, False)
                x = k.x[:, 2 * g:2 * g + 2, :].rearrange("p t d -> p (t d)")
                e.wait_ge(s_d, n)
                chain(e.scalar_tensor_tensor(x, cnt[:, :], 1.0 / steps, x, ALU.mult, ALU.add))
                for t in (2 * g, 2 * g + 1):
                    tile_stats(e, k, t)


def windowed_attention(nc, k):
    with ExitStack() as ctx:
        sb, _, _ = tools(nc, ctx)
        qT = sb("q4T", [P, TILES, KD, P])
        kT = sb("k4T", [P, TILES, KD, P])
        vx = sb("vx", [P, TILES, H, DV])
        windowed_projections(nc, k, qT, kT, vx)
        windowed_heads(nc, k, qT, kT, vx)


def windowed_projections(nc, k, qT, kT, vx):
    with ExitStack() as ctx:
        sb, ps, sem = tools(nc, ctx)
        qk = [sb(f"qk{i}", [P, 2 * H, DH]) for i in range(2)]
        t2 = [sb(f"t2{i}", [P, 2 * H, DH]) for i in range(2)]
        t1 = [sb(f"t1{i}", [P, 2 * H, DH]) for i in range(2)]
        rot = [sb(f"rot{i}", [P, 2 * H, DH]) for i in range(2)]
        QK = [ps(f"QK{i}") for i in range(2)]
        V = [ps(f"V{i}") for i in range(2)]
        TQ = [ps(f"TQ{i}") for i in range(2)]
        s_pj = sem("w_pj")
        s_vj = sem("w_vj")
        s_b = sem("w_b")
        s_v = sem("w_v")
        s_sn = sem("w_sn")
        s_cs = sem("w_cs")
        s_rt = sem("w_rt")
        s_tq = sem("w_tq")
        s_qe = sem("w_qe")
        with nc.Block() as block:
            @block.tensor
            def _(e):
                e.wait_ge(k.s_w4, k.n_w4)

                def turn(t):
                    e.wait_ge(s_rt, t + 1)
                    if t >= 2:
                        e.wait_ge(s_qe, t - 1)
                    for c in range(2 * KD):
                        i = e.transpose(TQ[t % 2][:, c * P:(c + 1) * P],
                                        rot[t % 2][:, c * HG:(c + 1) * HG, :].rearrange("p h d -> p (h d)"),
                                        k.ident[:, :])
                    i.then_inc(s_tq, 1)

                for t in range(TILES):
                    if t >= 2:
                        e.wait_ge(s_b, t - 1)
                        e.wait_ge(s_v, t - 1)
                    tok = slice(t * P, (t + 1) * P)
                    for src, w, dst in ((k.xT, k.w4[0], QK[t % 2][:, 0:D]), (k.c0T, k.w4[1], QK[t % 2][:, D:2 * D]),
                                        (k.c0T, k.w4[2], V[t % 2][:, 0:D])):
                        for c in range(KD):
                            i = e.matmul(dst, src[:, c, tok], w[:, c, :], start=c == 0, stop=c == 1)
                        if w is not k.w4[0]:
                            i.then_inc(s_pj if w is k.w4[1] else s_vj, 1)
                    if t:
                        turn(t - 1)
                turn(TILES - 1)

            @block.scalar
            def _(e):
                for t in range(TILES):
                    e.wait_ge(s_tq, t + 1)
                    src = TQ[t % 2][:, :].rearrange("p (c n) -> p c n", n=P)
                    e.activation(qT[:, t, :, :], src[:, 0:KD, :], ACT.Copy)
                    e.activation(kT[:, t, :, :], src[:, KD:2 * KD, :], ACT.Copy).then_inc(s_qe, 1)

            @block.gpsimd
            def _(e):
                e.wait_ge(k.s_w4, k.n_w4)
                e.memset(vx[:, :, :, DH:DV], 1.0)

                for t in range(TILES):
                    e.wait_ge(s_b, t + 1)
                    if t >= 2:
                        e.wait_ge(s_rt, t - 1)
                    hd = DH // 2
                    sn = [k.trig[:, 1, i * hd:(i + 1) * hd].unsqueeze(1).to_broadcast([P, 2 * H, hd]) for i in range(2)]
                    e.tensor_tensor(t2[t % 2][:, :, 0:hd], qk[t % 2][:, :, hd:DH], sn[0], ALU.mult)
                    e.tensor_tensor(t2[t % 2][:, :, hd:DH], qk[t % 2][:, :, 0:hd], sn[1], ALU.mult).then_inc(s_sn, 1)

            @block.vector
            def _(e):
                e.wait_ge(k.s_w4, k.n_w4)
                bias = k.rows[:, ROWV["bq4"]:ROWV["bq4"] + 2, :].rearrange("p r (h d) -> p (r h) d", d=DH)

                for t in range(TILES):
                    r = t % 2
                    e.wait_ge(s_pj, t + 1)
                    e.wait_ge(s_sn, t - 1) if t >= 2 else None
                    e.tensor_tensor(qk[r][:, :, :], QK[r][:, :].rearrange("p (h d) -> p h d", d=DH), bias, ALU.add
                                    ).then_inc(s_b, 1)
                    e.wait_ge(s_vj, t + 1)
                    e.tensor_tensor(vx[:, t, :, 0:DH], V[r][:, 0:D].rearrange("p (h d) -> p h d", d=DH),
                                    rowvec(k, "bv4").rearrange("p (h d) -> p h d", d=DH), ALU.add
                                    ).then_inc(s_v, 1)
                    e.wait_ge(s_b, t + 1)
                    cs = k.trig[:, 0, :].unsqueeze(1).to_broadcast([P, 2 * H, DH])
                    e.tensor_tensor(t1[r][:, :, :], qk[r][:, :, :], cs, ALU.mult).then_inc(s_cs, 1)
                    e.wait_ge(s_cs, t + 1)
                    e.wait_ge(s_sn, t + 1)
                    if t >= 2:
                        e.wait_ge(s_tq, t - 1)
                    e.tensor_tensor(rot[r][:, :, :], t1[r][:, :, :], t2[r][:, :, :], ALU.add).then_inc(s_rt, 1)
                e.tensor_tensor(k.x[:, :, :], k.x[:, :, :],
                                rowvec(k, "bo4").unsqueeze(1).to_broadcast([P, TILES, D]), ALU.add)


def windowed_heads(nc, k, qT, kT, vx):
    scale = float(DH) ** -0.5
    with ExitStack() as ctx:
        sb, ps, sem = tools(nc, ctx)
        qs = [sb(f"hqs{i}", [P, KD, P]) for i in range(2)]
        kb = [sb(f"hkb{i}", [P, 2, KD, HG * L]) for i in range(2)]
        mx = [sb(f"hmx{i}", [P, H]) for i in range(2)]
        sm = [sb(f"hsm{i}", [P, H, L]) for i in range(2)]
        pb = [sb(f"hpb{i}", [P, H, P]) for i in range(2)]
        pT = sb("hpT", [P, H, P])
        ri = sb("hri", [P, H])
        on = [sb(f"hon{i}", [P, D]) for i in range(2)]
        onT = sb("honT", [P, KD, P])
        S = ps("hS", [P, 2 * HALF])
        TP = [ps(f"hTP{i}") for i in range(4)]
        O = ps("hO")
        X = ps("hX")
        s_z = sem("h_z")
        s_qs = sem("h_qs")
        s_sc = sem("h_sc")
        s_mx = sem("h_mx")
        s_sm = sem("h_sm")
        s_ex = sem("h_ex")
        s_tp = sem("h_tp")
        s_te = sem("h_te")
        s_pv = sem("h_pv")
        s_ri = sem("h_ri")
        s_on = sem("h_on")
        s_ot = sem("h_ot")
        s_oe = sem("h_oe")
        s_wo = sem("h_wo")
        s_xa = sem("h_xa")
        block = ctx.enter_context(nc.Block())

        def pipeline(e, sub):
            for i in range(2):
                sub(i, i % 2, lambda d, i=i: i - d >= 0)
            with e.Fori(1, TILES // 2) as j:
                sub(j * 2, 0, lambda d: True)
                sub(j * 2 + 1, 1, lambda d: True)
            for i in range(TILES, TILES + 2):
                sub(i, i % 2, lambda d, i=i: i - d < TILES)

        def at(a, i):
            return a[:, i] if isinstance(i, int) else a[:, bass.ds(i, 1)].squeeze(1)

        @block.tensor
        def _(e):
            def sub(i, r, live):
                if live(0):
                    e.wait_ge(s_qs, i + 1)
                    e.wait_ge(s_sm, i)
                    for c in range(KD):
                        e.matmul(S[:, c * HALF:(c + 1) * HALF], k.ident_bf[:, :], k.causal_bf[:, :],
                                 start=True, stop=True)
                        for b in range(2):
                            j = e.matmul(S[64 * b:64 * b + 64, c * HALF:(c + 1) * HALF],
                                         qs[r][:, c, 64 * b:64 * b + 64], kb[r][:, b, c, :],
                                         start=False, stop=True, skip_group_check=True)
                    j.then_inc(s_sc, 1)
                if live(1):
                    e.wait_ge(s_ex, i * 2)
                    for g in range(4):
                        for u in range(4):
                            j = e.transpose(TP[g][:, u * P:(u + 1) * P], pb[1 - r][:, 4 * g + u, :], k.ident[:, :])
                        j.then_inc(s_tp, 1)
                if live(2):
                    e.wait_ge(s_on, i - 1)
                    if not isinstance(i, int) or i > 2:
                        e.wait_ge(s_xa, i - 2)
                    for c in range(KD):
                        j = e.transpose(X[:, c * P:(c + 1) * P], on[r][:, c * P:(c + 1) * P], k.ident[:, :])
                    j.then_inc(s_ot, 1)
                if live(1):
                    e.wait_ge(s_on, i - 1)
                    v = at(vx, i - 1)
                    for g in range(4):
                        e.wait_ge(s_te, (i - 1) * 4 + g + 1)
                        for h in range(4 * g, 4 * g + 4):
                            j = e.matmul(O[:, h * DV:(h + 1) * DV], pT[:, h, :], v[:, h, :], start=True, stop=True)
                    j.then_inc(s_pv, 1)
                if live(2):
                    e.wait_ge(s_oe, i - 1)
                    for c in range(KD):
                        j = e.matmul(X[:, D:2 * D], onT[:, c, :], k.w4[3][:, c, :], start=c == 0, stop=c == 1)
                    j.then_inc(s_wo, 1)

            pipeline(e, sub)

        @block.scalar
        def _(e):
            e.wait_ge(s_z, 2)

            def sub(i, r, live):
                if live(1):
                    e.wait_ge(s_pv, i - 1)
                    for g in range(4):
                        e.wait_ge(s_tp, (i - 1) * 4 + g + 1)
                        e.activation(pT[:, 4 * g:4 * g + 4, :], TP[g][:, :].rearrange("p (u n) -> p u n", n=P),
                                     ACT.Copy).then_inc(s_te, 1)
                if live(2):
                    e.wait_ge(s_ot, i - 1)
                    if not isinstance(i, int) or i > 2:
                        e.wait_ge(s_wo, i - 2)
                    e.activation(onT[:, :, :], X[:, 0:D].rearrange("p (c n) -> p c n", c=KD), ACT.Copy
                                 ).then_inc(s_oe, 1)
                if live(0):
                    if not isinstance(i, int) or i >= 2:
                        e.wait_ge(s_tp, (i - 1) * 4)
                    e.wait_ge(s_sm, i + 1)
                    for b in range(2):
                        rows = slice(64 * b, 64 * b + 64)
                        e.activation(pb[r][rows, :, 64 * b:64 * b + 64], sm[r][rows, :, :], ACT.Exp, scale=scale
                                     ).then_inc(s_ex, 1)

            pipeline(e, sub)

        @block.gpsimd
        def _(e):
            for r in range(2):
                e.memset(pb[r][:, :, :], 0.0).then_inc(s_z, 1)

            def sub(i, r, live):
                if live(0):
                    if not isinstance(i, int) or i >= 2:
                        e.wait_ge(s_sc, i - 1)
                    e.tensor_copy(qs[r][:, :, :], at(qT, i))
                    keys = at(kT, i)
                    for b in range(2):
                        for c in range(KD):
                            j = e.tensor_tensor(kb[r][:, b, c, :].rearrange("p (h n) -> p h n", n=L),
                                                keys[:, c, b * L:(b + 1) * L].unsqueeze(1).to_broadcast([P, HG, L]),
                                                k.own_head[:, :].unsqueeze(2).to_broadcast([P, HG, L]), ALU.mult)
                    j.then_inc(s_qs, 1)

            pipeline(e, sub)

        @block.vector
        def _(e):
            def sub(i, r, live):
                if live(0):
                    e.wait_ge(s_sc, i + 1)
                    Sv = S[:, :].rearrange("p (h n) -> p h n", n=L)
                    e.reduce_max(mx[r][:, :], Sv, AX.X).then_inc(s_mx, 1)
                    e.wait_ge(s_mx, i + 1)
                    if not isinstance(i, int) or i >= 2:
                        e.wait_ge(s_ex, (i - 1) * 2)
                    e.tensor_tensor(sm[r][:, :, :], Sv, mx[r][:, :].unsqueeze(2).to_broadcast([P, H, L]),
                                    ALU.subtract).then_inc(s_sm, 1)
                if live(1):
                    e.wait_ge(s_pv, i)
                    Ov = O[:, 0:H * DV].rearrange("p (h d) -> p h d", d=DV)
                    e.reciprocal(ri[:, :], Ov[:, :, DH]).then_inc(s_ri, 1)
                    e.wait_ge(s_ri, i)
                    e.tensor_tensor(on[1 - r][:, :].rearrange("p (h d) -> p h d", d=DH), Ov[:, :, 0:DH],
                                    ri[:, :].unsqueeze(2).to_broadcast([P, H, DH]), ALU.mult).then_inc(s_on, 1)
                if live(2):
                    e.wait_ge(s_wo, i - 1)
                    x = at(k.x, i - 2)
                    e.tensor_tensor(x, x, X[:, D:2 * D], ALU.add).then_inc(s_xa, 1)
                    e.wait_ge(s_xa, i - 1)
                    tile_stats(e, k, i - 2)

            pipeline(e, sub)


def phase_attention(nc, k):
    scale = 1.0 / float(D) ** 0.5
    n_pairs = float(L * L)
    with ExitStack() as ctx:
        sb, ps, sem = tools(nc, ctx)
        qT = sb("q5T", [P, KD, TOK])
        kT = sb("k5T", [P, KD, TOK])
        v = sb("v5", [P, TILES, D])
        qp = sb("qp", [P, TILES, 2])
        diag = sb("diag", [P, 2, TILES, L])
        dd = sb("dd", [P, 2, TILES, L])
        dq = sb("dq", [P, 2, TILES, L])
        dist = sb("dist", [P, TILES, L])
        dev = sb("dev", [P, TILES, L])
        small = sb("small", [P, 8, TILES])
        rowsum, mean, rowsq, var, std, thr, mx, tot = (small[:, i, :] for i in range(8))
        ri = sb("ri5", [P, TILES])
        ok = sb("ok", [P, TILES, L])
        ady = sb("ady", [P, TILES, L])
        sm = sb("sm5", [P, TILES, L])
        pb = sb("pb5", [P, TILES, P])
        pT = sb("p5T", [P, TILES, P])
        cn = sb("cn", [P, TILES, D])
        cnT = sb("cnT", [P, KD, TOK])
        nrm = sb("nrm", [P, 2, TILES])
        qsq = sb("qsq", [P, TILES, 2])
        re = sb("re", [P, TILES, 2])
        reT = sb("reT", [2, TOK])
        bias = sb("bias5", [P, D])
        BK = [ps(f"BK{i}") for i in range(8)]
        s_pe = sem("p_pe")
        s_ac = sem("p_ac")
        s_ve = sem("p_ve")
        s_z = sem("p_z")
        block = ctx.enter_context(nc.Block())
        pe_at, ac_at, ve_at = {}, {}, {}
        pe_steps = (["qp"] + [("qk", n) for n in range(8)] + ["row"] + [("v", g) for g in range(4)] + ["sum"]
                    + ["scores", "sumsq", "reT"] + [("pT", g) for g in range(2)] + [("pv", g) for g in range(4)]
                    + [("cT", g) for g in range(4)] + [("o", g) for g in range(4)])
        for n, name in enumerate(pe_steps):
            pe_at[name] = n + 1
        ac_steps = ([("qk", n) for n in range(8)] + [("v", g) for g in range(4)] + ["nrm", "std", "exp0", "exp", "reT"]
                    + [("pT", 1)] + [("cT", g) for g in range(4)])
        for n, name in enumerate(ac_steps):
            ac_at[name] = n + 1
        ve_steps = ["qp", "qsq", "nrm2", "diag", "dd", "dq", "dist", "rowsum", "mean", "dev", "devsq", "rowsq",
                    "var", "nrmx", "nri", "re", "bias", "ady0", "ady", "ok", "okc", "thr", "in", "ok2", "add", "masked",
                    "mx", "sub", "den", "ri", ("pT", 0)] + [("cn", g) for g in range(4)] + ["xadd0", "xadd"] + [("x", g) for g in range(4)]
        for n, name in enumerate(ve_steps):
            ve_at[name] = n + 1
        made = {"pe": 0, "ac": 0, "ve": 0}

        def mark(ins, table, who, sem_, name):
            made[who] += 1
            assert table[name] == made[who], (name, made[who])
            ins.then_inc(sem_, 1)

        @block.tensor
        def _(e):
            done = lambda ins, name: mark(ins, pe_at, "pe", s_pe, name)
            ac = lambda name: e.wait_ge(s_ac, ac_at[name])
            ve = lambda name: e.wait_ge(s_ve, ve_at[name])
            e.wait_ge(k.s_w5, k.n_w5)
            for t in range(TILES):
                for c in range(KD):
                    i = e.matmul(BK[6][:, 2 * t:2 * t + 2], k.xT[:, c, t * P:(t + 1) * P], k.wtq[:, c, :],
                                 start=c == 0, stop=c == 1)
            done(i, "qp")
            n = 0
            for w, m in ((0, 0), (0, 1), (1, 0), (1, 1)):
                for h in range(2):
                    if n >= 4:
                        ac(("qk", n - 4))
                    for c in range(KD):
                        i = e.matmul(BK[n % 4][:, :], k.w5[w][:, c, m * P:(m + 1) * P],
                                     k.xT[:, c, h * HALF:(h + 1) * HALF], start=c == 0, stop=c == 1)
                    done(i, ("qk", n))
                    n += 1
            ve("diag")
            for g in range(2):
                i = e.matmul(BK[4 + g][:, :], k.same_batch[:, :], diag[:, g, :, :].rearrange("p t n -> p (t n)"),
                             start=True, stop=True)
            done(i, "row")
            for g in range(4):
                ac(("qk", 4 + g))
                for u in range(2):
                    t = 2 * g + u
                    for c in range(KD):
                        i = e.matmul(BK[g][:, u * D:(u + 1) * D], k.xT[:, c, t * P:(t + 1) * P], k.w5[2][:, c, :],
                                     start=c == 0, stop=c == 1)
                done(i, ("v", g))
            ve("rowsum")
            done(e.matmul(BK[6][:, 64:64 + TILES], k.same_batch[:, :], rowsum, start=True, stop=True), "sum")
            for t in range(TILES):
                for c in range(KD):
                    for b in range(2):
                        q = slice(t * P + 64 * b, t * P + 64 * b + 64)
                        i = e.matmul(BK[7][64 * b:64 * b + 64, t * L:(t + 1) * L], qT[:, c, q], kT[:, c, q],
                                     start=c == 0, stop=c == 1)
            done(i, "scores")
            ve("rowsq")
            done(e.matmul(BK[6][:, 128:128 + TILES], k.same_batch[:, :], rowsq, start=True, stop=True), "sumsq")
            ve("re")
            ac(("v", 3))
            for t in range(TILES):
                i = e.transpose(BK[t // 4][0:2, (t % 4) * P:(t % 4 + 1) * P], re[:, t, :], k.ident[:, :])
            done(i, "reT")
            ve("ri")
            ac("exp")
            ac("reT")
            for g in range(2):
                for u in range(4):
                    i = e.transpose(BK[4 + g][:, u * P:(u + 1) * P], pb[:, 4 * g + u, :], k.ident[:, :])
                done(i, ("pT", g))
            ve(("pT", 0))
            ac(("pT", 1))
            for g in range(4):
                for u in range(2):
                    t = 2 * g + u
                    i = e.matmul(BK[g][:, u * D:(u + 1) * D], pT[:, t, :], v[:, t, :], start=True, stop=True)
                done(i, ("pv", g))
            for g in range(4):
                ve(("cn", g))
                for u in range(2):
                    for c in range(KD):
                        i = e.transpose(BK[4 + g][:, (2 * u + c) * P:(2 * u + c + 1) * P],
                                        cn[:, 2 * g + u, c * P:(c + 1) * P], k.ident[:, :])
                done(i, ("cT", g))
            for g in range(4):
                ac(("cT", g))
                for u in range(2):
                    t = 2 * g + u
                    for c in range(KD):
                        e.matmul(BK[g][:, u * D:(u + 1) * D], cnT[:, c, t * P:(t + 1) * P], k.w5[3][:, c, :],
                                 start=c == 0, stop=False)
                    i = e.matmul(BK[g][:, u * D:(u + 1) * D], reT[:, t * P:(t + 1) * P], k.wfq[:, :],
                                 start=False, stop=True)
                done(i, ("o", g))

        @block.scalar
        def _(e):
            done = lambda ins, name: mark(ins, ac_at, "ac", s_ac, name)
            pe = lambda name: e.wait_ge(s_pe, pe_at[name])
            ve = lambda name: e.wait_ge(s_ve, ve_at[name])
            n = 0
            for dst, b in ((qT, "bq5"), (kT, "bk5")):
                for m in range(KD):
                    for h in range(2):
                        pe(("qk", n))
                        done(e.activation(dst[:, m, h * HALF:(h + 1) * HALF], BK[n % 4][:, :], ACT.Identity,
                                          bias=col(k, b, m)), ("qk", n))
                        n += 1
            for g in range(4):
                pe(("v", g))
                done(e.activation(v[:, 2 * g:2 * g + 2, :].rearrange("p t d -> p (t d)"), BK[g][:, :], ACT.Copy),
                     ("v", g))
            ve("nrm2")
            done(e.activation(nrm[:, 1, :], nrm[:, 0, :], ACT.Sqrt), "nrm")
            ve("var")
            done(e.activation(std, var, ACT.Sqrt), "std")
            e.wait_ge(s_z, 1)
            ve("sub")
            for b in range(2):
                rows = slice(64 * b, 64 * b + 64)
                done(e.activation(pb[rows, :, 64 * b:64 * b + 64], sm[rows, :, :], ACT.Exp, scale=scale),
                     "exp0" if b == 0 else "exp")
            pe("reT")
            for g in range(2):
                i = e.activation(reT[:, g * HALF:(g + 1) * HALF], BK[g][0:2, :], ACT.Copy)
            done(i, "reT")
            pe(("pT", 1))
            done(e.activation(pT[:, 4:8, :], BK[5][:, :].rearrange("p (t n) -> p t n", n=P), ACT.Copy), ("pT", 1))
            for g in range(4):
                pe(("cT", g))
                src = BK[4 + g][:, :].rearrange("p (u c n) -> p c u n", u=2, c=KD)
                dst = cnT[:, :, 2 * g * P:(2 * g + 2) * P].rearrange("p c (u n) -> p c u n", u=2)
                done(e.activation(dst, src, ACT.Copy), ("cT", g))

        @block.gpsimd
        def _(e):
            e.memset(pb[:, :, :], 0.0).then_inc(s_z, 1)
            e.memset(k.one[:, :], 1.0).then_inc(s_z, 1)
            e.wait_ge(s_z, 2)
            for x in range(2):
                split_expert(e, k, x, x, 0)

        @block.sync
        def _(e):
            for x in range(2):
                load_expert(e, k, x, x)

        @block.vector
        def _(e):
            pe = lambda name: e.wait_ge(s_pe, pe_at[name])
            ac = lambda name: e.wait_ge(s_ac, ac_at[name])

            def done(ins, name):
                mark(ins, ve_at, "ve", s_ve, name)

            def chain(ins, name):
                done(ins, name)
                e.wait_ge(s_ve, ve_at[name])

            wide = lambda a: a.unsqueeze(2).to_broadcast([P, TILES, L])
            e.wait_ge(k.s_w5, k.n_w5)
            pe("qp")
            chain(e.tensor_tensor(qp[:, :, :], BK[6][:, 0:2 * TILES].rearrange("p (t w) -> p t w", w=2),
                                  k.btq[:, :].unsqueeze(1).to_broadcast([P, TILES, 2]), ALU.add), "qp")
            chain(e.tensor_tensor(qsq[:, :, :], qp[:, :, :], qp[:, :, :], ALU.mult), "qsq")
            chain(e.tensor_tensor(nrm[:, 0, :], qsq[:, :, 0], qsq[:, :, 1], ALU.add), "nrm2")
            for g in range(2):
                i = e.tensor_tensor(diag[:, g, :, :], wide(qp[:, :, g]),
                                    k.diag64[:, :].unsqueeze(1).to_broadcast([P, TILES, L]), ALU.mult)
            chain(i, "diag")
            pe("row")
            for g in range(2):
                i = e.tensor_tensor(dd[:, g, :, :], wide(qp[:, :, g]),
                                    BK[4 + g][:, :].rearrange("p (t n) -> p t n", n=L), ALU.subtract)
            chain(i, "dd")
            chain(e.tensor_tensor(dq[:, :, :, :].rearrange("p g t n -> p (g t n)"),
                                  dd[:, :, :, :].rearrange("p g t n -> p (g t n)"),
                                  dd[:, :, :, :].rearrange("p g t n -> p (g t n)"), ALU.mult), "dq")
            chain(e.tensor_tensor(dist[:, :, :], dq[:, 0, :, :], dq[:, 1, :, :], ALU.add), "dist")
            chain(e.reduce_sum(rowsum, dist[:, :, :], AX.X), "rowsum")
            pe("sum")
            chain(e.tensor_scalar(mean, BK[6][:, 64:64 + TILES], 1.0 / n_pairs, None, ALU.mult), "mean")
            chain(e.tensor_tensor(dev[:, :, :], dist[:, :, :], wide(mean), ALU.subtract), "dev")
            chain(e.tensor_tensor(dev[:, :, :], dev[:, :, :], dev[:, :, :], ALU.mult), "devsq")
            chain(e.reduce_sum(rowsq, dev[:, :, :], AX.X), "rowsq")
            pe("sumsq")
            done(e.tensor_scalar(var, BK[6][:, 128:128 + TILES], 1.0 / (n_pairs - 1.0), None, ALU.mult), "var")
            ac("nrm")
            chain(e.tensor_scalar(nrm[:, 0, :], nrm[:, 1, :], 1e-12, None, ALU.max), "nrmx")
            chain(e.reciprocal(nrm[:, 1, :], nrm[:, 0, :]), "nri")
            done(e.scalar_tensor_tensor(re[:, :, :], qp[:, :, :], 0.1,
                                        nrm[:, 1, :].unsqueeze(2).to_broadcast([P, TILES, 2]), ALU.mult, ALU.mult),
                 "re")
            done(e.scalar_tensor_tensor(bias[:, :], rowvec(k, "bfq"), 0.1, rowvec(k, "bo5"), ALU.mult, ALU.add),
                 "bias")
            chain(e.tensor_scalar(ady[:, :, :], dd[:, 1, :, :], -4096.0, None, ALU.mult), "ady0")
            chain(e.scalar_tensor_tensor(ady[:, :, :], dd[:, 1, :, :], 4096.0, ady[:, :, :], ALU.mult, ALU.max), "ady")
            chain(e.scalar_tensor_tensor(ok[:, :, :], dd[:, 0, :, :], -1.0, ady[:, :, :], ALU.mult, ALU.is_le), "ok")
            chain(e.tensor_tensor(ok[:, :, :], ok[:, :, :], k.causal[:, :].unsqueeze(1).to_broadcast([P, TILES, L]),
                                  ALU.mult), "okc")
            ac("std")
            chain(e.scalar_tensor_tensor(thr, std, 1.25, mean, ALU.mult, ALU.add), "thr")
            chain(e.tensor_tensor(dev[:, :, :], dist[:, :, :], wide(thr), ALU.is_le), "in")
            chain(e.tensor_tensor(ok[:, :, :], ok[:, :, :], dev[:, :, :], ALU.mult), "ok2")
            chain(e.tensor_scalar(ok[:, :, :], ok[:, :, :], -NEG, NEG, ALU.mult, ALU.add), "add")
            pe("scores")
            chain(e.tensor_tensor(sm[:, :, :], BK[7][:, :].rearrange("p (t n) -> p t n", n=L), ok[:, :, :], ALU.add),
                  "masked")
            chain(e.reduce_max(mx, sm[:, :, :], AX.X), "mx")
            done(e.tensor_tensor(sm[:, :, :], sm[:, :, :], wide(mx), ALU.subtract), "sub")
            ac("exp")
            for b in range(2):
                rows = slice(64 * b, 64 * b + 64)
                i = e.reduce_sum(tot[rows], pb[rows, :, 64 * b:64 * b + 64], AX.X)
            chain(i, "den")
            done(e.reciprocal(ri[:, :], tot), "ri")
            pe(("pT", 0))
            done(e.tensor_copy(pT[:, 0:4, :], BK[4][:, :].rearrange("p (t n) -> p t n", n=P)), ("pT", 0))
            for g in range(4):
                pe(("pv", g))
                for u in range(2):
                    t = 2 * g + u
                    i = e.scalar_tensor_tensor(cn[:, t, :], BK[g][:, u * D:(u + 1) * D], ri[:, t:t + 1],
                                               rowvec(k, "bv5"), ALU.mult, ALU.add)
                done(i, ("cn", g))
            chain(e.tensor_tensor(k.x[:, :, :].rearrange("p t d -> p (t d)"), k.x[:, :, :].rearrange("p t d -> p (t d)"),
                                  k.xn[:, :, :].rearrange("p t d -> p (t d)"), ALU.add), "xadd0")
            chain(e.tensor_tensor(k.x[:, :, :], k.x[:, :, :], bias[:, :].unsqueeze(1).to_broadcast([P, TILES, D]),
                                  ALU.add), "xadd")
            for g in range(4):
                pe(("o", g))
                x = k.x[:, 2 * g:2 * g + 2, :].rearrange("p t d -> p (t d)")
                chain(e.tensor_tensor(x, x, BK[g][:, :], ALU.add), ("x", g))
                for t in (2 * g, 2 * g + 1):
                    tile_stats(e, k, t)


def load_expert(e, k, x, r):
    for i in range(2):
        src = k.w_experts[i][x] if isinstance(x, int) else k.w_experts[i][bass.ds(x, 1)].squeeze(0)
        e.dma_start(k.w6[r][:, i, :, :], src.rearrange("(c p) n -> p c n", p=P)).then_inc(k.s_w[r], 16)


def split_expert(e, k, x, r, j):
    e.wait_ge(k.s_w[r], j * 32 + 32)
    for i in range(2):
        e.tensor_tensor(k.w_hi[r][:, i, :, :], k.w6[r][:, i, :, :],
                        k.one[:, :].unsqueeze(2).to_broadcast([P, KD, D]), ALU.mult).then_inc(k.s_hi, 1)
    for i in range(2):
        e.wait_ge(k.s_hi, x * 2 + (i + 1))
        e.tensor_tensor(k.w_lo[r][:, i, :, :], k.w6[r][:, i, :, :], k.w_hi[r][:, i, :, :].bitcast(F32), ALU.subtract
                        ).then_inc(k.s_ws, 1)


def experts(nc, k):
    with ExitStack() as ctx:
        sb, ps, sem = tools(nc, ctx)
        score = sb("score", [P, TILES, E])
        top = sb("top", [P, TILES, 8])
        idx = sb("idx", [P, TILES, 8], U32)
        idf = sb("idf", [P, TILES, 8])
        pick = [sb(f"pick{i}", [P, TILES, E]) for i in range(TOPK)]
        comb = sb("comb", [P, TILES, E])
        combT = sb("combT", [E, TOK])
        b1 = [sb(f"eb1{i}", [P, 2]) for i in range(2)]
        hid = [sb(f"hid{n}", [P, HALF]) for n in range(4)]
        h_hi = [sb(f"h_hi{i}", [P, KD, TOK], F32R) for i in range(2)]
        h_lo = [sb(f"h_lo{i}", [P, KD, TOK], F32R) for i in range(2)]
        HB = [ps(f"HB{i}") for i in range(4)]
        OB = [ps(f"OB{i}") for i in range(4)]
        s_g = sem("e_g")
        s_t = sem("e_t")
        s_ct = sem("e_ct")
        s_b1 = sem("e_b1")
        s_h = sem("e_h")
        s_r = sem("e_r")
        s_l = sem("e_l")
        s_o = sem("e_o")
        s_a = sem("e_a")
        block = ctx.enter_context(nc.Block())
        blocks = [(m, h) for h in range(2) for m in range(KD)]

        def per_expert(e, body, between=None):
            body(0, 0, 0)
            if between:
                between()
            body(1, 1, 0)
            with e.Fori(1, E // 2) as j:
                for r in range(2):
                    body(j * 2 + r, r, j)

        @block.sync
        def _(e):
            with e.Fori(1, E // 2) as j:
                for r in range(2):
                    e.wait_ge(k.s_ws, j * 4 + (2 * r - 2))
                    load_expert(e, k, j * 2 + r, r)

        @block.tensor
        def _(e):
            e.wait_ge(k.s_w6, k.n_w6)
            for t in range(TILES):
                for c in range(KD):
                    i = e.matmul(OB[0][:, t * E:(t + 1) * E], k.xT[:, c, t * P:(t + 1) * P], k.wg[:, c, :],
                                 start=c == 0, stop=c == 1)
            i.then_inc(s_g, 1)

            e.transpose(OB[3][:, 0:P], k.ident[:, :], k.ident[:, :]).then_inc(s_o, 1)

            def product(dst, hi, lo, w_hi, w_lo, first, last):
                for i, (a, b) in enumerate(((hi, w_hi), (hi, w_lo), (lo, w_hi))):
                    ins = e.matmul(dst, a, b, start=first and i == 0, stop=last and i == 2)
                return ins

            def hidden(x, r):
                e.wait_ge(k.s_ws, x * 2 + 2)
                for n, (m, h) in enumerate(blocks):
                    e.wait_ge(s_r, x * 4 + (n + 1))
                    cols, tok = slice(m * P, (m + 1) * P), slice(h * HALF, (h + 1) * HALF)
                    for c in range(KD):
                        i = product(HB[n][:, :], k.w_hi[r][:, 0, c, cols], k.w_lo[r][:, 0, c, cols],
                                    k.x_hi[:, c, tok], k.x_lo[:, c, tok], c == 0, c == 1)
                    i.then_inc(s_h, 1)

            def output(x, r):
                for g in range(4):
                    if g % 2 == 0:
                        e.wait_ge(s_r, x * 4 + (4 + 2 * (g // 2) + 2))
                        e.wait_ge(s_l, x * 4 + (4 + 2 * (g // 2) + 2))
                    e.wait_ge(s_a, x * 4 + (g + 1))
                    for u in range(2):
                        tok = slice((2 * g + u) * P, (2 * g + u + 1) * P)
                        for c in range(KD):
                            i = product(OB[g][:, u * D:(u + 1) * D], h_hi[r][:, c, tok], h_lo[r][:, c, tok],
                                        k.w_hi[r][:, 1, c, :], k.w_lo[r][:, 1, c, :], c == 0, c == 1)
                    i.then_inc(s_o, 1)

            def body(x, r, j):
                hidden(x, r)
                if isinstance(x, int) and x == 0:
                    shares()
                output(x, r)

            def shares():
                e.wait_ge(s_t, 7)
                for t in range(TILES):
                    i = e.transpose(OB[1 + t // 4][0:E, (t % 4) * P:(t % 4 + 1) * P], comb[:, t, :], k.ident[:, :])
                i.then_inc(s_g, 1)
                e.wait_ge(s_ct, 2)
                for g in range(4):
                    for u in range(2):
                        t = 2 * g + u
                        i = e.matmul(OB[g][:, u * D:(u + 1) * D], combT[:, t * P:(t + 1) * P], k.b2[:, :],
                                     start=True, stop=True)
                    i.then_inc(s_g, 1)

            per_expert(e, body)

        @block.scalar
        def _(e):
            for n in range(4):
                e.activation(hid[n][:, 0:1], k.ident[:, 0:1], ACT.Copy).then_inc(s_r, 1)
            e.wait_ge(s_r, 4)

            def body(x, r, j):
                e.wait_ge(s_b1, x + 1)
                for n, (m, h) in enumerate(blocks):
                    e.wait_ge(s_h, x * 4 + (n + 1))
                    if n == 0:
                        e.wait_ge(s_o, j * 8 + 1)
                    e.wait_ge(s_l, x * 4 + (n + 1))
                    for dst in (hid[n][:, :], h_hi[r][:, m, h * HALF:(h + 1) * HALF]):
                        i = e.activation(dst, HB[n][:, :], ACT.Relu, bias=b1[r][:, m:m + 1])
                    i.then_inc(s_r, 1)

            def comb_rows():
                e.wait_ge(s_g, 2)
                for n in range(2):
                    e.activation(combT[:, n * HALF:(n + 1) * HALF], OB[1 + n][0:E, :], ACT.Copy).then_inc(s_ct, 1)

            per_expert(e, body, comb_rows)

        @block.gpsimd
        def _(e):
            a0, _ = COLS["b1"]

            def body(x, r, j):
                e.wait_ge(s_r, x * 4 + 1)
                src = slice(x * 2 + a0, x * 2 + a0 + 2) if isinstance(x, int) else bass.ds(x * 2 + a0, 2)
                e.tensor_copy(b1[r][:, :], k.cols[:, src]).then_inc(s_b1, 1)
                if not isinstance(x, int):
                    e.wait_ge(s_o, j * 8 + (4 * r - 3))
                    split_expert(e, k, x, r, j)

            per_expert(e, body)

        @block.vector
        def _(e):
            e.wait_ge(k.s_w6, k.n_w6)
            n = 0

            def chain(ins):
                nonlocal n
                n += 1
                ins.then_inc(s_t, 1)
                e.wait_ge(s_t, n)

            for r in range(2):
                for m in range(2):
                    e.memset(pick[r][:, m, 0:1], 0.0).then_inc(s_l, 1)
            e.wait_ge(s_g, 1)
            e.wait_ge(s_l, 4)
            chain(e.tensor_tensor(score[:, :, :], OB[0][:, 0:TILES * E].rearrange("p (t x) -> p t x", x=E),
                                  k.gateb[:, :].unsqueeze(1).to_broadcast([P, TILES, E]), ALU.add))
            for t in range(TILES):
                i = e.max(top[:, t, :], score[:, t, :])
            chain(i)
            for t in range(TILES):
                i = e.max_index(idx[:, t, :], top[:, t, :], score[:, t, :])
            chain(i)
            chain(e.tensor_copy(idf[:, :, :], idx[:, :, :]))
            for i in range(TOPK):
                ins = e.tensor_tensor(pick[i][:, :, :], k.iota8[:, :].unsqueeze(1).to_broadcast([P, TILES, E]),
                                      idf[:, :, i:i + 1].to_broadcast([P, TILES, E]), ALU.is_equal)
            chain(ins)
            for i in range(TOPK):
                ins = e.tensor_tensor(pick[i][:, :, :], pick[i][:, :, :], top[:, :, i:i + 1].to_broadcast([P, TILES, E]),
                                      ALU.mult)
            chain(ins)
            chain(e.tensor_tensor(comb[:, :, :], pick[0][:, :, :], pick[1][:, :, :], ALU.add))

            def shares():
                for g in range(4):
                    e.wait_ge(s_g, 3 + g)
                    x = k.x[:, 2 * g:2 * g + 2, :].rearrange("p t d -> p (t d)")
                    e.tensor_tensor(x, x, OB[g][:, :], ALU.add).then_inc(s_a, 1)

            def body(x, r, j):
                for n, (m, h) in enumerate(blocks):
                    e.wait_ge(s_r, x * 4 + (n + 5))
                    e.tensor_tensor(h_lo[r][:, m, h * HALF:(h + 1) * HALF], hid[n][:, :],
                                    h_hi[r][:, m, h * HALF:(h + 1) * HALF].bitcast(F32), ALU.subtract
                                    ).then_inc(s_l, 1)
                if isinstance(x, int) and x == 0:
                    shares()
                for g in range(4):
                    e.wait_ge(s_o, x * 4 + (g + 2))
                    e.wait_ge(s_a, x * 4 + (g + 1))
                    for u in range(2):
                        t = 2 * g + u
                        share = comb[:, t, x:x + 1] if isinstance(x, int) else comb[:, t, :][:, bass.ds(x, 1)]
                        i = e.scalar_tensor_tensor(k.x[:, t, :], OB[g][:, u * D:(u + 1) * D], share,
                                                   k.x[:, t, :], ALU.mult, ALU.add)
                    i.then_inc(s_a, 1)

            per_expert(e, body)


def perceiver(nc, t, out):
    with ExitStack() as ctx:
        sb, ps, sem = tools(nc, ctx)
        k = Names()
        k.ctx, k.ctxT = t["ctx"], t["ctxT"]
        k.x = sb("x", [P, TILES, D])
        k.xn = sb("xn", [P, TILES, D])
        k.xT = sb("xT", [P, KD, TOK])
        k.ident = sb("ident", [P, P])
        k.cols = sb("cols", [P, NCOLS])
        k.rows = sb("rows", [P, NROWS, D])
        k.bc_dram = nc.dram_tensor("bc_rows", (2 * DS, TOK), F32, kind="Internal").ap()
        k.trig = sb("trig", [P, 2, DH])
        k.own_head = sb("own_head", [P, HG])
        k.causal = sb("causal", [P, L])
        k.ident_bf = sb("ident_bf", [P, P], BF16)
        k.causal_bf = sb("causal_bf", [P, HG * L], BF16)
        k.same_batch = sb("same_batch", [P, P])
        k.diag64 = sb("diag64", [P, L])
        k.iota8 = sb("iota8", [P, E])
        k.stats = sb("stats", [P, TILES, 6])
        k.wtq = sb("wtq", [P, KD, 2])
        k.wfq = sb("wfq", [2, D])
        k.btq = sb("btq", [P, 2])
        k.wg = sb("wg", [P, KD, E])
        k.gateb = sb("gateb", [P, E])
        k.b2 = sb("b2", [E, D])
        k.s_w5, k.s_w6 = sem("s_w5"), sem("s_w6")
        k.n_w5 = 16 * 7
        k.n_w6 = 16 * 3
        k.s_w3, k.s_w4 = sem("s_w3"), sem("s_w4")
        k.n_w3 = 32
        k.n_w4 = 16 * (5 + KD)
        k.s_w2 = sem("s_w2")
        k.n_w2 = 80 + 1
        k.s_x, k.s_rows, k.s_const, k.s_w0, s_out = (sem(n) for n in ("s_x", "s_rows", "s_const", "s_w0", "s_out"))
        k.n_ident = k.n_const = 8 + 3 + 3 + E
        k.n_w0 = 64

        ctx1 = ctx.enter_context(ExitStack())
        sb1, _, _ = tools(nc, ctx1)
        k.wq0, k.wk0T, k.wv0 = (sb1(n, [P, KD, D]) for n in ("wq0", "wk0T", "wv0"))
        k.cT = [sb1(f"cT{r}", [P, 2, KD, LK]) for r in range(2)]
        k.cN = [sb1(f"cN{r}", [FULL + 1, 2, ROWS, D]) for r in range(2)]
        k.s_dT = [sem(f"a_dT{r}") for r in range(2)]
        k.s_dN = [sem(f"a_dN{r}") for r in range(2)]
        with nc.Block() as block:
            @block.sync
            def _(e):
                e.dma_start(k.x[:, :, :], t["x"].rearrange("b l d -> (b l) d").rearrange("(t p) d -> p t d", p=P)
                            ).then_inc(k.s_x, 16)
                e.dma_start(k.cols[:, :], t["cols"]).then_inc(k.s_w0, 16)
                for n, w in (("wq0", k.wq0), ("wk0T", k.wk0T), ("wv0", k.wv0)):
                    e.dma_start(w[:, :, :], t[n].rearrange("(c p) n -> p c n", p=P)).then_inc(k.s_w0, 16)
                e.dma_start(k.rows[:, :, :].rearrange("p r d -> p (r d)"),
                            t["rows"].rearrange("r d -> (r d)").unsqueeze(0).to_broadcast([P, NROWS * D])
                            ).then_inc(k.s_rows, 16)
                load_columns(e, k, 0, 0)
                load_rows(e, k, 0, 0)
                load_columns(e, k, 1, 1)
                load_rows(e, k, 1, 1)
                e.dma_start(k.trig[:, :, :], t["trig"]).then_inc(k.s_w4, 16)
                e.dma_start(k.wtq[:, :, :], t["wtq"].rearrange("(c p) n -> p c n", p=P)).then_inc(k.s_w5, 16)
                e.dma_start(k.wfq[:, :], t["wfq"]).then_inc(k.s_w5, 16)
                e.dma_start(k.btq[:, :], t["btq"].unsqueeze(0).to_broadcast([P, 2])).then_inc(k.s_w5, 16)
                e.dma_start(k.wg[:, :, :], t["wg"].rearrange("(c p) n -> p c n", p=P)).then_inc(k.s_w6, 16)
                e.dma_start(k.gateb[:, :], t["gateb"].unsqueeze(0).to_broadcast([P, E])).then_inc(k.s_w6, 16)
                e.dma_start(k.b2[:, :], t["b2"]).then_inc(k.s_w6, 16)

            @block.vector
            def _(e):
                e.wait_ge(k.s_const, k.n_const)
                e.tensor_copy(k.ident_bf[:, :], k.ident[:, :])
                e.tensor_scalar(k.causal_bf[:, :].rearrange("p (h n) -> p h n", n=L),
                                k.causal[:, :].unsqueeze(1).to_broadcast([P, HG, L]), -NEG, NEG,
                                ALU.mult, ALU.add)

            @block.gpsimd
            def _(e):
                n = 0

                def chain(ins):
                    nonlocal n
                    n += 1
                    ins.then_inc(k.s_const, 1)
                    e.wait_ge(k.s_const, n)

                def keep(m, op, fill, base, pattern, mult):
                    chain(e.affine_select(out=m, in_=m, compare_op=op, fill=fill, base=base,
                                          pattern=pattern, channel_multiplier=mult))

                chain(e.memset(k.ident[:, :], 0.0))
                keep(k.ident[:, :], ALU.not_equal, 1.0, 0, [[-1, P]], 1)
                chain(e.memset(k.causal[:, :], 1.0))
                for b in range(2):
                    keep(k.causal[64 * b:64 * b + 64, :], ALU.is_ge, 0.0, 0, [[-1, L]], 1)
                chain(e.memset(k.own_head[:, :], 1.0))
                keep(k.own_head[:, :], ALU.is_ge, 0.0, 0, [[-DH, HG]], 1)
                keep(k.own_head[:, :], ALU.is_ge, 0.0, DH - 1, [[DH, HG]], -1)
                chain(e.memset(k.diag64[:, :], 0.0))
                for b in range(2):
                    keep(k.diag64[64 * b:64 * b + 64, :], ALU.not_equal, 1.0, 0, [[-1, L]], 1)
                chain(e.memset(k.same_batch[:, :], 0.0))
                for b in range(2):
                    chain(e.memset(k.same_batch[64 * b:64 * b + 64, 64 * b:64 * b + 64], 1.0))
                for i in range(E):
                    chain(e.memset(k.iota8[:, i:i + 1], float(i)))

        layer_norm(nc, k, "ln0")
        cross_attention(nc, k)
        ctx1.close()
        ctx4, ctx3, ctx2 = (ctx.enter_context(ExitStack()) for _ in range(3))
        sb4, sb3, sb2 = (tools(nc, c)[0] for c in (ctx4, ctx3, ctx2))
        k.w5 = [sb4(f"w5{i}", [P, KD, D]) for i in range(4)]
        k.w4 = [sb4(f"w4{i}", [P, KD, D]) for i in range(4)]
        k.c0T = sb4("c0T", [P, KD, TOK])
        k.w_fc = sb3("w_fc", [P, KD, FF])
        k.w_pr = sb3("w_pr", [P, FM, D])
        k.w_in = sb2("w_in", [P, KD, 2 * DI])
        k.w_xp = sb2("w_xp", [P, CH, 64])
        k.w_dt = sb2("w_dt", [DTR, DI])
        k.w_out = sb2("w_out", [P, CH, D])

        def late_weights(block):
            @block.gpsimd
            def _(e):
                e.memset(k.w_xp[:, :, DTR:32], 0.0).then_inc(k.s_w2, 1)

            @block.sync
            def _(e):
                e.dma_start(k.w_in[:, :, :], t["w_in"].rearrange("(c p) n -> p c n", p=P)).then_inc(k.s_w2, 16)
                e.dma_start(k.w_xp[:, :, 0:DTR], t["w_xp"][:, 0:DTR].rearrange("(c p) n -> p c n", p=P)
                            ).then_inc(k.s_w2, 16)
                e.dma_start(k.w_xp[:, :, 32:64], t["w_xp"][:, DTR:DTR + 2 * DS].rearrange("(c p) n -> p c n", p=P)
                            ).then_inc(k.s_w2, 16)
                e.dma_start(k.w_dt[:, :], t["w_dt"]).then_inc(k.s_w2, 16)
                e.dma_start(k.w_out[:, :, :], t["w_out"].rearrange("(c p) n -> p c n", p=P)).then_inc(k.s_w2, 16)
                e.dma_start(k.w_fc[:, :, :], t["w_fc"].rearrange("(c p) n -> p c n", p=P)).then_inc(k.s_w3, 16)
                e.dma_start(k.w_pr[:, :, :], t["w_pr"].rearrange("(c p) n -> p c n", p=P)).then_inc(k.s_w3, 16)
                for i in range(4):
                    e.dma_start(k.w4[i][:, :, :], t[f"w4{i}"].rearrange("(c p) n -> p c n", p=P)).then_inc(k.s_w4, 16)
                for i in range(4):
                    e.dma_start(k.w5[i][:, :, :], t[f"w5{i}"].rearrange("(c p) n -> p c n", p=P)).then_inc(k.s_w5, 16)
                for c in range(KD):
                    e.dma_start(k.c0T[:, c, :].rearrange("p (b n) -> p b n", n=L),
                                t["ctxT"][:, c * P:(c + 1) * P, 0:L].rearrange("b p n -> p b n")).then_inc(k.s_w4, 16)

        layer_norm(nc, k, "ln1", late_weights)
        with ExitStack() as mctx:
            sb, _, _ = tools(nc, mctx)
            m = Names()
            m.bc_dram = k.bc_dram
            m.u, m.sres, m.delta, m.du = (sb(n, [P, CH, TOK]) for n in ("u", "sres", "delta", "du"))
            m.diagD = sb("diagD", [P, CH, P])
            m.negA = sb("negA", [P, CH, DS])
            m.Bb = [sb("Bb0", [P, TOK])[:, :], k.w_in[:, 0, :]]
            m.Cb = [sb(f"Cb{i}", [P, TOK])[:, :] for i in range(2)]
            m.s_bl = [sem(f"n_bl{i}") for i in range(2)]
            m.s_cl = [sem(f"n_cl{i}") for i in range(2)]
            mamba_front(nc, k, m)
            mamba_scan(nc, k, m)
        ctx2.close()
        layer_norm(nc, k, "ln2")
        spiking_ffn(nc, k)
        ctx3.close()
        layer_norm(nc, k, "ln3")
        windowed_attention(nc, k)
        layer_norm(nc, k, "ln4")
        with ExitStack() as ectx:
            sb, _, _ = tools(nc, ectx)
            k.w_experts = (t["w1"], t["w2"])
            k.w6 = [sb(f"w6{r}", [P, 2, KD, D]) for r in range(2)]
            k.w_hi = [sb(f"w_hi{r}", [P, 2, KD, D], F32R) for r in range(2)]
            k.w_lo = [sb(f"w_lo{r}", [P, 2, KD, D], F32R) for r in range(2)]
            k.x_hi, k.x_lo = (sb(n, [P, KD, TOK], F32R) for n in ("x_hi", "x_lo"))
            k.one = sb("one", [P, 1])
            k.s_w = [sem(f"e_w{i}") for i in range(2)]
            k.s_hi = sem("e_hi")
            k.s_ws = sem("e_ws")
            phase_attention(nc, k)
            layer_norm(nc, k, "ln5", split=(k.x_hi, k.x_lo))
            experts(nc, k)

        with nc.Block() as block:
            @block.sync
            def _(e):
                e.dma_start(out.rearrange("b l d -> (b l) d").rearrange("(t p) d -> p t d", p=P), k.x[:, :, :]
                            ).then_inc(s_out, 16)
                e.wait_ge(s_out, 16)




def rotary():
    half = DH // 2
    inv = (1.0 / 10000.0 ** (np.arange(half, dtype=np.float32) / half)).astype(np.float32)
    ang = np.arange(L, dtype=np.float32)[:, None] * inv[None, :]
    cos, sin = np.cos(ang), np.sin(ang)
    table = np.stack([np.concatenate([cos, cos], 1), np.concatenate([-sin, sin], 1)], 1)
    return np.concatenate([table, table], 0).astype(np.float32)


def layout(inputs):
    a = {n: np.asarray(v) for n, v in inputs.items()}
    T = np.transpose
    cols = [T(a["L0_xattn_bq"].reshape(2, P)), T(a["L0_xattn_bk"].reshape(2, P)),
            T(a["L0_attn_in_proj_b"].reshape(8, P)),
            T(a["L0_attn_conv_w"].reshape(4, P, 4), (1, 0, 2)).reshape(P, 16),
            T(a["L0_attn_conv_b"].reshape(4, P)), T(a["L0_attn_dt_proj_b"].reshape(4, P)),
            T(a["L0_attn_D_param"].reshape(4, P)),
            T(a["L0_attn_A_log"].reshape(4, P, 16), (1, 0, 2)).reshape(P, 64),
            T(a["L1_attn_bq"].reshape(2, P)), T(a["L1_attn_bk"].reshape(2, P)),
            T(a["L1_ffn_b1"].reshape(16, P))]
    rows = [a[n] for n in ("L0_xattn_bv", "L0_attn_out_proj_b", "L1_xattn_bq", "L1_xattn_bk", "L1_xattn_bv",
                           "L1_xattn_bo", "L1_attn_bv", "L1_attn_bo", "L1_attn_bfq")]
    return {
        "x": a["x"], "ctx": a["ctx_1024"], "ctxT": T(a["ctx_1024"], (0, 2, 1)),
        "cols": np.concatenate(cols, axis=1), "rows": np.stack(rows),
        "w_in": T(a["L0_attn_in_proj_w"]), "w_xp": T(a["L0_attn_x_proj_w"]),
        "w_dt": T(a["L0_attn_dt_proj_w"]), "w_out": T(a["L0_attn_out_proj_w"]),
        "w_fc": T(a["L0_ffn_W_fc"]), "w_pr": T(a["L0_ffn_W_proj"]),
        **{f"w4{i}": T(a[f"L1_xattn_W{c}"]) for i, c in enumerate("qkvo")}, "trig": rotary(),
        **{f"w5{i}": T(a[f"L1_attn_W{c}"]) for i, c in enumerate("qkvo")},
        "wtq": T(a["L1_attn_Wtq"]), "wfq": T(a["L1_attn_Wfq"]), "btq": a["L1_attn_btq"],
        "wg": a["L1_ffn_gate_w"], "gateb": a["L1_ffn_gate_b"], "b2": a["L1_ffn_b2"],
        "w1": a["L1_ffn_w1"], "w2": a["L1_ffn_w2"],
        "wq0": a["L0_xattn_Wq"], "wk0T": T(a["L0_xattn_Wk"]), "wv0": a["L0_xattn_Wv"],
    }


def kernel(**inputs):
    import concourse.bacc as _bacc
    from concourse.bass_utils import run_bass_kernel_spmd as _run

    nc = _bacc.Bacc("TRN2", target_bir_lowering=False, num_devices=1)
    arrays, args = {}, {}
    for name, v in layout(inputs).items():
        v = np.ascontiguousarray(v)
        arrays[f"in_{name}"] = v
        args[name] = nc.dram_tensor(f"in_{name}", v.shape, mybir.dt.from_np(v.dtype), kind="ExternalInput").ap()
    out = nc.dram_tensor("out_dram", (B, L, D), F32, kind="ExternalOutput").ap()
    perceiver(nc, args, out)
    r = _run(nc, [arrays], core_ids=[0])
    return r.results[0]["out_dram"]
```

```python
from contextlib import ExitStack

import numpy as np
import concourse.bass as bass
from concourse import mybir

F32 = mybir.dt.float32
F32R = mybir.dt.float32r
U32 = mybir.dt.uint32
ALU = mybir.AluOpType
ACT = mybir.ActivationFunctionType
AX = mybir.AxisListType

P = 128
B, L, D = 16, 64, 256
LK = 1601
TOK = B * L
TILES = TOK // P
KD = D // P
HALF = 512
EPS = 1e-5
NEG = -3.0e38

ROWS = 13
FULL = LK // ROWS
LAST = LK - FULL * ROWS
SC_W = [min(HALF, LK - c * HALF) for c in range(4)]

DI, DS, DTR, KC = 512, 16, 16, 4
CH = DI // P
FF = 1024
FM = FF // P
H, DH = 16, 16
HG = P // DH
DV = DH + 1
E, TOPK = 8, 2

COLS = {}
_n = 0
for _name, _w in (("bq0", 2), ("bk0", 2), ("inb", 8), ("convw", 16), ("convb", 4), ("dtb", 4),
                  ("dpar", 4), ("alog", 64), ("bq5", 2), ("bk5", 2), ("b1", 16)):
    COLS[_name] = (_n, _w)
    _n += _w
NCOLS = _n
ROWV = {n: i for i, n in enumerate(("bv0", "outb", "bq4", "bk4", "bv4", "bo4", "bv5", "bo5", "bfq"))}
NROWS = len(ROWV)


class Names:
    pass


def tools(nc, ctx):
    def sb(name, shape, dt=F32):
        return ctx.enter_context(nc.sbuf_tensor(name, shape, dt))

    def ps(name, shape=(P, HALF), dt=F32):
        return ctx.enter_context(nc.psum_tensor(name, list(shape), dt))

    def sem(name):
        return ctx.enter_context(nc.semaphore(name))

    return sb, ps, sem


def col(k, name, i=0):
    a, _ = COLS[name]
    return k.cols[:, a + i:a + i + 1]


def rowvec(k, name):
    return k.rows[:, ROWV[name], :]


def layer_norm(nc, k, tag, loads=None, split=None):
    with ExitStack() as ctx:
        sb, ps, sem = tools(nc, ctx)
        mv = sb(f"{tag}_mv", [P, TILES, 2])
        veps = sb(f"{tag}_veps", [P, TILES])
        sd = sb(f"{tag}_sd", [P, TILES])
        rstd = sb(f"{tag}_rstd", [P, TILES])
        tp = [ps(f"{tag}_tp{i}") for i in range(4)]
        s_dve = sem(f"{tag}_dve")
        s_sd = sem(f"{tag}_sd_ready")
        s_xn = sem(f"{tag}_xn")
        s_tp = sem(f"{tag}_tp_done")
        s_ev = sem(f"{tag}_ev")
        block = ctx.enter_context(nc.Block())
        if loads:
            loads(block)

        @block.vector
        def _(e):
            if tag == "ln0":
                e.wait_ge(k.s_x, 16)
            if tag == "ln0":
                for t in range(TILES):
                    i = e.bn_stats(k.stats[:, t, :], k.x[:, t, :])
                i.then_inc(s_dve, 1)
                e.wait_ge(s_dve, 1)
            base = 1 if tag == "ln0" else 0
            for t in range(TILES):
                i = e.bn_aggr(mv[:, t, :], k.stats[:, t, :])
            i.then_inc(s_dve, 1)
            e.wait_ge(s_dve, base + 1)
            e.tensor_scalar(veps[:, :], mv[:, :, 1], EPS, None, ALU.add).then_inc(s_dve, 1)
            e.wait_ge(s_sd, 1)
            e.reciprocal(rstd[:, :], sd[:, :]).then_inc(s_dve, 1)
            e.wait_ge(s_dve, base + 3)
            for t in range(TILES):
                e.tensor_scalar(k.xn[:, t, :], k.x[:, t, :], mv[:, t, 0:1], rstd[:, t:t + 1],
                                ALU.subtract, ALU.mult).then_inc(s_xn, 1)
            if split:
                for t in range(TILES):
                    tok = slice(t * P, (t + 1) * P)
                    e.wait_ge(s_ev, t + 1)
                    e.tensor_tensor(split[1][:, :, tok], k.xT[:, :, tok], split[0][:, :, tok].bitcast(F32),
                                    ALU.subtract)

        @block.scalar
        def _(e):
            e.wait_ge(s_dve, 3 if tag == "ln0" else 2)
            e.activation(sd[:, :], veps[:, :], ACT.Sqrt).then_inc(s_sd, 1)
            for t in range(TILES):
                e.wait_ge(s_tp, t + 1)
                if split:
                    e.activation(split[0][:, :, t * P:(t + 1) * P],
                                 tp[t % 4][:, 0:D].rearrange("p (c n) -> p c n", c=KD), ACT.Copy)
                e.activation(k.xT[:, :, t * P:(t + 1) * P],
                             tp[t % 4][:, 0:D].rearrange("p (c n) -> p c n", c=KD), ACT.Copy
                             ).then_inc(s_ev, 1)

        @block.tensor
        def _(e):
            if tag == "ln0":
                e.wait_ge(k.s_const, k.n_ident)
            for t in range(TILES):
                e.wait_ge(s_xn, t + 1)
                if t >= 4:
                    e.wait_ge(s_ev, t - 3)
                for c in range(KD):
                    i = e.transpose(tp[t % 4][:, c * P:(c + 1) * P], k.xn[:, t, c * P:(c + 1) * P],
                                    k.ident[:, :])
                i.then_inc(s_tp, 1)


def tile_stats(e, k, t):
    pick = (lambda a: a[:, t, :]) if isinstance(t, int) else (lambda a: a[:, bass.ds(t, 1), :].squeeze(1))
    return e.bn_stats(pick(k.stats), pick(k.x))


def load_columns(e, k, i, r):
    src = k.ctxT[2 * i:2 * i + 2] if isinstance(i, int) else k.ctxT[bass.ds(i * 2, 2), :, :]
    e.dma_start(k.cT[r][:, :, :, :], src.rearrange("b (c p) n -> p b c n", p=P)).then_inc(k.s_dT[r], 16)


def load_rows(e, k, i, r):
    src = k.ctx[2 * i:2 * i + 2] if isinstance(i, int) else k.ctx[bass.ds(i * 2, 2), :, :]
    e.dma_start(k.cN[r][0:FULL, :, :, :],
                src[:, 0:FULL * ROWS, :].rearrange("b (p c) d -> p b c d", c=ROWS)).then_inc(k.s_dN[r], 16)
    e.dma_start(k.cN[r][FULL:FULL + 1, :, 0:LAST, :],
                src[:, FULL * ROWS:LK, :].rearrange("b (p c) d -> p b c d", p=1)).then_inc(k.s_dN[r], 16)


def cross_attention(nc, k):
    scale = 1.0 / float(D) ** 0.5
    with ExitStack() as ctx:
        sb, ps, sem = tools(nc, ctx)
        qT = sb("qT", [P, KD, TOK])
        qkT = sb("qkT", [P, KD, TOK + P])
        qbk = sb("qbk", [P, TILES])
        qs = [sb(f"qs{r}", [P, KD, P]) for r in range(2)]
        cT, cN, s_dT, s_dN = k.cT, k.cN, k.s_dT, k.s_dN
        prob = [sb(f"prob{r}", [P, LK]) for r in range(2)]
        pT = sb("pT", [P, ROWS, P])
        mx = sb("mx", [P, 1])
        full_max = sb("full_max", [P, 1])
        nbias = sb("nbias", [P, 1])
        total = [sb(f"total{r}", [P, 1]) for r in range(2)]
        rinv = sb("rinv", [P, 1])
        on = [sb(f"on{r}", [P, D]) for r in range(2)]
        onT = sb("onT", [P, KD, P])
        S = ps("S", [P, 4 * HALF])
        tps = [ps(f"ptp{i}") for i in range(2)]
        O = ps("O")
        X = ps("X")
        s_pp = sem("a_pp")
        s_pe = sem("a_pe")
        s_qb = sem("a_qb")
        s_q0 = sem("a_q0")
        s_qs = sem("a_qs")
        s_sc = sem("a_sc")
        s_m1 = sem("a_m1")
        s_mx = sem("a_mx")
        s_ex = sem("a_ex")
        s_tp = sem("a_tp")
        s_te = sem("a_te")
        s_pv = sem("a_pv")
        s_ri = sem("a_ri")
        s_on = sem("a_on")
        s_ot = sem("a_ot")
        s_oe = sem("a_oe")
        s_wv = sem("a_wv")
        s_xa = sem("a_xa")
        block = ctx.enter_context(nc.Block())
        groups = [range(0, 4), range(4, 8), range(8, 12), range(12, 13)]

        pblocks = [(part, m, h) for h in range(2) for part in range(2) for m in range(KD)]

        def pipeline(e, sub, second_half):
            for i in range(2):
                sub(i, i % 2, lambda d, i=i: i - d >= 0)
                if i == 0:
                    second_half()
            with e.Fori(1, TILES // 2) as j:
                sub(j * 2, 0, lambda d: True)
                sub(j * 2 + 1, 1, lambda d: True)
            for i in range(TILES, TILES + 2):
                sub(i, i % 2, lambda d, i=i: i - d < TILES)

        @block.sync
        def _(e):
            e.wait_ge(s_sc, 1)
            load_columns(e, k, 2, 0)
            e.wait_ge(s_sc, 2)
            load_columns(e, k, 3, 1)
            e.wait_ge(s_pv, 1)
            load_rows(e, k, 2, 0)
            with e.Fori(2, TILES // 2) as j:
                for r in range(2):
                    e.wait_ge(s_sc, j * 2 + (r - 1))
                    load_columns(e, k, j * 2 + r, r)
                    e.wait_ge(s_pv, j * 2 + (r - 2))
                    load_rows(e, k, j * 2 + (r - 1), 1 - r)
            e.wait_ge(s_pv, TILES - 2)
            load_rows(e, k, TILES - 1, 1)

        @block.tensor
        def _(e):
            e.wait_ge(k.s_w0, k.n_w0)

            def project(half):
                for n in range(4 * half, 4 * half + 4):
                    part, m, h = pblocks[n]
                    if n >= 2:
                        e.wait_ge(s_pe, n if n % 4 == 2 else n - 1)
                    w, src = ((k.wq0, k.xT), (k.wk0T, qT))[part]
                    for c in range(KD):
                        i = e.matmul(tps[n % 2][:, :], w[:, c, m * P:(m + 1) * P],
                                     src[:, c, h * HALF:(h + 1) * HALF], start=c == 0, stop=c == 1)
                    i.then_inc(s_pp, 1)
                if half:
                    e.wait_ge(s_q0, 1)
                for t in range(4 * half, 4 * half + 4):
                    for c in range(KD):
                        i = e.matmul(X[:, t:t + 1], qT[:, c, t * P:(t + 1) * P], col(k, "bk0", c),
                                     start=c == 0, stop=c == 1)
                i.then_inc(s_qb, 1)

            def second_half():
                project(1)
                e.wait_ge(s_q0, 2)
                e.wait_ge(s_pe, 8)

            project(0)

            def turn(i, q, g):
                if g >= 2:
                    e.wait_ge(s_te, (i - 1) * 4 + g - 1)
                for c in groups[g]:
                    kc = FULL + (c < LAST)
                    j = e.transpose(tps[g % 2][0:kc, (c % 4) * P:(c % 4 + 1) * P],
                                    prob[q][:, c:c + (kc - 1) * ROWS + 1:ROWS], k.ident[:, :])
                j.then_inc(s_tp, 1)

            def sub(i, r, live):
                if live(1):
                    e.wait_ge(s_ex, i)
                    for g in range(2):
                        turn(i, 1 - r, g)
                if live(2):
                    e.wait_ge(s_on, i - 1)
                    for c in range(KD):
                        j = e.transpose(X[:, c * P:(c + 1) * P], on[r][:, c * P:(c + 1) * P], k.ident[:, :])
                    j.then_inc(s_ot, 1)
                if live(0):
                    e.wait_ge(s_qs, i + 1)
                    e.wait_ge(s_dT[r], 16 * (i // 2 + 1) if isinstance(i, int) else (i - r) * 8 + 16)
                    e.wait_ge(s_ex, i)
                    for c, w in enumerate(SC_W):
                        for kt in range(KD):
                            for b in range(2):
                                j = e.matmul(S[64 * b:64 * b + 64, c * HALF:c * HALF + w],
                                             qs[r][:, kt, 64 * b:64 * b + 64],
                                             cT[r][:, b, kt, c * HALF:c * HALF + w],
                                             start=kt == 0, stop=kt == 1)
                    j.then_inc(s_sc, 1)
                if live(2):
                    e.wait_ge(s_oe, i - 1)
                    for c in range(KD):
                        j = e.matmul(X[:, D:2 * D], onT[:, c, :], k.wv0[:, c, :], start=c == 0, stop=c == 1)
                    j.then_inc(s_wv, 1)
                if live(1):
                    q = 1 - r
                    e.wait_ge(s_dN[q], 32 * ((i - 1) // 2 + 1) if isinstance(i, int) else (i - 1 - q) * 16 + 32)

                    def pv(g):
                        e.wait_ge(s_te, (i - 1) * 4 + g + 1)
                        if g == 0:
                            e.wait_ge(s_on, i - 1)
                        for c in groups[g]:
                            kc = FULL + (c < LAST)
                            for b in range(2):
                                j = e.matmul(O[64 * b:64 * b + 64, 0:D], pT[0:kc, c, 64 * b:64 * b + 64],
                                             cN[q][0:kc, b, c, :], start=c == 0, stop=c == ROWS - 1)
                        return j

                    for g in range(2):
                        pv(g)
                        turn(i, q, g + 2)
                    pv(2)
                    pv(3).then_inc(s_pv, 1)

            pipeline(e, sub, second_half)

        @block.scalar
        def _(e):
            def move(half):
                for n in range(4 * half, 4 * half + 4):
                    part, m, h = pblocks[n]
                    e.wait_ge(s_pp, n + 1)
                    if part == 0:
                        e.activation(qT[:, m, h * HALF:(h + 1) * HALF], tps[n % 2][:, :], ACT.Identity,
                                     bias=col(k, "bq0", m)).then_inc(s_pe, 1)
                    else:
                        e.activation(qkT[:, m, h * HALF:(h + 1) * HALF], tps[n % 2][:, :], ACT.Copy
                                     ).then_inc(s_pe, 1)

            second_half = lambda: move(1)
            move(0)

            def sub(i, r, live):
                if live(2):
                    e.wait_ge(s_ot, i - 1)
                    if not isinstance(i, int) or i > 2:
                        e.wait_ge(s_wv, i - 2)
                    e.activation(onT[:, :, :], X[:, 0:D].rearrange("p (c n) -> p c n", c=KD), ACT.Copy
                                 ).then_inc(s_oe, 1)
                if live(0):
                    if not isinstance(i, int) or i >= 2:
                        e.wait_ge(s_tp, (i - 1) * 4)
                    e.wait_ge(s_mx, i + 1)
                    e.activation(prob[r][:, :], S[:, 0:LK], ACT.Exp, bias=nbias[:, :], scale=scale,
                                 accum_out=total[r][:, :]).then_inc(s_ex, 1)

            pipeline(e, sub, second_half)

        @block.vector
        def _(e):
            e.wait_ge(k.s_rows, 16)
            e.tensor_tensor(k.x[:, :, :], k.x[:, :, :],
                            rowvec(k, "bv0").unsqueeze(1).to_broadcast([P, TILES, D]), ALU.add)
            e.memset(qkT[:, :, TOK:TOK + P], 0.0)

            def scale_qbk(half):
                at = slice(4 * half, 4 * half + 4)
                e.wait_ge(s_qb, half + 1)
                e.tensor_scalar(qbk[:, at], X[:, at], scale, None, ALU.mult).then_inc(s_q0, 1)
                e.wait_ge(s_pe, 4 * (half + 1))
                e.wait_ge(s_q0, half + 1)

            second_half = lambda: scale_qbk(1)
            scale_qbk(0)

            def queries(i, r):
                src = qkT[:, :, i * P:(i + 1) * P] if isinstance(i, int) else qkT[:, :, bass.ds(i * P, P)]
                e.tensor_copy(qs[r][:, :, :], src).then_inc(s_qs, 1)

            queries(0, 0)

            def evacuate(i, g):
                e.wait_ge(s_tp, (i - 1) * 4 + g + 1)
                if g == 0:
                    e.wait_ge(s_pv, i - 1)
                n, c0 = len(groups[g]), groups[g][0]
                if c0 < LAST:
                    e.tensor_copy(pT[0:FULL + 1, 0:LAST, :],
                                  tps[0][0:FULL + 1, 0:LAST * P].rearrange("p (c n) -> p c n", n=P))
                    e.tensor_copy(pT[0:FULL, LAST:4, :],
                                  tps[0][0:FULL, LAST * P:4 * P].rearrange("p (c n) -> p c n", n=P)
                                  ).then_inc(s_te, 1)
                else:
                    e.tensor_copy(pT[0:FULL, c0:c0 + n, :],
                                  tps[g % 2][0:FULL, 0:n * P].rearrange("p (c n) -> p c n", n=P)
                                  ).then_inc(s_te, 1)

            def sub(i, r, live):
                if live(1):
                    for g in range(2):
                        evacuate(i, g)
                one = (lambda a, n: a[:, n:n + 1] if isinstance(n, int) else a[:, bass.ds(n, 1)])
                if live(0):
                    e.wait_ge(s_sc, i + 1)
                    e.reduce_max(mx[:, :], S[:, 0:LK], AX.X).then_inc(s_m1, 1)
                    e.wait_ge(s_m1, i * 2 + 1)
                    e.tensor_scalar(full_max[:, :], mx[:, :], scale, one(qbk, i), ALU.mult, ALU.add
                                    ).then_inc(s_m1, 1)
                    e.wait_ge(s_m1, i * 2 + 2)
                    e.wait_ge(s_ex, i)
                    e.tensor_scalar(nbias[:, :], full_max[:, :], -1.0, one(qbk, i), ALU.mult, ALU.add
                                    ).then_inc(s_mx, 1)
                    queries(i + 1, 1 - r)
                if live(2):
                    e.wait_ge(s_wv, i - 1)
                    dst = k.x[:, i - 2, :] if isinstance(i, int) else k.x[:, bass.ds(i - 2, 1), :].squeeze(1)
                    e.tensor_tensor(dst, dst, X[:, D:2 * D], ALU.add).then_inc(s_xa, 1)
                if live(1):
                    q = 1 - r
                    for g in (2, 3):
                        evacuate(i, g)
                if live(2):
                    e.wait_ge(s_xa, i - 1)
                    tile_stats(e, k, i - 2)
                if live(1):
                    e.reciprocal(rinv[:, :], total[q][:, :]).then_inc(s_ri, 1)
                    e.wait_ge(s_ri, i)
                    e.wait_ge(s_pv, i)
                    e.tensor_scalar(on[q][:, :], O[:, 0:D], rinv[:, :], None, ALU.mult).then_inc(s_on, 1)

            pipeline(e, sub, second_half)


def mamba_front(nc, k, m):
    with ExitStack() as ctx:
        sb, ps, sem = tools(nc, ctx)
        BH = HALF // L
        xpad = [sb(f"xpad{r}", [P, BH, L + KC - 1]) for r in range(2)]
        acc = [sb(f"acc{r}", [P, BH, L]) for r in range(2)]
        expA = sb("expA", [P, CH * DS])
        dtr = sb("dtr", [DTR, TOK])
        bc = sb("bc", [64, TOK])
        zp = [ps(f"zp{i}") for i in range(4)]
        xq = [ps(f"xq{i}") for i in range(2)]
        dq = [ps(f"dq{i}") for i in range(2)]
        s_in = sem("m_in")
        s_xp = sem("m_xp")
        s_pad = sem("m_pad")
        s_cv = sem("m_cv")
        s_u = sem("m_u")
        s_rs = sem("m_rs")
        s_xj = sem("m_xj")
        s_xe = sem("m_xe")
        s_dt = sem("m_dt")
        s_az = sem("m_az")
        s_ez = sem("m_ez")
        s_lz = sem("m_lz")
        s_rz = sem("m_rz")
        s_dl = sem("m_dl")
        s_bc = sem("m_bc")
        s_a = sem("m_a")
        block = ctx.enter_context(nc.Block())
        xblocks = [(c, h) for h in range(2) for c in range(CH)]

        @block.tensor
        def _(e):
            e.wait_ge(k.s_w2, k.n_w2)
            def project(n):
                if n >= 4:
                    e.wait_ge(s_xp, min(n - 3, 8))
                    if n - 3 > 8:
                        e.wait_ge(s_rs, n - 3 - 8)
                c, h = xblocks[n % 8]
                for kt in range(KD):
                    i = e.matmul(zp[n % 4][:, :], k.w_in[:, kt, (n // 8 * CH + c) * P:(n // 8 * CH + c + 1) * P],
                                 k.xT[:, kt, h * HALF:(h + 1) * HALF], start=kt == 0, stop=kt == 1)
                i.then_inc(s_in, 1)

            def x_proj(h):
                e.wait_ge(s_u, CH * (h + 1))
                for c in range(CH):
                    i = e.matmul(xq[h][0:64, :], k.w_xp[:, c, :], m.u[:, c, h * HALF:(h + 1) * HALF],
                                 start=c == 0, stop=c == CH - 1)
                i.then_inc(s_xj, 1)

            def dt_proj(n):
                h, c = n // CH, n % CH
                e.wait_ge(s_xe, h + 1)
                if n >= 2:
                    e.wait_ge(s_az, n - 1)
                    e.wait_ge(s_rz, n - 1)
                e.matmul(dq[n % 2][:, :], k.w_dt[:, c * P:(c + 1) * P], dtr[:, h * HALF:(h + 1) * HALF],
                         start=True, stop=True).then_inc(s_dt, 1)

            for n in range(8):
                project(n)
            for step, n in ((x_proj, 0), (project, 8), (project, 9), (dt_proj, 0), (dt_proj, 1), (project, 10),
                            (project, 11), (dt_proj, 2), (dt_proj, 3), (x_proj, 1), (project, 12), (project, 13),
                            (dt_proj, 4), (dt_proj, 5), (dt_proj, 6), (dt_proj, 7), (project, 14), (project, 15)):
                step(n)

        @block.scalar
        def _(e):
            def gate(n):
                c, h = xblocks[n]
                e.wait_ge(s_in, 8 + n + 1)
                e.activation(m.sres[:, c, h * HALF:(h + 1) * HALF], zp[n % 4][:, :], ACT.Silu,
                             bias=col(k, "inb", CH + c)).then_inc(s_rs, 1)

            def silu_u(n):
                c, h = xblocks[n]
                e.wait_ge(s_cv, 4 * n + 4)
                e.activation(m.u[:, c, h * HALF:(h + 1) * HALF].rearrange("p (b l) -> p b l", l=L),
                             acc[n % 2][:, :, :], ACT.Silu).then_inc(s_u, 1)

            e.wait_ge(s_pad, 1)
            for n, (c, h) in enumerate(xblocks):
                e.wait_ge(s_in, n + 1)
                if n >= 2:
                    e.wait_ge(s_cv, 4 * (n - 2) + 4)
                e.activation(xpad[n % 2][:, :, KC - 1:], zp[n % 4][:, :].rearrange("p (b l) -> p b l", l=L),
                             ACT.Identity, bias=col(k, "inb", c)).then_inc(s_xp, 1)
                if n >= 1:
                    silu_u(n - 1)

            halves = [m.delta[:, :, h * HALF:(h + 1) * HALF] for h in range(2)]

            def absolute(n):
                e.wait_ge(s_dt, n + 1)
                e.activation(halves[n // CH][:, n % CH, :], dq[n % 2][:, :], ACT.Abs, bias=col(k, "dtb", n % CH)
                             ).then_inc(s_az, 1)

            for step, n in ((absolute, 0), (absolute, 1), (silu_u, 7), (gate, 0), (gate, 1), (absolute, 2),
                            (absolute, 3), (gate, 2), (gate, 3), (gate, 4), (gate, 5), (absolute, 4), (absolute, 5),
                            (absolute, 6), (absolute, 7)):
                step(n)
            e.wait_ge(s_az, 2 * CH)
            e.activation(m.delta[:, :, :], m.delta[:, :, :], ACT.Exp, scale=-1.0).then_inc(s_ez, 1)
            a0, aw = COLS["alog"]
            e.activation(expA[:, :], k.cols[:, a0:a0 + aw], ACT.Exp).then_inc(s_a, 1)
            e.wait_ge(s_ez, 1)
            for h in range(2):
                e.activation(halves[h], halves[h], ACT.Ln, bias=1.0).then_inc(s_lz, 1)
            e.wait_ge(s_a, 1)
            e.mul(m.negA[:, :, :].rearrange("p c n -> p (c n)"), expA[:, :], -1.0)
            for n in range(6, 8):
                gate(n)

        @block.vector
        def _(e):
            for r in range(2):
                i = e.memset(xpad[r][:, :, 0:KC - 1], 0.0)
            i.then_inc(s_pad, 1)
            def convolve(n):
                c, r = xblocks[n][0], n % 2
                e.wait_ge(s_xp, n + 1)
                if n >= 2:
                    e.wait_ge(s_u, n - 1)
                for j in range(KC):
                    tap = col(k, "convw", c * KC + j)
                    if j == 0:
                        e.tensor_scalar(acc[r][:, :, :], xpad[r][:, :, 0:L], tap, col(k, "convb", c),
                                        ALU.mult, ALU.add).then_inc(s_cv, 1)
                    else:
                        e.wait_ge(s_cv, 4 * n + j)
                        e.scalar_tensor_tensor(acc[r][:, :, :], xpad[r][:, :, j:j + L], tap, acc[r][:, :, :],
                                               ALU.mult, ALU.add).then_inc(s_cv, 1)

            def keep_rows(h):
                hs = slice(h * HALF, (h + 1) * HALF)
                e.wait_ge(s_xj, h + 1)
                e.tensor_copy(dtr[:, hs], xq[h][0:DTR, :])
                e.tensor_copy(bc[32:64, hs], xq[h][32:64, :]).then_inc(s_xe, 1)

            def positive(h):
                for n in range(CH * h, CH * (h + 1)):
                    e.wait_ge(s_dt, n + 1)
                    e.wait_ge(s_az, n + 1)
                    e.tensor_scalar(m.du[:, n % CH, h * HALF:(h + 1) * HALF], dq[n % 2][:, :],
                                    col(k, "dtb", n % CH), 0.0, ALU.add, ALU.max).then_inc(s_rz, 1)

            def deltas(h):
                hs = slice(h * HALF, (h + 1) * HALF)
                e.wait_ge(s_rz, CH * (h + 1))
                e.wait_ge(s_lz, h + 1)
                for c in range(CH):
                    e.tensor_tensor(m.delta[:, c, hs], m.delta[:, c, hs], m.du[:, c, hs], ALU.add
                                    ).then_inc(s_dl, 1)
                if h == 1:
                    for c in range(1, CH):
                        e.wait_ge(s_dl, CH + c + 1)
                        e.tensor_tensor(m.du[:, c, hs], m.delta[:, c, hs], m.u[:, c, hs], ALU.mult)

            for n in range(6):
                convolve(n)
            keep_rows(0)
            for n in range(6, 8):
                convolve(n)
            positive(0)
            keep_rows(1)
            for c in range(CH):
                e.tensor_scalar(m.diagD[:, c, :], k.ident[:, :], col(k, "dpar", c), None, ALU.mult)
            positive(1)
            e.wait_ge(k.s_rows, 32)
            e.tensor_tensor(k.x[:, :, :], k.x[:, :, :],
                            rowvec(k, "outb").unsqueeze(1).to_broadcast([P, TILES, D]), ALU.add)
            deltas(0)
            deltas(1)

        @block.gpsimd
        def _(e):
            for n, (c, h) in enumerate(xblocks[:5]):
                hs = slice(h * HALF, (h + 1) * HALF)
                e.wait_ge(s_dl, n + 1)
                e.tensor_tensor(m.du[:, c, hs], m.delta[:, c, hs], m.u[:, c, hs], ALU.mult)

        @block.sync
        def _(e):
            e.wait_ge(s_xe, 2)
            e.dma_start(m.bc_dram, bc[32:64, :]).then_inc(s_bc, 16)
            e.wait_ge(s_bc, 16)
            load_state(e, m, 0, m.Bb[0], 0, m.s_bl[0])
            for q in range(2):
                load_state(e, m, q, m.Cb[q], DS, m.s_cl[q])


def load_state(e, m, n, buf, row, s):
    src = m.bc_dram[row + n:row + n + 1, :] if isinstance(n, int) else m.bc_dram[bass.ds(n + row, 1), :]
    e.dma_start(buf, src.to_broadcast([P, TOK])).then_inc(s, 16)


def mamba_scan(nc, k, m):
    with ExitStack() as ctx:
        sb, ps, sem = tools(nc, ctx)
        ND = 4
        Bb, Cb, s_bl, s_cl = m.Bb, m.Cb, m.s_bl, m.s_cl
        A = [k.xn[:, 4 * i:4 * i + 4, :].rearrange("p t d -> p (t d)") for i in range(2)]
        dbu = [sb(f"dbu{i}", [P, TOK]) for i in range(ND)]
        hh = [sb(f"hh{i}", [P, TOK]) for i in range(ND)]
        Y = ps("Y", [P, CH, TOK])
        s_A = sem("n_A")
        s_bu = sem("n_bu")
        s_h = sem("n_h")
        s_hc = sem("n_hc")
        s_y = sem("n_y")
        s_yg = sem("n_yg")
        s_o = sem("n_o")
        s_xa = sem("n_xa")
        block = ctx.enter_context(nc.Block())
        STEPS = DS * CH

        def out(t, n):
            return Y[:, t // 4, (t % 4) * D:(t % 4 + n) * D]

        def steps(e, body):
            with e.Fori(0, DS // 2) as j:
                for q in range(2):
                    for c in range(CH):
                        body(j * 2 + q, q, c, j * (2 * CH) + (q * CH + c))

        @block.sync
        def _(e):
            load_state(e, m, 1, Bb[1], 0, s_bl[1])
            with e.Fori(1, DS // 2) as j:
                for q in range(2):
                    e.wait_ge(s_bu, j * (2 * CH) + (q - 1) * CH)
                    load_state(e, m, j * 2 + q, Bb[q], 0, s_bl[q])
                    e.wait_ge(s_hc, j * (2 * CH) + (q - 1) * CH)
                    load_state(e, m, j * 2 + q, Cb[q], DS, s_cl[q])

        @block.scalar
        def _(e):
            def body(n, q, c, s):
                by_batch = lambda a: a.rearrange("p (b l) -> p b l", l=L)[:, :, 1:L]
                e.wait_ge(s_h, s + 3)
                e.activation(by_batch(A[c % 2]), by_batch(m.delta[:, c, :]), ACT.Exp,
                             scale=m.negA[:, c, :][:, bass.ds(n, 1)]).then_inc(s_A, 1)

            steps(e, body)

        @block.gpsimd
        def _(e):
            def body(n, q, c, s):
                if c == 0:
                    e.wait_ge(s_bl[q], n * 8 + (16 - 8 * q))
                e.wait_ge(s_h, s + 1)
                e.tensor_tensor(dbu[c % ND][:, :], m.du[:, c, :], Bb[q], ALU.mult).then_inc(s_bu, 1)

            steps(e, body)

        @block.vector
        def _(e):
            for r in range(2):
                zero = A[r].rearrange("p (b l) -> p b l", l=L)[:, :, 0]
                for b in range(0, B, B // 2):
                    e.memset(zero[:, b:b + B // 2], 0.0).then_inc(s_h, 1)

            def emit_hc(n, q, c, s):
                if c == 0:
                    e.wait_ge(s_cl[q], n * 8 + (16 - 8 * q))
                e.wait_ge(s_h, s + 5)
                e.tensor_tensor(hh[c][:, :], hh[c][:, :], Cb[q], ALU.mult).then_inc(s_hc, 1)

            def body(n, q, c, s):
                e.wait_ge(s_A, s + 1)
                e.wait_ge(s_bu, s + 1)
                e.wait_ge(s_y, s + 1)
                e.tensor_tensor_scan(hh[c][:, :], A[c % 2], dbu[c][:, :], 0.0, ALU.mult, ALU.add
                                     ).then_inc(s_h, 1)
                if c:
                    emit_hc(n, q, c - 1, s - 1)
                if c == CH - 1:
                    emit_hc(n, q, c, s)

            steps(e, body)
            for c in range(CH):
                e.wait_ge(s_y, STEPS + 1 + c)
                e.tensor_tensor(m.sres[:, c, :], Y[:, c, :], m.sres[:, c, :], ALU.mult).then_inc(s_yg, 1)
            for g in range(TILES // 2):
                e.wait_ge(s_o, g + 1)
                x = k.x[:, 2 * g:2 * g + 2, :].rearrange("p t d -> p (t d)")
                e.tensor_tensor(x, x, out(2 * g, 2), ALU.add).then_inc(s_xa, 1)
                e.wait_ge(s_xa, g + 1)
                for t in (2 * g, 2 * g + 1):
                    tile_stats(e, k, t)

        @block.tensor
        def _(e):
            for c in range(CH):
                for h in range(2):
                    i = e.matmul(Y[:, c, h * HALF:(h + 1) * HALF], m.diagD[:, c, :],
                                 m.u[:, c, h * HALF:(h + 1) * HALF], start=True, stop=False,
                                 skip_group_check=True)
                i.then_inc(s_y, 1)

            def body(n, q, c, s):
                e.wait_ge(s_hc, s + 1)
                for h in range(2):
                    i = e.matmul(Y[:, c, h * HALF:(h + 1) * HALF], k.ident[:, :],
                                 hh[c][:, h * HALF:(h + 1) * HALF], start=False, stop=True,
                                 skip_group_check=True)
                i.then_inc(s_y, 1)

            steps(e, body)

            def out_proj(t, c):
                return e.matmul(out(t, 1), m.sres[:, c, t * P:(t + 1) * P], k.w_out[:, c, :],
                                start=c == 0 and t % 2 == 0, stop=True, skip_group_check=True)

            for c in range(CH):
                e.wait_ge(s_yg, c + 1)
                for t in range(TILES // 2):
                    i = out_proj(t, c)
                    if c == CH - 1 and t % 2:
                        i.then_inc(s_o, 1)
            for t in range(TILES // 2, TILES, 2):
                for c in range(CH):
                    for u in range(2):
                        i = out_proj(t + u, c)
                i.then_inc(s_o, 1)


def spiking_ffn(nc, k):
    beta, thr, steps = 0.9, 1.0, 5
    with ExitStack() as ctx:
        sb, ps, sem = tools(nc, ctx)
        r_sb = [sb(f"r{i}", [P, HALF]) for i in range(2)]
        hT = sb("hT", [P, FM, TOK])
        y = [sb(f"y{i}", [P, 2 * D]) for i in range(2)]
        mem = [sb(f"mem{i}", [P, 2 * D]) for i in range(2)]
        drive = sb("drive", [P, 2 * D])
        cnt = sb("cnt", [P, 2 * D])
        raw = [sb(f"raw{i}", [P, 2 * D]) for i in range(4)]
        fp = [ps(f"fp{i}") for i in range(4)]
        yp = [ps(f"yp{i}") for i in range(2)]
        s_fc = sem("f_fc")
        s_re = sem("f_re")
        s_h = sem("f_h")
        s_pr = sem("f_pr")
        s_y = sem("f_y")
        s_kv = sem("f_kv")
        s_ke = sem("f_ke")
        s_kp = sem("f_kp")
        s_d = sem("f_d")
        block = ctx.enter_context(nc.Block())
        blocks = [(m, h) for h in range(2) for m in range(FM)]

        @block.tensor
        def _(e):
            e.wait_ge(k.s_w3, k.n_w3)
            AHEAD = 3
            for h in range(2):
                for n in (range(FM + AHEAD), range(FM + AHEAD, 2 * FM))[h]:
                    m, hf = n % FM, n // FM
                    if n >= 4:
                        e.wait_ge(s_re, n - 3)
                    for kt in range(KD):
                        i = e.matmul(fp[n % 4][:, :], k.w_fc[:, kt, m * P:(m + 1) * P],
                                     k.xT[:, kt, hf * HALF:(hf + 1) * HALF], start=kt == 0, stop=kt == 1)
                    i.then_inc(s_fc, 1)
                e.wait_ge(s_h, FM * (h + 1))
                for g in (2 * h, 2 * h + 1):
                    if g >= 2:
                        e.wait_ge(s_y, g - 1)
                    for u in range(2):
                        t = 2 * g + u
                        for m in range(FM):
                            i = e.matmul(yp[g % 2][:, u * D:(u + 1) * D], hT[:, m, t * P:(t + 1) * P],
                                         k.w_pr[:, m, :], start=m == 0, stop=m == FM - 1)
                    i.then_inc(s_pr, 1)

            e.wait_ge(k.s_w4, k.n_w4)
            for t in range(TILES):
                e.wait_ge(s_re, 2 * FM)
                if t >= 4:
                    e.wait_ge(s_ke, t - 3)
                for i in range(2):
                    for c in range(KD):
                        ins = e.matmul(fp[t % 4][:, i * D:(i + 1) * D], k.c0T[:, c, t * P:(t + 1) * P],
                                       k.w4[1 + i][:, c, :], start=c == 0, stop=c == 1)
                ins.then_inc(s_kv, 1)

        @block.scalar
        def _(e):
            for h in range(2):
                for n in range(FM * h, FM * (h + 1)):
                    m = n % FM
                    e.wait_ge(s_fc, n + 1)
                    if n >= 2:
                        e.wait_ge(s_h, n - 1)
                    e.activation(r_sb[n % 2][:, :], fp[n % 4][:, :], ACT.Relu).then_inc(s_re, 1)
                for g in (2 * h, 2 * h + 1):
                    e.wait_ge(s_pr, g + 1)
                    if g >= 2:
                        e.wait_ge(s_d, 14 * (g - 1))
                    e.activation(y[g % 2][:, :], yp[g % 2][:, :], ACT.Copy).then_inc(s_y, 1)

            for t in range(TILES):
                e.wait_ge(s_kv, t + 1)
                if t >= 4:
                    e.wait_ge(s_kp, t - 3)
                e.activation(raw[t % 4][:, :], fp[t % 4][:, :], ACT.Copy).then_inc(s_ke, 1)

        @block.gpsimd
        def _(e):
            for n, (m, h) in enumerate(blocks):
                e.wait_ge(s_re, n + 1)
                r = r_sb[n % 2]
                e.tensor_tensor(hT[:, m, h * HALF:(h + 1) * HALF], r[:, :], r[:, :], ALU.mult).then_inc(s_h, 1)

            e.memset(k.vx[:, :, :, DH:DV], 1.0)
            for t in range(TILES):
                e.wait_ge(s_ke, t + 1)
                by_head = lambda a: a.rearrange("p (h d) -> p h d", d=DH)
                e.tensor_tensor(k.qkb[:, t, H:2 * H, :], by_head(raw[t % 4][:, 0:D]), by_head(rowvec(k, "bk4")), ALU.add)
                e.tensor_tensor(k.vx[:, t, :, 0:DH], by_head(raw[t % 4][:, D:2 * D]), by_head(rowvec(k, "bv4")),
                                ALU.add).then_inc(s_kp, 1)

        @block.vector
        def _(e):
            n = 0

            def chain(ins, wait=True):
                nonlocal n
                n += 1
                ins.then_inc(s_d, 1)
                if wait:
                    e.wait_ge(s_d, n)

            def count(cur, first):
                if first:
                    chain(e.tensor_scalar(cnt[:, :], cur, thr, None, ALU.is_gt), wait=False)
                else:
                    chain(e.scalar_tensor_tensor(cnt[:, :], cur, thr, cnt[:, :], ALU.is_gt, ALU.add), wait=False)
                e.wait_ge(s_d, n - 1)

            for g in range(TILES // 2):
                e.wait_ge(s_y, g + 1)
                yg = y[g % 2][:, :]
                cur = yg
                for s in range(1, steps):
                    nxt = mem[s % 2][:, :]
                    chain(e.scalar_tensor_tensor(drive[:, :], cur, beta, yg, ALU.mult, ALU.add), wait=False)
                    count(cur, s == 1)
                    chain(e.scalar_tensor_tensor(nxt, cur, thr, drive[:, :], ALU.is_gt, ALU.subtract,
                                                 reverse1=True))
                    cur = nxt
                count(cur, False)
                x = k.x[:, 2 * g:2 * g + 2, :].rearrange("p t d -> p (t d)")
                e.wait_ge(s_d, n)
                chain(e.scalar_tensor_tensor(x, cnt[:, :], 1.0 / steps, x, ALU.mult, ALU.add))
                for t in (2 * g, 2 * g + 1):
                    tile_stats(e, k, t)


def windowed_attention(nc, k):
    with ExitStack() as ctx:
        sb, _, _ = tools(nc, ctx)
        qT = sb("q4T", [P, TILES, KD, P])
        kT = sb("k4T", [P, TILES, KD, P])
        windowed_projections(nc, k, qT, kT)
        windowed_heads(nc, k, qT, kT, k.vx)


def windowed_projections(nc, k, qT, kT):
    with ExitStack() as ctx:
        sb, ps, sem = tools(nc, ctx)
        NR = 4
        t2 = [sb(f"t2{i}", [P, 2 * H, DH]) for i in range(NR)]
        t1 = [sb(f"t1{i}", [P, 2 * H, DH]) for i in range(NR)]
        rot = [sb(f"rot{i}", [P, 2 * H, DH]) for i in range(NR)]
        Q = [ps(f"Q{i}") for i in range(4)]
        TQ = [ps(f"TQ{i}") for i in range(2)]
        s_pj = sem("w_pj")
        s_b = sem("w_b")
        s_sn = sem("w_sn")
        s_cs = sem("w_cs")
        s_rt = sem("w_rt")
        s_tq = sem("w_tq")
        s_qe = sem("w_qe")
        with nc.Block() as block:
            @block.tensor
            def _(e):
                e.wait_ge(k.s_w4, k.n_w4)

                def turn(t):
                    e.wait_ge(s_rt, t + 1)
                    if t >= 2:
                        e.wait_ge(s_qe, t - 1)
                    for c in range(2 * KD):
                        i = e.transpose(TQ[t % 2][:, c * P:(c + 1) * P],
                                        rot[t % NR][:, c * HG:(c + 1) * HG, :].rearrange("p h d -> p (h d)"),
                                        k.ident[:, :])
                    i.then_inc(s_tq, 1)

                def project(t):
                    if t >= 4:
                        e.wait_ge(s_b, t - 3)
                    for c in range(KD):
                        i = e.matmul(Q[t % 4][:, 0:D], k.xT[:, c, t * P:(t + 1) * P], k.w4[0][:, c, :],
                                     start=c == 0, stop=c == 1)
                    i.then_inc(s_pj, 1)

                for t in range(4):
                    project(t)
                for t in range(TILES):
                    if t + 4 < TILES:
                        project(t + 4)
                    turn(t)

            @block.scalar
            def _(e):
                for t in range(TILES):
                    e.wait_ge(s_tq, t + 1)
                    src = TQ[t % 2][:, :].rearrange("p (c n) -> p c n", n=P)
                    e.activation(qT[:, t, :, :], src[:, 0:KD, :], ACT.Copy)
                    e.activation(kT[:, t, :, :], src[:, KD:2 * KD, :], ACT.Copy).then_inc(s_qe, 1)

            @block.gpsimd
            def _(e):
                e.wait_ge(k.s_w4, k.n_w4)
                for t in range(TILES):
                    e.wait_ge(s_b, t + 1)
                    if t >= NR:
                        e.wait_ge(s_rt, t - NR + 1)
                    hd = DH // 2
                    sn = [k.trig[:, 1, i * hd:(i + 1) * hd].unsqueeze(1).to_broadcast([P, 2 * H, hd]) for i in range(2)]
                    e.tensor_tensor(t2[t % NR][:, :, 0:hd], k.qkb[:, t, :, hd:DH], sn[0], ALU.mult)
                    e.tensor_tensor(t2[t % NR][:, :, hd:DH], k.qkb[:, t, :, 0:hd], sn[1], ALU.mult).then_inc(s_sn, 1)

            @block.vector
            def _(e):
                e.wait_ge(k.s_w4, k.n_w4)
                bias = rowvec(k, "bq4").rearrange("p (h d) -> p h d", d=DH)

                def queries(t):
                    e.wait_ge(s_pj, t + 1)
                    e.tensor_tensor(k.qkb[:, t, 0:H, :], Q[t % 4][:, 0:D].rearrange("p (h d) -> p h d", d=DH), bias,
                                    ALU.add).then_inc(s_b, 1)

                def cosines(t):
                    e.wait_ge(s_b, t + 1)
                    if t >= NR:
                        e.wait_ge(s_rt, t - NR + 1)
                    cs = k.trig[:, 0, :].unsqueeze(1).to_broadcast([P, 2 * H, DH])
                    e.tensor_tensor(t1[t % NR][:, :, :], k.qkb[:, t, :, :], cs, ALU.mult).then_inc(s_cs, 1)

                def rotate(t):
                    e.wait_ge(s_cs, t + 1)
                    e.wait_ge(s_sn, t + 1)
                    if t >= NR:
                        e.wait_ge(s_tq, t - NR + 1)
                    e.tensor_tensor(rot[t % NR][:, :, :], t1[t % NR][:, :, :], t2[t % NR][:, :, :], ALU.add
                                    ).then_inc(s_rt, 1)

                queries(0)
                queries(1)
                cosines(0)
                for t in range(TILES):
                    if t + 2 < TILES:
                        queries(t + 2)
                    if t + 1 < TILES:
                        cosines(t + 1)
                    rotate(t)
                e.tensor_tensor(k.x[:, :, :], k.x[:, :, :],
                                rowvec(k, "bo4").unsqueeze(1).to_broadcast([P, TILES, D]), ALU.add)


def windowed_heads(nc, k, qT, kT, vx):
    scale = float(DH) ** -0.5
    with ExitStack() as ctx:
        sb, ps, sem = tools(nc, ctx)
        qs = [sb(f"hqs{i}", [P, KD, P]) for i in range(2)]
        kb = [sb(f"hkb{i}", [P, 2, KD, HG * L]) for i in range(2)]
        mx = [sb(f"hmx{i}", [P, H]) for i in range(2)]
        sm = [sb(f"hsm{i}", [P, H, L]) for i in range(2)]
        pb = [sb(f"hpb{i}", [P, H, L]) for i in range(2)]
        pT = sb("hpT", [P, H // 2, P])
        v2 = [sb(f"hv2{i}", [P, H // 2, 2, 2, DV]) for i in range(2)]
        ri = sb("hri", [P, H])
        on = [sb(f"hon{i}", [P, D]) for i in range(2)]
        onT = sb("honT", [P, KD, P])
        S = ps("hS", [P, 2 * HALF])
        TP = [ps(f"hTP{i}") for i in range(2)]
        O = ps("hO")
        X = ps("hX")
        s_z = sem("h_z")
        s_v2 = sem("h_v2")
        s_qs = sem("h_qs")
        s_sc = sem("h_sc")
        s_mk = sem("h_mk")
        s_mx = sem("h_mx")
        s_sm = sem("h_sm")
        s_ex = sem("h_ex")
        s_tp = sem("h_tp")
        s_te = sem("h_te")
        s_pv = sem("h_pv")
        s_ri = sem("h_ri")
        s_on = sem("h_on")
        s_ot = sem("h_ot")
        s_oe = sem("h_oe")
        s_wo = sem("h_wo")
        s_xa = sem("h_xa")
        block = ctx.enter_context(nc.Block())

        def pipeline(e, sub):
            for i in range(4):
                sub(i, i % 2, i - 2, i - 3, lambda t: t >= 0)
            with e.Fori(2, TILES // 2) as j:
                for r in range(2):
                    sub(j * 2 + r, r, j * 2 + (r - 2), j * 2 + (r - 3), lambda t: True)
            for i in range(TILES, TILES + 3):
                sub(i, i % 2, i - 2, i - 3, lambda t: t < TILES)

        def at(a, i):
            return a[:, i] if isinstance(i, int) else a[:, bass.ds(i, 1)].squeeze(1)

        @block.tensor
        def _(e):
            def sub(i, r, a, c, has):
                if has(i):
                    e.wait_ge(s_qs, i + 1)
                    e.wait_ge(s_mk, i)
                    for g in range(KD):
                        for b in range(2):
                            j = e.matmul(S[64 * b:64 * b + 64, g * HALF:(g + 1) * HALF],
                                         qs[r][:, g, 64 * b:64 * b + 64], kb[r][:, b, g, :],
                                         start=True, stop=True)
                    j.then_inc(s_sc, 1)
                if has(a):
                    e.wait_ge(s_ex, a + 1)
                    for g in range(2):
                        for u in range(4):
                            h = 2 * (4 * g + u)
                            j = e.transpose(TP[g][:, u * P:(u + 1) * P],
                                            pb[r][:, h:h + 2, :].rearrange("p h n -> p (h n)"), k.ident[:, :])
                        j.then_inc(s_tp, 1)
                if has(c):
                    e.wait_ge(s_on, c + 1)
                    e.wait_ge(s_xa, c)
                    for g in range(KD):
                        j = e.transpose(X[:, g * P:(g + 1) * P], on[1 - r][:, g * P:(g + 1) * P], k.ident[:, :])
                    j.then_inc(s_ot, 1)
                if has(a):
                    e.wait_ge(s_on, a)
                    e.wait_ge(s_v2, a + 1)
                    for g in range(2):
                        e.wait_ge(s_te, a * 2 + (g + 1))
                        for h in range(4 * g, 4 * g + 4):
                            for b in range(2):
                                j = e.matmul(O[64 * b:64 * b + 64, 2 * h * DV:2 * (h + 1) * DV],
                                             pT[:, h, 64 * b:64 * b + 64],
                                             v2[r][:, h, b, :, :].rearrange("p u d -> p (u d)"), start=True, stop=True)
                    j.then_inc(s_pv, 1)
                if has(c):
                    e.wait_ge(s_oe, c + 1)
                    for g in range(KD):
                        j = e.matmul(X[:, D:2 * D], onT[:, g, :], k.w4[3][:, g, :], start=g == 0, stop=g == 1)
                    j.then_inc(s_wo, 1)

            pipeline(e, sub)

        @block.scalar
        def _(e):
            def sub(i, r, a, c, has):
                if has(a):
                    e.wait_ge(s_pv, a)
                    for g in range(2):
                        e.wait_ge(s_tp, a * 2 + (g + 1))
                        e.activation(pT[:, 4 * g:4 * g + 4, :], TP[g][:, :].rearrange("p (u n) -> p u n", n=P),
                                     ACT.Copy).then_inc(s_te, 1)
                if has(c):
                    e.wait_ge(s_ot, c + 1)
                    e.wait_ge(s_wo, c)
                    e.activation(onT[:, :, :], X[:, 0:D].rearrange("p (c n) -> p c n", c=KD), ACT.Copy
                                 ).then_inc(s_oe, 1)
                if has(i):
                    if not isinstance(i, int) or i >= 2:
                        e.wait_ge(s_tp, (i - 1) * 2)
                    e.wait_ge(s_sm, i + 1)
                    e.activation(pb[r][:, :, :], sm[r][:, :, :], ACT.Exp, scale=scale).then_inc(s_ex, 1)

            pipeline(e, sub)

        @block.gpsimd
        def _(e):
            for r in range(2):
                e.memset(v2[r][:, :, :, :, :], 0.0).then_inc(s_z, 1)

            def sub(i, r, a, c, has):
                if has(i):
                    if not isinstance(i, int) or i >= 2:
                        e.wait_ge(s_sc, i - 1)
                    e.tensor_copy(qs[r][:, :, :], at(qT, i))
                    keys = at(kT, i)
                    for b in range(2):
                        for c in range(KD):
                            j = e.tensor_tensor(kb[r][:, b, c, :].rearrange("p (h n) -> p h n", n=L),
                                                keys[:, c, b * L:(b + 1) * L].unsqueeze(1).to_broadcast([P, HG, L]),
                                                k.own_head[:, :].unsqueeze(2).to_broadcast([P, HG, L]), ALU.mult)
                    j.then_inc(s_qs, 1)

            pipeline(e, sub)

        @block.vector
        def _(e):
            e.wait_ge(s_z, 2)
            e.wait_ge(k.s_vs, 32)

            def sub(i, r, a, c, has):
                if has(i):
                    if not isinstance(i, int) or i >= 2:
                        e.wait_ge(s_pv, i - 1)
                    for u in range(2):
                        rows = slice(64 * u, 64 * u + 64)
                        for b in range(2):
                            src = at(vx if b == u else k.vs, i)[rows, :, :].rearrange("p (h w) d -> p h w d", w=2)
                            j = e.tensor_copy(v2[r][rows, :, b, u, :], src[:, :, u, :])
                    j.then_inc(s_v2, 1)
                    e.wait_ge(s_sc, i + 1)
                    if not isinstance(i, int) or i >= 2:
                        e.wait_ge(s_ex, i - 1)
                    e.tensor_tensor(sm[r][:, :, :], S[:, :].rearrange("p (h n) -> p h n", n=L),
                                    k.masked[:, :].unsqueeze(1).to_broadcast([P, H, L]), ALU.add).then_inc(s_mk, 1)
                    e.wait_ge(s_mk, i + 1)
                    e.reduce_max(mx[r][:, :], sm[r][:, :, :], AX.X).then_inc(s_mx, 1)
                    e.wait_ge(s_mx, i + 1)
                    e.tensor_tensor(sm[r][:, :, :], sm[r][:, :, :], mx[r][:, :].unsqueeze(2).to_broadcast([P, H, L]),
                                    ALU.subtract).then_inc(s_sm, 1)
                if has(a):
                    e.wait_ge(s_pv, a + 1)
                    Ov = O[:, 0:H * DV].rearrange("p (h d) -> p h d", d=DV)
                    e.reciprocal(ri[:, :], Ov[:, :, DH]).then_inc(s_ri, 1)
                    e.wait_ge(s_ri, a + 1)
                    e.tensor_tensor(on[r][:, :].rearrange("p (h d) -> p h d", d=DH), Ov[:, :, 0:DH],
                                    ri[:, :].unsqueeze(2).to_broadcast([P, H, DH]), ALU.mult).then_inc(s_on, 1)
                if has(c):
                    e.wait_ge(s_wo, c + 1)
                    x = at(k.x, c)
                    e.tensor_tensor(x, x, X[:, D:2 * D], ALU.add).then_inc(s_xa, 1)
                    e.wait_ge(s_xa, c + 1)
                    tile_stats(e, k, c)

            pipeline(e, sub)


def phase_attention(nc, k):
    scale = 1.0 / float(D) ** 0.5
    n_pairs = float(L * L)
    with ExitStack() as ctx:
        sb, ps, sem = tools(nc, ctx)
        qT = sb("q5T", [P, KD, TOK])
        kT = sb("k5T", [P, KD, TOK])
        v = sb("v5", [P, TILES, D])
        qp = sb("qp", [P, TILES, 2])
        diag = sb("diag", [P, 2, TILES, L])
        dd = sb("dd", [P, 2, TILES, L])
        dq = sb("dq", [P, 2, TILES, L])
        dist = sb("dist", [P, TILES, L])
        dev = sb("dev", [P, TILES, L])
        small = sb("small", [P, 8, TILES])
        rowsum, mean, rowsq, var, std, thr, mx, tot = (small[:, i, :] for i in range(8))
        ri = sb("ri5", [P, TILES])
        ok = sb("ok", [P, TILES, L])
        ady = sb("ady", [P, TILES, L])
        sm = sb("sm5", [P, TILES, L])
        pb = sb("pb5", [P, TILES, P])
        pT = sb("p5T", [P, TILES, P])
        cn = sb("cn", [P, TILES, D])
        cnT = sb("cnT", [P, KD, TOK])
        nrm = sb("nrm", [P, 2, TILES])
        qsq = sb("qsq", [P, TILES, 2])
        re = sb("re", [P, TILES, 2])
        reT = sb("reT", [2, TOK])
        bias = sb("bias5", [P, D])
        BK = [ps(f"BK{i}") for i in range(8)]
        s_pe = sem("p_pe")
        s_ac = sem("p_ac")
        s_ve = sem("p_ve")
        s_z = sem("p_z")
        block = ctx.enter_context(nc.Block())
        pe_at, ac_at, ve_at = {}, {}, {}
        pe_steps = (["qp", ("qk", 0), ("qk", 1), "row"] + [("qk", n) for n in range(2, 6)] + ["sum", ("qk", 6), ("qk", 7)]
                    + ["sumsq", "scores"] + [("v", g) for g in range(4)] + ["reT"] + [("pT", g) for g in range(2)] + [("pv", g) for g in range(4)]
                    + [("cT", g) for g in range(4)] + [("o", g) for g in range(4)])
        for n, name in enumerate(pe_steps):
            pe_at[name] = n + 1
        ac_steps = ([("qk", n) for n in range(8)] + ["nrm", "std"] + [("v", g) for g in range(4)] + ["exp0", "exp", "reT"]
                    + [("pT", 1)] + [("cT", g) for g in range(4)])
        for n, name in enumerate(ac_steps):
            ac_at[name] = n + 1
        ve_steps = ["qp", "qsq", "nrm2", "diag", "dd", "dq", "dist", "rowsum", "mean", "dev", "devsq", "rowsq",
                    "var", "nrmx", "nri", "re", "bias", "ady0", "ady", "ok", "okc", "thr", "in", "ok2", "add", "masked",
                    "mx", "sub", "den", "ri", ("pT", 0)] + [("cn", g) for g in range(4)] + ["xadd0", "xadd"] + [("x", g) for g in range(4)]
        for n, name in enumerate(ve_steps):
            ve_at[name] = n + 1
        made = {"pe": 0, "ac": 0, "ve": 0}

        def mark(ins, table, who, sem_, name):
            made[who] += 1
            assert table[name] == made[who], (name, made[who])
            ins.then_inc(sem_, 1)

        @block.tensor
        def _(e):
            done = lambda ins, name: mark(ins, pe_at, "pe", s_pe, name)
            ac = lambda name: e.wait_ge(s_ac, ac_at[name])
            ve = lambda name: e.wait_ge(s_ve, ve_at[name])
            e.wait_ge(k.s_w5, k.n_w5)
            for t in range(TILES):
                for c in range(KD):
                    i = e.matmul(BK[6][:, 2 * t:2 * t + 2], k.xT[:, c, t * P:(t + 1) * P], k.wtq[:, c, :],
                                 start=c == 0, stop=c == 1)
            done(i, "qp")
            def project(n):
                w, m, h = n // 4, n // 2 % 2, n % 2
                if n >= 4:
                    ac(("qk", n - 4))
                for c in range(KD):
                    i = e.matmul(BK[n % 4][:, :], k.w5[w][:, c, m * P:(m + 1) * P],
                                 k.xT[:, c, h * HALF:(h + 1) * HALF], start=c == 0, stop=c == 1)
                done(i, ("qk", n))

            for n in range(2):
                project(n)
            ve("diag")
            for g in range(2):
                i = e.matmul(BK[4 + g][:, :], k.same_batch[:, :], diag[:, g, :, :].rearrange("p t n -> p (t n)"),
                             start=True, stop=True)
            done(i, "row")
            for n in range(2, 6):
                project(n)
            ve("rowsum")
            done(e.matmul(BK[6][:, 64:64 + TILES], k.same_batch[:, :], rowsum, start=True, stop=True), "sum")
            for n in range(6, 8):
                project(n)
            ve("rowsq")
            done(e.matmul(BK[6][:, 128:128 + TILES], k.same_batch[:, :], rowsq, start=True, stop=True), "sumsq")
            ac(("qk", 7))
            for t in range(TILES):
                for c in range(KD):
                    for b in range(2):
                        q = slice(t * P + 64 * b, t * P + 64 * b + 64)
                        i = e.matmul(BK[7][64 * b:64 * b + 64, t * L:(t + 1) * L], qT[:, c, q], kT[:, c, q],
                                     start=c == 0, stop=c == 1)
            done(i, "scores")
            for g in range(4):
                for u in range(2):
                    t = 2 * g + u
                    for c in range(KD):
                        i = e.matmul(BK[g][:, u * D:(u + 1) * D], k.xT[:, c, t * P:(t + 1) * P], k.w5[2][:, c, :],
                                     start=c == 0, stop=c == 1)
                done(i, ("v", g))
            ve("re")
            ac(("v", 3))
            for t in range(TILES):
                i = e.transpose(BK[t // 4][0:2, (t % 4) * P:(t % 4 + 1) * P], re[:, t, :], k.ident[:, :])
            done(i, "reT")
            ve("ri")
            ac("exp")
            ac("reT")
            for g in range(2):
                for u in range(4):
                    i = e.transpose(BK[4 + g][:, u * P:(u + 1) * P], pb[:, 4 * g + u, :], k.ident[:, :])
                done(i, ("pT", g))
            ve(("pT", 0))
            ac(("pT", 1))
            for g in range(4):
                for u in range(2):
                    t = 2 * g + u
                    i = e.matmul(BK[g][:, u * D:(u + 1) * D], pT[:, t, :], v[:, t, :], start=True, stop=True)
                done(i, ("pv", g))
            for g in range(4):
                ve(("cn", g))
                for u in range(2):
                    for c in range(KD):
                        i = e.transpose(BK[4 + g][:, (2 * u + c) * P:(2 * u + c + 1) * P],
                                        cn[:, 2 * g + u, c * P:(c + 1) * P], k.ident[:, :])
                done(i, ("cT", g))
            for g in range(4):
                ac(("cT", g))
                for u in range(2):
                    t = 2 * g + u
                    for c in range(KD):
                        e.matmul(BK[g][:, u * D:(u + 1) * D], cnT[:, c, t * P:(t + 1) * P], k.w5[3][:, c, :],
                                 start=c == 0, stop=False)
                    i = e.matmul(BK[g][:, u * D:(u + 1) * D], reT[:, t * P:(t + 1) * P], k.wfq[:, :],
                                 start=False, stop=True)
                done(i, ("o", g))

        @block.scalar
        def _(e):
            done = lambda ins, name: mark(ins, ac_at, "ac", s_ac, name)
            pe = lambda name: e.wait_ge(s_pe, pe_at[name])
            ve = lambda name: e.wait_ge(s_ve, ve_at[name])
            n = 0
            for dst, b in ((qT, "bq5"), (kT, "bk5")):
                for m in range(KD):
                    for h in range(2):
                        pe(("qk", n))
                        done(e.activation(dst[:, m, h * HALF:(h + 1) * HALF], BK[n % 4][:, :], ACT.Identity,
                                          bias=col(k, b, m)), ("qk", n))
                        n += 1
            ve("nrm2")
            done(e.activation(nrm[:, 1, :], nrm[:, 0, :], ACT.Sqrt), "nrm")
            ve("var")
            done(e.activation(std, var, ACT.Sqrt), "std")
            for g in range(4):
                pe(("v", g))
                done(e.activation(v[:, 2 * g:2 * g + 2, :].rearrange("p t d -> p (t d)"), BK[g][:, :], ACT.Copy),
                     ("v", g))
            e.wait_ge(s_z, 1)
            ve("sub")
            for b in range(2):
                rows = slice(64 * b, 64 * b + 64)
                done(e.activation(pb[rows, :, 64 * b:64 * b + 64], sm[rows, :, :], ACT.Exp, scale=scale),
                     "exp0" if b == 0 else "exp")
            pe("reT")
            for g in range(2):
                i = e.activation(reT[:, g * HALF:(g + 1) * HALF], BK[g][0:2, :], ACT.Copy)
            done(i, "reT")
            pe(("pT", 1))
            done(e.activation(pT[:, 4:8, :], BK[5][:, :].rearrange("p (t n) -> p t n", n=P), ACT.Copy), ("pT", 1))
            for g in range(4):
                pe(("cT", g))
                src = BK[4 + g][:, :].rearrange("p (u c n) -> p c u n", u=2, c=KD)
                dst = cnT[:, :, 2 * g * P:(2 * g + 2) * P].rearrange("p c (u n) -> p c u n", u=2)
                done(e.activation(dst, src, ACT.Copy), ("cT", g))

        @block.gpsimd
        def _(e):
            e.memset(pb[:, :, :], 0.0).then_inc(s_z, 1)
            e.memset(k.one[:, :], 1.0).then_inc(s_z, 1)
            e.wait_ge(s_z, 2)
            for x in range(2):
                split_expert(e, k, x, x, 0)

        @block.sync
        def _(e):
            for x in range(2):
                load_expert(e, k, x, x)

        @block.vector
        def _(e):
            pe = lambda name: e.wait_ge(s_pe, pe_at[name])
            ac = lambda name: e.wait_ge(s_ac, ac_at[name])

            def done(ins, name):
                mark(ins, ve_at, "ve", s_ve, name)

            def chain(ins, name):
                done(ins, name)
                e.wait_ge(s_ve, ve_at[name])

            wide = lambda a: a.unsqueeze(2).to_broadcast([P, TILES, L])
            e.wait_ge(k.s_w5, k.n_w5)
            pe("qp")
            chain(e.tensor_tensor(qp[:, :, :], BK[6][:, 0:2 * TILES].rearrange("p (t w) -> p t w", w=2),
                                  k.btq[:, :].unsqueeze(1).to_broadcast([P, TILES, 2]), ALU.add), "qp")
            chain(e.tensor_tensor(qsq[:, :, :], qp[:, :, :], qp[:, :, :], ALU.mult), "qsq")
            chain(e.tensor_tensor(nrm[:, 0, :], qsq[:, :, 0], qsq[:, :, 1], ALU.add), "nrm2")
            for g in range(2):
                i = e.tensor_tensor(diag[:, g, :, :], wide(qp[:, :, g]),
                                    k.diag64[:, :].unsqueeze(1).to_broadcast([P, TILES, L]), ALU.mult)
            chain(i, "diag")
            pe("row")
            for g in range(2):
                i = e.tensor_tensor(dd[:, g, :, :], wide(qp[:, :, g]),
                                    BK[4 + g][:, :].rearrange("p (t n) -> p t n", n=L), ALU.subtract)
            chain(i, "dd")
            chain(e.tensor_tensor(dq[:, :, :, :].rearrange("p g t n -> p (g t n)"),
                                  dd[:, :, :, :].rearrange("p g t n -> p (g t n)"),
                                  dd[:, :, :, :].rearrange("p g t n -> p (g t n)"), ALU.mult), "dq")
            chain(e.tensor_tensor(dist[:, :, :], dq[:, 0, :, :], dq[:, 1, :, :], ALU.add), "dist")
            chain(e.reduce_sum(rowsum, dist[:, :, :], AX.X), "rowsum")
            pe("sum")
            chain(e.tensor_scalar(mean, BK[6][:, 64:64 + TILES], 1.0 / n_pairs, None, ALU.mult), "mean")
            chain(e.tensor_tensor(dev[:, :, :], dist[:, :, :], wide(mean), ALU.subtract), "dev")
            chain(e.tensor_tensor(dev[:, :, :], dev[:, :, :], dev[:, :, :], ALU.mult), "devsq")
            chain(e.reduce_sum(rowsq, dev[:, :, :], AX.X), "rowsq")
            pe("sumsq")
            done(e.tensor_scalar(var, BK[6][:, 128:128 + TILES], 1.0 / (n_pairs - 1.0), None, ALU.mult), "var")
            ac("nrm")
            chain(e.tensor_scalar(nrm[:, 0, :], nrm[:, 1, :], 1e-12, None, ALU.max), "nrmx")
            chain(e.reciprocal(nrm[:, 1, :], nrm[:, 0, :]), "nri")
            done(e.scalar_tensor_tensor(re[:, :, :], qp[:, :, :], 0.1,
                                        nrm[:, 1, :].unsqueeze(2).to_broadcast([P, TILES, 2]), ALU.mult, ALU.mult),
                 "re")
            done(e.scalar_tensor_tensor(bias[:, :], rowvec(k, "bfq"), 0.1, rowvec(k, "bo5"), ALU.mult, ALU.add),
                 "bias")
            chain(e.tensor_scalar(ady[:, :, :], dd[:, 1, :, :], -4096.0, None, ALU.mult), "ady0")
            chain(e.scalar_tensor_tensor(ady[:, :, :], dd[:, 1, :, :], 4096.0, ady[:, :, :], ALU.mult, ALU.max), "ady")
            chain(e.scalar_tensor_tensor(ok[:, :, :], dd[:, 0, :, :], -1.0, ady[:, :, :], ALU.mult, ALU.is_le), "ok")
            chain(e.tensor_tensor(ok[:, :, :], ok[:, :, :], k.causal[:, :].unsqueeze(1).to_broadcast([P, TILES, L]),
                                  ALU.mult), "okc")
            ac("std")
            chain(e.scalar_tensor_tensor(thr, std, 1.25, mean, ALU.mult, ALU.add), "thr")
            chain(e.tensor_tensor(dev[:, :, :], dist[:, :, :], wide(thr), ALU.is_le), "in")
            chain(e.tensor_tensor(ok[:, :, :], ok[:, :, :], dev[:, :, :], ALU.mult), "ok2")
            chain(e.tensor_scalar(ok[:, :, :], ok[:, :, :], -NEG, NEG, ALU.mult, ALU.add), "add")
            pe("scores")
            chain(e.tensor_tensor(sm[:, :, :], BK[7][:, :].rearrange("p (t n) -> p t n", n=L), ok[:, :, :], ALU.add),
                  "masked")
            chain(e.reduce_max(mx, sm[:, :, :], AX.X), "mx")
            done(e.tensor_tensor(sm[:, :, :], sm[:, :, :], wide(mx), ALU.subtract), "sub")
            ac("exp")
            for b in range(2):
                rows = slice(64 * b, 64 * b + 64)
                i = e.reduce_sum(tot[rows], pb[rows, :, 64 * b:64 * b + 64], AX.X)
            chain(i, "den")
            done(e.reciprocal(ri[:, :], tot), "ri")
            pe(("pT", 0))
            done(e.tensor_copy(pT[:, 0:4, :], BK[4][:, :].rearrange("p (t n) -> p t n", n=P)), ("pT", 0))
            for g in range(4):
                pe(("pv", g))
                for u in range(2):
                    t = 2 * g + u
                    i = e.scalar_tensor_tensor(cn[:, t, :], BK[g][:, u * D:(u + 1) * D], ri[:, t:t + 1],
                                               rowvec(k, "bv5"), ALU.mult, ALU.add)
                done(i, ("cn", g))
            chain(e.tensor_tensor(k.x[:, :, :].rearrange("p t d -> p (t d)"), k.x[:, :, :].rearrange("p t d -> p (t d)"),
                                  k.xn[:, :, :].rearrange("p t d -> p (t d)"), ALU.add), "xadd0")
            chain(e.tensor_tensor(k.x[:, :, :], k.x[:, :, :], bias[:, :].unsqueeze(1).to_broadcast([P, TILES, D]),
                                  ALU.add), "xadd")
            for g in range(4):
                pe(("o", g))
                x = k.x[:, 2 * g:2 * g + 2, :].rearrange("p t d -> p (t d)")
                chain(e.tensor_tensor(x, x, BK[g][:, :], ALU.add), ("x", g))
                for t in (2 * g, 2 * g + 1):
                    tile_stats(e, k, t)


def load_expert(e, k, x, r):
    for i in range(2):
        src = k.w_experts[i][x] if isinstance(x, int) else k.w_experts[i][bass.ds(x, 1)].squeeze(0)
        e.dma_start(k.w6[r][:, i, :, :], src.rearrange("(c p) n -> p c n", p=P)).then_inc(k.s_w[r], 16)


def split_expert(e, k, x, r, j):
    e.wait_ge(k.s_w[r], j * 32 + 32)
    for i in range(2):
        e.tensor_tensor(k.w_hi[r][:, i, :, :], k.w6[r][:, i, :, :],
                        k.one[:, :].unsqueeze(2).to_broadcast([P, KD, D]), ALU.mult).then_inc(k.s_hi, 1)
    for i in range(2):
        e.wait_ge(k.s_hi, x * 2 + (i + 1))
        e.tensor_tensor(k.w_lo[r][:, i, :, :], k.w6[r][:, i, :, :], k.w_hi[r][:, i, :, :].bitcast(F32), ALU.subtract
                        ).then_inc(k.s_ws, 1)


def experts(nc, k, out):
    with ExitStack() as ctx:
        sb, ps, sem = tools(nc, ctx)
        score = sb("score", [P, TILES, E])
        top = sb("top", [P, TILES, 8])
        idx = sb("idx", [P, TILES, 8], U32)
        idf = sb("idf", [P, TILES, 8])
        pick = [sb(f"pick{i}", [P, TILES, E]) for i in range(TOPK)]
        comb = sb("comb", [P, TILES, E])
        combT = sb("combT", [E, TOK])
        b1 = [sb(f"eb1{i}", [P, 2]) for i in range(2)]
        hid = [sb(f"hid{n}", [P, HALF]) for n in range(4)]
        h_hi = [sb(f"h_hi{i}", [P, KD, TOK], F32R) for i in range(2)]
        h_lo = [sb(f"h_lo{i}", [P, KD, TOK], F32R) for i in range(2)]
        HB = [ps(f"HB{i}") for i in range(4)]
        OB = [ps(f"OB{i}") for i in range(4)]
        s_g = sem("e_g")
        s_t = sem("e_t")
        s_ct = sem("e_ct")
        s_b1 = sem("e_b1")
        s_h = sem("e_h")
        s_r = sem("e_r")
        s_l = sem("e_l")
        s_o = sem("e_o")
        s_out = sem("e_out")
        s_a = sem("e_a")
        block = ctx.enter_context(nc.Block())
        blocks = [(m, h) for h in range(2) for m in range(KD)]

        def per_expert(e, body, between=None):
            body(0, 0, 0)
            if between:
                between()
            body(1, 1, 0)
            with e.Fori(1, E // 2) as j:
                for r in range(2):
                    body(j * 2 + r, r, j)

        @block.sync
        def _(e):
            with e.Fori(1, E // 2) as j:
                for r in range(2):
                    e.wait_ge(k.s_ws, j * 4 + (2 * r - 2))
                    load_expert(e, k, j * 2 + r, r)
            tiles = out.rearrange("b l d -> (b l) d").rearrange("(t p) d -> p t d", p=P)
            for g in range(4):
                e.wait_ge(s_a, 4 * E + g + 1)
                e.dma_start(tiles[:, 2 * g:2 * g + 2, :], k.x[:, 2 * g:2 * g + 2, :]).then_inc(s_out, 16)
            e.wait_ge(s_out, 64)

        @block.tensor
        def _(e):
            e.wait_ge(k.s_w6, k.n_w6)
            for t in range(TILES):
                for c in range(KD):
                    i = e.matmul(OB[0][:, t * E:(t + 1) * E], k.xT[:, c, t * P:(t + 1) * P], k.wg[:, c, :],
                                 start=c == 0, stop=c == 1)
            i.then_inc(s_g, 1)

            e.transpose(OB[3][:, 0:P], k.ident[:, :], k.ident[:, :]).then_inc(s_o, 1)

            def product(dst, hi, lo, w_hi, w_lo, first, last):
                for i, (a, b) in enumerate(((hi, w_hi), (hi, w_lo), (lo, w_hi))):
                    ins = e.matmul(dst, a, b, start=first and i == 0, stop=last and i == 2)
                return ins

            def hidden(x, r):
                e.wait_ge(k.s_ws, x * 2 + 2)
                for n, (m, h) in enumerate(blocks):
                    e.wait_ge(s_r, x * 4 + (n + 1))
                    cols, tok = slice(m * P, (m + 1) * P), slice(h * HALF, (h + 1) * HALF)
                    for c in range(KD):
                        i = product(HB[n][:, :], k.w_hi[r][:, 0, c, cols], k.w_lo[r][:, 0, c, cols],
                                    k.x_hi[:, c, tok], k.x_lo[:, c, tok], c == 0, c == 1)
                    i.then_inc(s_h, 1)

            def output(x, r):
                for g in range(4):
                    if g % 2 == 0:
                        e.wait_ge(s_r, x * 4 + (4 + 2 * (g // 2) + 2))
                        e.wait_ge(s_l, x * 4 + (4 + 2 * (g // 2) + 2))
                    e.wait_ge(s_a, x * 4 + (g + 1))
                    for u in range(2):
                        tok = slice((2 * g + u) * P, (2 * g + u + 1) * P)
                        for c in range(KD):
                            i = product(OB[g][:, u * D:(u + 1) * D], h_hi[r][:, c, tok], h_lo[r][:, c, tok],
                                        k.w_hi[r][:, 1, c, :], k.w_lo[r][:, 1, c, :], c == 0, c == 1)
                    i.then_inc(s_o, 1)

            def body(x, r, j):
                hidden(x, r)
                if isinstance(x, int) and x == 0:
                    shares()
                output(x, r)

            def shares():
                e.wait_ge(s_t, 7)
                for t in range(TILES):
                    i = e.transpose(OB[1 + t // 4][0:E, (t % 4) * P:(t % 4 + 1) * P], comb[:, t, :], k.ident[:, :])
                i.then_inc(s_g, 1)
                e.wait_ge(s_ct, 2)
                for g in range(4):
                    for u in range(2):
                        t = 2 * g + u
                        i = e.matmul(OB[g][:, u * D:(u + 1) * D], combT[:, t * P:(t + 1) * P], k.b2[:, :],
                                     start=True, stop=True)
                    i.then_inc(s_g, 1)

            per_expert(e, body)

        @block.scalar
        def _(e):
            for n in range(4):
                e.activation(hid[n][:, 0:1], k.ident[:, 0:1], ACT.Copy).then_inc(s_r, 1)
            e.wait_ge(s_r, 4)

            def body(x, r, j):
                e.wait_ge(s_b1, x + 1)
                for n, (m, h) in enumerate(blocks):
                    e.wait_ge(s_h, x * 4 + (n + 1))
                    if n == 0:
                        e.wait_ge(s_o, j * 8 + 1)
                    e.wait_ge(s_l, x * 4 + (n + 1))
                    for dst in (hid[n][:, :], h_hi[r][:, m, h * HALF:(h + 1) * HALF]):
                        i = e.activation(dst, HB[n][:, :], ACT.Relu, bias=b1[r][:, m:m + 1])
                    i.then_inc(s_r, 1)

            def comb_rows():
                e.wait_ge(s_g, 2)
                for n in range(2):
                    e.activation(combT[:, n * HALF:(n + 1) * HALF], OB[1 + n][0:E, :], ACT.Copy).then_inc(s_ct, 1)

            per_expert(e, body, comb_rows)

        @block.gpsimd
        def _(e):
            a0, _ = COLS["b1"]

            def body(x, r, j):
                e.wait_ge(s_r, x * 4 + 1)
                src = slice(x * 2 + a0, x * 2 + a0 + 2) if isinstance(x, int) else bass.ds(x * 2 + a0, 2)
                e.tensor_copy(b1[r][:, :], k.cols[:, src]).then_inc(s_b1, 1)
                if not isinstance(x, int):
                    e.wait_ge(s_o, j * 8 + (4 * r - 3))
                    split_expert(e, k, x, r, j)

            per_expert(e, body)

        @block.vector
        def _(e):
            e.wait_ge(k.s_w6, k.n_w6)
            n = 0

            def chain(ins):
                nonlocal n
                n += 1
                ins.then_inc(s_t, 1)
                e.wait_ge(s_t, n)

            for r in range(2):
                for m in range(2):
                    e.memset(pick[r][:, m, 0:1], 0.0).then_inc(s_l, 1)
            e.wait_ge(s_g, 1)
            e.wait_ge(s_l, 4)
            chain(e.tensor_tensor(score[:, :, :], OB[0][:, 0:TILES * E].rearrange("p (t x) -> p t x", x=E),
                                  k.gateb[:, :].unsqueeze(1).to_broadcast([P, TILES, E]), ALU.add))
            for t in range(TILES):
                i = e.max(top[:, t, :], score[:, t, :])
            chain(i)
            for t in range(TILES):
                i = e.max_index(idx[:, t, :], top[:, t, :], score[:, t, :])
            chain(i)
            chain(e.tensor_copy(idf[:, :, :], idx[:, :, :]))
            for i in range(TOPK):
                ins = e.tensor_tensor(pick[i][:, :, :], k.iota8[:, :].unsqueeze(1).to_broadcast([P, TILES, E]),
                                      idf[:, :, i:i + 1].to_broadcast([P, TILES, E]), ALU.is_equal)
            chain(ins)
            for i in range(TOPK):
                ins = e.tensor_tensor(pick[i][:, :, :], pick[i][:, :, :], top[:, :, i:i + 1].to_broadcast([P, TILES, E]),
                                      ALU.mult)
            chain(ins)
            chain(e.tensor_tensor(comb[:, :, :], pick[0][:, :, :], pick[1][:, :, :], ALU.add))

            def shares():
                for g in range(4):
                    e.wait_ge(s_g, 3 + g)
                    x = k.x[:, 2 * g:2 * g + 2, :].rearrange("p t d -> p (t d)")
                    e.tensor_tensor(x, x, OB[g][:, :], ALU.add).then_inc(s_a, 1)

            def body(x, r, j):
                for n, (m, h) in enumerate(blocks):
                    e.wait_ge(s_r, x * 4 + (n + 5))
                    e.tensor_tensor(h_lo[r][:, m, h * HALF:(h + 1) * HALF], hid[n][:, :],
                                    h_hi[r][:, m, h * HALF:(h + 1) * HALF].bitcast(F32), ALU.subtract
                                    ).then_inc(s_l, 1)
                if isinstance(x, int) and x == 0:
                    shares()
                for g in range(4):
                    e.wait_ge(s_o, x * 4 + (g + 2))
                    e.wait_ge(s_a, x * 4 + (g + 1))
                    for u in range(2):
                        t = 2 * g + u
                        share = comb[:, t, x:x + 1] if isinstance(x, int) else comb[:, t, :][:, bass.ds(x, 1)]
                        i = e.scalar_tensor_tensor(k.x[:, t, :], OB[g][:, u * D:(u + 1) * D], share,
                                                   k.x[:, t, :], ALU.mult, ALU.add)
                    i.then_inc(s_a, 1)

            per_expert(e, body)


def perceiver(nc, t, out):
    with ExitStack() as ctx:
        sb, ps, sem = tools(nc, ctx)
        k = Names()
        k.ctx, k.ctxT = t["ctx"], t["ctxT"]
        k.x = sb("x", [P, TILES, D])
        k.xn = sb("xn", [P, TILES, D])
        k.xT = sb("xT", [P, KD, TOK])
        k.ident = sb("ident", [P, P])
        k.cols = sb("cols", [P, NCOLS])
        k.rows = sb("rows", [P, NROWS, D])
        k.bc_dram = nc.dram_tensor("bc_rows", (2 * DS, TOK), F32, kind="Internal").ap()
        k.trig = sb("trig", [P, 2, DH])
        k.own_head = sb("own_head", [P, HG])
        k.causal = sb("causal", [P, L])
        k.masked = sb("masked", [P, L])
        k.same_batch = sb("same_batch", [P, P])
        k.diag64 = sb("diag64", [P, L])
        k.iota8 = sb("iota8", [P, E])
        k.stats = sb("stats", [P, TILES, 6])
        k.wtq = sb("wtq", [P, KD, 2])
        k.wfq = sb("wfq", [2, D])
        k.btq = sb("btq", [P, 2])
        k.wg = sb("wg", [P, KD, E])
        k.gateb = sb("gateb", [P, E])
        k.b2 = sb("b2", [E, D])
        k.s_w5, k.s_w6 = sem("s_w5"), sem("s_w6")
        k.n_w5 = 16 * 7
        k.n_w6 = 16 * 3
        k.s_w3, k.s_w4 = sem("s_w3"), sem("s_w4")
        k.n_w3 = 32
        k.n_w4 = 16 * (5 + KD)
        k.s_w2 = sem("s_w2")
        k.n_w2 = 80 + 1
        k.s_x, k.s_rows, k.s_const, k.s_w0 = (sem(n) for n in ("s_x", "s_rows", "s_const", "s_w0"))
        k.n_ident = k.n_const = 8 + 3 + 3 + E
        k.n_w0 = 64

        ctx1 = ctx.enter_context(ExitStack())
        sb1, _, _ = tools(nc, ctx1)
        k.wq0, k.wk0T, k.wv0 = (sb1(n, [P, KD, D]) for n in ("wq0", "wk0T", "wv0"))
        k.cT = [sb1(f"cT{r}", [P, 2, KD, LK]) for r in range(2)]
        k.cN = [sb1(f"cN{r}", [FULL + 1, 2, ROWS, D]) for r in range(2)]
        k.s_dT = [sem(f"a_dT{r}") for r in range(2)]
        k.s_dN = [sem(f"a_dN{r}") for r in range(2)]
        def load_vectors(e, a, b):
            e.dma_start(k.rows[:, a:b, :].rearrange("p r d -> p (r d)"),
                        t["rows"][a:b].rearrange("r d -> (r d)").unsqueeze(0).to_broadcast([P, (b - a) * D])
                        ).then_inc(k.s_rows, 16)

        def early_loads(block):
            @block.sync
            def _(e):
                load_columns(e, k, 1, 1)
                load_rows(e, k, 1, 1)
                e.dma_start(k.trig[:, :, :], t["trig"]).then_inc(k.s_w4, 16)
                e.dma_start(k.wtq[:, :, :], t["wtq"].rearrange("(c p) n -> p c n", p=P)).then_inc(k.s_w5, 16)
                e.dma_start(k.wfq[:, :], t["wfq"]).then_inc(k.s_w5, 16)
                e.dma_start(k.btq[:, :], t["btq"].unsqueeze(0).to_broadcast([P, 2])).then_inc(k.s_w5, 16)
                e.dma_start(k.wg[:, :, :], t["wg"].rearrange("(c p) n -> p c n", p=P)).then_inc(k.s_w6, 16)
                e.dma_start(k.gateb[:, :], t["gateb"].unsqueeze(0).to_broadcast([P, E])).then_inc(k.s_w6, 16)
                e.dma_start(k.b2[:, :], t["b2"]).then_inc(k.s_w6, 16)

        with nc.Block() as block:
            @block.sync
            def _(e):
                e.dma_start(k.x[:, :, :], t["x"].rearrange("b l d -> (b l) d").rearrange("(t p) d -> p t d", p=P)
                            ).then_inc(k.s_x, 16)
                e.dma_start(k.cols[:, :], t["cols"]).then_inc(k.s_w0, 16)
                for n, w in (("wq0", k.wq0), ("wk0T", k.wk0T), ("wv0", k.wv0)):
                    e.dma_start(w[:, :, :], t[n].rearrange("(c p) n -> p c n", p=P)).then_inc(k.s_w0, 16)
                load_vectors(e, 0, 1)
                load_columns(e, k, 0, 0)
                load_rows(e, k, 0, 0)

            @block.vector
            def _(e):
                e.wait_ge(k.s_const, k.n_const)
                e.tensor_scalar(k.masked[:, :], k.causal[:, :], -NEG, NEG, ALU.mult, ALU.add)

            @block.gpsimd
            def _(e):
                n = 0

                def chain(ins):
                    nonlocal n
                    n += 1
                    ins.then_inc(k.s_const, 1)
                    e.wait_ge(k.s_const, n)

                def keep(m, op, fill, base, pattern, mult):
                    chain(e.affine_select(out=m, in_=m, compare_op=op, fill=fill, base=base,
                                          pattern=pattern, channel_multiplier=mult))

                chain(e.memset(k.ident[:, :], 0.0))
                keep(k.ident[:, :], ALU.not_equal, 1.0, 0, [[-1, P]], 1)
                chain(e.memset(k.causal[:, :], 1.0))
                for b in range(2):
                    keep(k.causal[64 * b:64 * b + 64, :], ALU.is_ge, 0.0, 0, [[-1, L]], 1)
                chain(e.memset(k.own_head[:, :], 1.0))
                keep(k.own_head[:, :], ALU.is_ge, 0.0, 0, [[-DH, HG]], 1)
                keep(k.own_head[:, :], ALU.is_ge, 0.0, DH - 1, [[DH, HG]], -1)
                chain(e.memset(k.diag64[:, :], 0.0))
                for b in range(2):
                    keep(k.diag64[64 * b:64 * b + 64, :], ALU.not_equal, 1.0, 0, [[-1, L]], 1)
                chain(e.memset(k.same_batch[:, :], 0.0))
                for b in range(2):
                    chain(e.memset(k.same_batch[64 * b:64 * b + 64, 64 * b:64 * b + 64], 1.0))
                for i in range(E):
                    chain(e.memset(k.iota8[:, i:i + 1], float(i)))

        layer_norm(nc, k, "ln0", early_loads)
        cross_attention(nc, k)
        ctx1.close()
        ctx4, ctx3, ctx2 = (ctx.enter_context(ExitStack()) for _ in range(3))
        sb4, sb3, sb2 = (tools(nc, c)[0] for c in (ctx4, ctx3, ctx2))
        k.w5 = [sb4(f"w5{i}", [P, KD, D]) for i in range(4)]
        k.w4 = [sb4(f"w4{i}", [P, KD, D]) for i in range(4)]
        k.c0T = sb4("c0T", [P, KD, TOK])
        k.w_fc = sb3("w_fc", [P, KD, FF])
        k.w_pr = sb3("w_pr", [P, FM, D])
        k.w_in = sb2("w_in", [P, KD, 2 * DI])
        k.w_xp = sb2("w_xp", [P, CH, 64])
        k.w_dt = sb2("w_dt", [DTR, DI])
        k.w_out = sb2("w_out", [P, CH, D])

        def late_weights(block):
            @block.gpsimd
            def _(e):
                e.memset(k.w_xp[:, :, DTR:32], 0.0).then_inc(k.s_w2, 1)

            @block.sync
            def _(e):
                e.dma_start(k.w_in[:, :, :], t["w_in"].rearrange("(c p) n -> p c n", p=P)).then_inc(k.s_w2, 16)
                e.dma_start(k.w_xp[:, :, 0:DTR], t["w_xp"][:, 0:DTR].rearrange("(c p) n -> p c n", p=P)
                            ).then_inc(k.s_w2, 16)
                e.dma_start(k.w_xp[:, :, 32:64], t["w_xp"][:, DTR:DTR + 2 * DS].rearrange("(c p) n -> p c n", p=P)
                            ).then_inc(k.s_w2, 16)
                e.dma_start(k.w_dt[:, :], t["w_dt"]).then_inc(k.s_w2, 16)
                e.dma_start(k.w_out[:, :, :], t["w_out"].rearrange("(c p) n -> p c n", p=P)).then_inc(k.s_w2, 16)
                load_vectors(e, 1, NROWS)
                e.dma_start(k.w_fc[:, :, :], t["w_fc"].rearrange("(c p) n -> p c n", p=P)).then_inc(k.s_w3, 16)
                e.dma_start(k.w_pr[:, :, :], t["w_pr"].rearrange("(c p) n -> p c n", p=P)).then_inc(k.s_w3, 16)
                for i in range(4):
                    e.dma_start(k.w4[i][:, :, :], t[f"w4{i}"].rearrange("(c p) n -> p c n", p=P)).then_inc(k.s_w4, 16)
                for i in range(4):
                    e.dma_start(k.w5[i][:, :, :], t[f"w5{i}"].rearrange("(c p) n -> p c n", p=P)).then_inc(k.s_w5, 16)
                for c in range(KD):
                    e.dma_start(k.c0T[:, c, :].rearrange("p (b n) -> p b n", n=L),
                                t["ctxT"][:, c * P:(c + 1) * P, 0:L].rearrange("b p n -> p b n")).then_inc(k.s_w4, 16)

        layer_norm(nc, k, "ln1", late_weights)
        with ExitStack() as mctx:
            sb, _, _ = tools(nc, mctx)
            m = Names()
            m.bc_dram = k.bc_dram
            m.u, m.sres, m.delta, m.du = (sb(n, [P, CH, TOK]) for n in ("u", "sres", "delta", "du"))
            m.diagD = sb("diagD", [P, CH, P])
            m.negA = sb("negA", [P, CH, DS])
            m.Bb = [sb("Bb0", [P, TOK])[:, :], k.w_in[:, 0, :]]
            m.Cb = [sb(f"Cb{i}", [P, TOK])[:, :] for i in range(2)]
            m.s_bl = [sem(f"n_bl{i}") for i in range(2)]
            m.s_cl = [sem(f"n_cl{i}") for i in range(2)]
            mamba_front(nc, k, m)
            mamba_scan(nc, k, m)
        ctx2.close()
        layer_norm(nc, k, "ln2")
        with ExitStack() as wctx:
            sb, _, _ = tools(nc, wctx)
            k.qkb = sb("qkb", [P, TILES, 2 * H, DH])
            k.vx = sb("vx", [P, TILES, H, DV])
            k.vs = sb("vs", [P, TILES, H, DV])
            k.s_vs = sem("s_vs")

            def swap_batches(block):
                @block.sync
                def _(e):
                    for b in range(2):
                        e.dma_start(k.vs[64 * b:64 * b + 64, :, :, :], k.vx[64 * (1 - b):64 * (1 - b) + 64, :, :, :]
                                    ).then_inc(k.s_vs, 16)

            spiking_ffn(nc, k)
            layer_norm(nc, k, "ln3", swap_batches)
            windowed_attention(nc, k)
        ctx3.close()
        layer_norm(nc, k, "ln4")
        with ExitStack() as ectx:
            sb, _, _ = tools(nc, ectx)
            k.w_experts = (t["w1"], t["w2"])
            k.w6 = [sb(f"w6{r}", [P, 2, KD, D]) for r in range(2)]
            k.w_hi = [sb(f"w_hi{r}", [P, 2, KD, D], F32R) for r in range(2)]
            k.w_lo = [sb(f"w_lo{r}", [P, 2, KD, D], F32R) for r in range(2)]
            k.x_hi, k.x_lo = (sb(n, [P, KD, TOK], F32R) for n in ("x_hi", "x_lo"))
            k.one = sb("one", [P, 1])
            k.s_w = [sem(f"e_w{i}") for i in range(2)]
            k.s_hi = sem("e_hi")
            k.s_ws = sem("e_ws")
            phase_attention(nc, k)
            layer_norm(nc, k, "ln5", split=(k.x_hi, k.x_lo))
            experts(nc, k, out)




def rotary():
    half = DH // 2
    inv = (1.0 / 10000.0 ** (np.arange(half, dtype=np.float32) / half)).astype(np.float32)
    ang = np.arange(L, dtype=np.float32)[:, None] * inv[None, :]
    cos, sin = np.cos(ang), np.sin(ang)
    table = np.stack([np.concatenate([cos, cos], 1), np.concatenate([-sin, sin], 1)], 1)
    return np.concatenate([table, table], 0).astype(np.float32)


def layout(inputs):
    a = {n: np.asarray(v) for n, v in inputs.items()}
    T = np.transpose
    cols = [T(a["L0_xattn_bq"].reshape(2, P)), T(a["L0_xattn_bk"].reshape(2, P)),
            T(a["L0_attn_in_proj_b"].reshape(8, P)),
            T(a["L0_attn_conv_w"].reshape(4, P, 4), (1, 0, 2)).reshape(P, 16),
            T(a["L0_attn_conv_b"].reshape(4, P)), T(a["L0_attn_dt_proj_b"].reshape(4, P)),
            T(a["L0_attn_D_param"].reshape(4, P)),
            T(a["L0_attn_A_log"].reshape(4, P, 16), (1, 0, 2)).reshape(P, 64),
            T(a["L1_attn_bq"].reshape(2, P)), T(a["L1_attn_bk"].reshape(2, P)),
            T(a["L1_ffn_b1"].reshape(16, P))]
    rows = [a[n] for n in ("L0_xattn_bv", "L0_attn_out_proj_b", "L1_xattn_bq", "L1_xattn_bk", "L1_xattn_bv",
                           "L1_xattn_bo", "L1_attn_bv", "L1_attn_bo", "L1_attn_bfq")]
    return {
        "x": a["x"], "ctx": a["ctx_1024"], "ctxT": T(a["ctx_1024"], (0, 2, 1)),
        "cols": np.concatenate(cols, axis=1), "rows": np.stack(rows),
        "w_in": T(a["L0_attn_in_proj_w"]), "w_xp": T(a["L0_attn_x_proj_w"]),
        "w_dt": T(a["L0_attn_dt_proj_w"]), "w_out": T(a["L0_attn_out_proj_w"]),
        "w_fc": T(a["L0_ffn_W_fc"]), "w_pr": T(a["L0_ffn_W_proj"]),
        **{f"w4{i}": T(a[f"L1_xattn_W{c}"]) for i, c in enumerate("qkvo")}, "trig": rotary(),
        **{f"w5{i}": T(a[f"L1_attn_W{c}"]) for i, c in enumerate("qkvo")},
        "wtq": T(a["L1_attn_Wtq"]), "wfq": T(a["L1_attn_Wfq"]), "btq": a["L1_attn_btq"],
        "wg": a["L1_ffn_gate_w"], "gateb": a["L1_ffn_gate_b"], "b2": a["L1_ffn_b2"],
        "w1": a["L1_ffn_w1"], "w2": a["L1_ffn_w2"],
        "wq0": a["L0_xattn_Wq"], "wk0T": T(a["L0_xattn_Wk"]), "wv0": a["L0_xattn_Wv"],
    }


def kernel(**inputs):
    import concourse.bacc as _bacc
    from concourse.bass_utils import run_bass_kernel_spmd as _run

    nc = _bacc.Bacc("TRN2", target_bir_lowering=False, num_devices=1)
    arrays, args = {}, {}
    for name, v in layout(inputs).items():
        v = np.ascontiguousarray(v)
        arrays[f"in_{name}"] = v
        args[name] = nc.dram_tensor(f"in_{name}", v.shape, mybir.dt.from_np(v.dtype), kind="ExternalInput").ap()
    out = nc.dram_tensor("out_dram", (B, L, D), F32, kind="ExternalOutput").ap()
    perceiver(nc, args, out)
    r = _run(nc, [arrays], core_ids=[0])
    return r.results[0]["out_dram"]
```
